# Optimizing a Trainium2 kernel written in Bass

```python
import numpy as np
import jax
import jax.numpy as jnp

def _softmax(x, axis=-1):
    return jax.nn.softmax(x, axis=axis)

def _gelu(x):
    return jax.nn.gelu(x, approximate=True)

def _silu(x):
    return jax.nn.silu(x)

def _sigmoid(x):
    return jax.nn.sigmoid(x)

def _layernorm(x, axis=-1, eps=1e-05):
    m = jnp.mean(x, axis=axis, keepdims=True)
    v = jnp.var(x, axis=axis, keepdims=True)
    return (x - m) / jnp.sqrt(v + eps)

def _scatter_add(tgt, idx, src, axis=0):
    return tgt.at[idx].add(src)

def _segment_sum(src, seg, n):
    return jax.ops.segment_sum(src, seg, n)
kernel_name = 'mk_flamingo_gated_d4_seqx_r8_5ba76f'

def setup_inputs(seed: int=0):
    np.random.seed(seed)
    _w = jnp.asarray

    def _rec_inputs():
        import jax
        import jax.numpy as jnp
        _rk = jax.random.key(seed)
        x = -0.0002928 + 1 * jax.random.normal(jax.random.fold_in(_rk, 1), (32, 128, 128), jnp.float32)
        _lenS = 128 - jax.random.randint(jax.random.fold_in(_rk, 7), (32,), 0, max(1, 128 // 4) + 1, jnp.int32)
        _lenS2 = 128 - jax.random.randint(jax.random.fold_in(_rk, 8), (32,), 0, max(1, 128 // 4) + 1, jnp.int32)
        _ctx_1024P = jax.random.normal(jax.random.fold_in(_rk, 11), (32, 16, 128), jnp.float32)
        _ctx_1024c = jax.random.dirichlet(jax.random.fold_in(_rk, 511), 0.3 * jnp.ones((16,), jnp.float32), (32, 128))
        _ctx_1024t = jnp.einsum('bsk,bkd->bsd', _ctx_1024c, _ctx_1024P)
        _ctx_1024t = _ctx_1024t * jax.lax.rsqrt(jnp.mean(jnp.square(_ctx_1024t)) + 1e-12) * 0.953939
        ctx_1024 = -1.39393e-06 + 0.999914 * (_ctx_1024t + 0.3 * jax.random.normal(jax.random.fold_in(_rk, 611), (32, 128, 128), jnp.float32))
        _validS = jnp.arange(128)[None, :] < _lenS[:, None]
        _validS2 = jnp.arange(128)[None, :] < _lenS2[:, None]
        _causal = jnp.tril(jnp.ones((128, 128), dtype=bool))
        mask_BxS2_ff1 = jnp.where(jnp.ones((32, 128), dtype=bool), 1.0, 0.0).astype(jnp.float32)
        mask_Bx1xS2_bf1 = jnp.ones((32, 1, 128), dtype=bool)
        mask_1x1xSxS2_ff0 = jnp.where(jnp.ones((1, 1, 128, 128), dtype=bool), 0.0, -1000000000.0).astype(jnp.float32)
        mask_BxS2_ik0 = jnp.where(jnp.broadcast_to(_validS2[:, :], (32, 128)), 0, 1).astype(jnp.int32)
        _g = jax.random.normal(jax.random.fold_in(_rk, 9001), (2, 4), jnp.float32)
        _g = jnp.sign(_g) * jnp.maximum(jnp.abs(_g), 1.0) + (_g == 0) * 1.0
        g_xattn = _g[0]
        g_ffn = _g[1]
        return (x, ctx_1024, mask_BxS2_ff1, mask_Bx1xS2_bf1, mask_1x1xSxS2_ff0, mask_BxS2_ik0, g_xattn, g_ffn)
    x, ctx_1024, mask_BxS2_ff1, mask_Bx1xS2_bf1, mask_1x1xSxS2_ff0, mask_BxS2_ik0, g_xattn, g_ffn = _rec_inputs()

    def _L0_xattn_setup():
        import jax, jax.numpy as jnp
        import numpy as np
        HIDDEN = 128
        HEADS = 16
        HEAD_DIM = HIDDEN // HEADS
        key = jax.random.key(seed)
        ks = jax.random.split(key, 11)
        B, S = (2, 256)
        s = 1.0 / np.sqrt(HIDDEN)
        return {'query': jax.random.normal(ks[0], (B, S, HIDDEN), jnp.float32), 'key': jax.random.normal(ks[1], (B, S, HIDDEN), jnp.float32), 'value': jax.random.normal(ks[2], (B, S, HIDDEN), jnp.float32), 'Wq': jax.random.normal(ks[3], (HIDDEN, HIDDEN), jnp.float32) * s, 'bq': jnp.zeros((HIDDEN,), jnp.float32), 'Wk': jax.random.normal(ks[4], (HIDDEN, HIDDEN), jnp.float32) * s, 'bk': jnp.zeros((HIDDEN,), jnp.float32), 'Wv': jax.random.normal(ks[5], (HIDDEN, HIDDEN), jnp.float32) * s, 'bv': jnp.zeros((HIDDEN,), jnp.float32), 'Wo': jax.random.normal(ks[6], (HIDDEN, HIDDEN), jnp.float32) * s, 'bo': jnp.zeros((HIDDEN,), jnp.float32)}
    _L0_xattn_all = _L0_xattn_setup()
    _L0_xattn_in = {k: v for k, v in _L0_xattn_all.items() if k in ('Wq', 'bq', 'Wk', 'bk', 'Wv', 'bv', 'Wo', 'bo')}
    del _L0_xattn_all

    def _L0_ffn_setup():
        import jax, jax.numpy as jnp
        import numpy as np
        B, S, D, E, TOP_K = (2, 128, 128, 8, 2)
        H = 4 * D
        key = jax.random.key(seed)
        ks = jax.random.split(key, 12)
        sc = 0.02
        return {'x': jax.random.normal(ks[0], (B, S, D), jnp.float32), 'Wg': jax.random.normal(ks[1], (E, D), jnp.float32) * sc, 'bg': jnp.zeros((E,), jnp.float32), 'bias': jnp.zeros((E,), jnp.float32), 'W1': jax.random.normal(ks[2], (E, H, D), jnp.float32) * sc, 'b1': jnp.zeros((E, H), jnp.float32), 'W2': jax.random.normal(ks[3], (E, D, H), jnp.float32) * sc, 'b2': jnp.zeros((E, D), jnp.float32), 'Ws1': jax.random.normal(ks[4], (H, D), jnp.float32) * sc, 'bs1': jnp.zeros((H,), jnp.float32), 'Ws2': jax.random.normal(ks[5], (D, H), jnp.float32) * sc, 'bs2': jnp.zeros((D,), jnp.float32)}
    _L0_ffn_all = _L0_ffn_setup()
    _L0_ffn_in = {k: v for k, v in _L0_ffn_all.items() if k in ('Wg', 'bg', 'bias', 'W1', 'b1', 'W2', 'b2', 'Ws1', 'bs1', 'Ws2', 'bs2')}
    del _L0_ffn_all

    def _L1_xattn_setup():
        import jax, jax.numpy as jnp
        import numpy as np
        D_MODEL = 128
        HEADS = 16
        DEPTH = D_MODEL // HEADS
        B, S = (4, 512)
        EPS_K = 1e-06
        EPS_LN = 1e-06

        def _layernorm(x, g, b):
            m = jnp.mean(x, axis=-1, keepdims=True)
            var = jnp.var(x, axis=-1, keepdims=True)
            return (x - m) * jax.lax.rsqrt(var + EPS_LN) * g + b

        def _split_heads(x):
            bsz, sl, _ = x.shape
            return x.reshape(bsz, sl, HEADS, DEPTH).transpose(0, 2, 1, 3)
        key = jax.random.key(seed)
        ks = jax.random.split(key, 8)
        lecun = 1.0 / np.sqrt(D_MODEL)
        glorot = np.sqrt(2.0 / (D_MODEL + D_MODEL))
        return {'q': jax.random.normal(ks[0], (B, S, D_MODEL), jnp.float32), 'k': jax.random.normal(ks[1], (B, S, D_MODEL), jnp.float32), 'v': jax.random.normal(ks[2], (B, S, D_MODEL), jnp.float32), 'mask': jnp.ones((B, S), jnp.float32), 'wq': jax.random.normal(ks[3], (D_MODEL, D_MODEL), jnp.float32) * lecun, 'wk': jax.random.normal(ks[4], (D_MODEL, D_MODEL), jnp.float32) * lecun, 'wv': jax.random.normal(ks[5], (D_MODEL, D_MODEL), jnp.float32) * lecun, 'ln_gamma': jnp.ones((D_MODEL,), jnp.float32), 'ln_beta': jnp.zeros((D_MODEL,), jnp.float32), 'dense_w': jax.random.normal(ks[6], (D_MODEL, D_MODEL), jnp.float32) * glorot, 'dense_b': jnp.zeros((D_MODEL,), jnp.float32)}
    _L1_xattn_all = _L1_xattn_setup()
    _L1_xattn_in = {k: v for k, v in _L1_xattn_all.items() if k in ('wq', 'wk', 'wv', 'ln_gamma', 'ln_beta', 'dense_w', 'dense_b')}
    del _L1_xattn_all

    def _L1_ffn_setup():
        import jax, jax.numpy as jnp
        import numpy as np
        B, S, D, H, E = (4, 256, 128, 256, 8)
        key = jax.random.key(seed)
        ks = jax.random.split(key, 8)
        scale = 0.02
        return {'x': jax.random.normal(ks[0], (B, S, D), dtype=jnp.float32), 'Wr': jax.random.normal(ks[1], (D, E), dtype=jnp.float32) * scale, 'br': jnp.zeros((E,), dtype=jnp.float32), 'W1': jax.random.normal(ks[2], (E, D, H), dtype=jnp.float32) * scale, 'b1': jnp.zeros((E, H), dtype=jnp.float32), 'W2': jax.random.normal(ks[3], (E, H, D), dtype=jnp.float32) * scale, 'b2': jnp.zeros((E, D), dtype=jnp.float32)}
    _L1_ffn_all = _L1_ffn_setup()
    _L1_ffn_in = {k: v for k, v in _L1_ffn_all.items() if k in ('Wr', 'br', 'W1', 'b1', 'W2', 'b2')}
    del _L1_ffn_all

    def _L2_xattn_setup():
        import jax, jax.numpy as jnp
        import numpy as np
        D_MODEL = 128
        N_HEADS = 16
        D_K = D_MODEL // N_HEADS
        key = jax.random.key(seed)
        ks = jax.random.split(key, 12)
        B, S, D = (4, 256, D_MODEL)
        s = 1.0 / np.sqrt(D)
        return {'Q': jax.random.normal(ks[0], (B, S, D), jnp.float32), 'K': jax.random.normal(ks[1], (B, S, D), jnp.float32), 'V': jax.random.normal(ks[2], (B, S, D), jnp.float32), 'mask': jnp.ones((B, 1, S), dtype=bool), 'Wq': jax.random.normal(ks[3], (D, D), jnp.float32) * s, 'bq': jnp.zeros((D,), jnp.float32), 'Wk': jax.random.normal(ks[4], (D, D), jnp.float32) * s, 'bk': jnp.zeros((D,), jnp.float32), 'Wv': jax.random.normal(ks[5], (D, D), jnp.float32) * s, 'bv': jnp.zeros((D,), jnp.float32), 'Wo': jax.random.normal(ks[6], (D, D), jnp.float32) * s, 'bo': jnp.zeros((D,), jnp.float32)}
    _L2_xattn_all = _L2_xattn_setup()
    _L2_xattn_in = {k: v for k, v in _L2_xattn_all.items() if k in ('Wq', 'bq', 'Wk', 'bk', 'Wv', 'bv', 'Wo', 'bo')}
    del _L2_xattn_all

    def _L2_ffn_setup():
        import math
        import jax, jax.numpy as jnp
        import numpy as np
        NUM_EXPERTS = 8
        CAPACITY_FACTOR = 1.5
        key = jax.random.key(seed)
        ks = jax.random.split(key, 4)
        B, T, D, F, E = (4, 256, 128, 512, NUM_EXPERTS)
        scale = 0.02
        return {'x': jax.random.normal(ks[0], (B, T, D), dtype=jnp.float32), 'router_w': jax.random.normal(ks[1], (E, D), dtype=jnp.float32) * scale, 'w1': jax.random.normal(ks[2], (E, D, F), dtype=jnp.float32) * scale, 'b1': jnp.zeros((E, F), dtype=jnp.float32), 'w2': jax.random.normal(ks[3], (E, F, D), dtype=jnp.float32) * scale, 'b2': jnp.zeros((E, D), dtype=jnp.float32)}
    _L2_ffn_all = _L2_ffn_setup()
    _L2_ffn_in = {k: v for k, v in _L2_ffn_all.items() if k in ('router_w', 'w1', 'b1', 'w2', 'b2')}
    del _L2_ffn_all

    def _L3_xattn_setup():
        import jax, jax.numpy as jnp
        import numpy as np
        H = 16
        D_MODEL = 128
        D_K = D_MODEL // H
        B, S = (4, 256)

        def _split_heads(x):
            b, s, _ = x.shape
            return x.reshape(b, s, H, D_K).transpose(0, 2, 1, 3)
        key = jax.random.key(seed)
        ks = jax.random.split(key, 12)
        scale = 1.0 / np.sqrt(D_MODEL)
        inp = {'query': jax.random.normal(ks[0], (B, S, D_MODEL), jnp.float32), 'key_in': jax.random.normal(ks[1], (B, S, D_MODEL), jnp.float32), 'value': jax.random.normal(ks[2], (B, S, D_MODEL), jnp.float32), 'src_mask': jnp.zeros((1, 1, S, S), jnp.float32), 'pad_mask': jax.random.randint(ks[3], (B, S), 0, 2, jnp.int32), 'Wq': jax.random.normal(ks[4], (D_MODEL, D_MODEL), jnp.float32) * scale, 'bq': jnp.zeros((D_MODEL,), jnp.float32), 'Wk': jax.random.normal(ks[5], (D_MODEL, D_MODEL), jnp.float32) * scale, 'bk': jnp.zeros((D_MODEL,), jnp.float32), 'Wv': jax.random.normal(ks[6], (D_MODEL, D_MODEL), jnp.float32) * scale, 'bv': jnp.zeros((D_MODEL,), jnp.float32), 'Wo': jax.random.normal(ks[7], (D_MODEL, D_MODEL), jnp.float32) * scale, 'bo': jnp.zeros((D_MODEL,), jnp.float32)}
        return inp
    _L3_xattn_all = _L3_xattn_setup()
    _L3_xattn_in = {k: v for k, v in _L3_xattn_all.items() if k in ('Wq', 'bq', 'Wk', 'bk', 'Wv', 'bv', 'Wo', 'bo')}
    del _L3_xattn_all

    def _L3_ffn_setup():
        import jax, jax.numpy as jnp
        import numpy as np
        N_EMBD = 128
        N_STATE = 512
        key = jax.random.key(seed)
        k_x, k_w1, k_b1, k_w2, k_b2 = jax.random.split(key, 5)
        x = jax.random.normal(k_x, (4, 256, N_EMBD), dtype=jnp.float32)
        w1 = jax.random.normal(k_w1, (N_EMBD, N_STATE), dtype=jnp.float32) * (1.0 / np.sqrt(N_EMBD))
        b1 = jax.random.normal(k_b1, (N_STATE,), dtype=jnp.float32) * 0.02
        w2 = jax.random.normal(k_w2, (N_STATE, N_EMBD), dtype=jnp.float32) * (1.0 / np.sqrt(N_STATE))
        b2 = jax.random.normal(k_b2, (N_EMBD,), dtype=jnp.float32) * 0.02
        return {'x': x, 'w1': w1, 'b1': b1, 'w2': w2, 'b2': b2}
    _L3_ffn_all = _L3_ffn_setup()
    _L3_ffn_in = {k: v for k, v in _L3_ffn_all.items() if k in ('w1', 'b1', 'w2', 'b2')}
    del _L3_ffn_all
    return {'x': x, 'ctx_1024': ctx_1024, 'mask_BxS2_ff1': mask_BxS2_ff1, 'mask_Bx1xS2_bf1': mask_Bx1xS2_bf1, 'mask_1x1xSxS2_ff0': mask_1x1xSxS2_ff0, 'mask_BxS2_ik0': mask_BxS2_ik0, 'g_xattn': g_xattn, 'g_ffn': g_ffn, 'L0_xattn_Wq': _L0_xattn_in['Wq'], 'L0_xattn_bq': _L0_xattn_in['bq'], 'L0_xattn_Wk': _L0_xattn_in['Wk'], 'L0_xattn_bk': _L0_xattn_in['bk'], 'L0_xattn_Wv': _L0_xattn_in['Wv'], 'L0_xattn_bv': _L0_xattn_in['bv'], 'L0_xattn_Wo': _L0_xattn_in['Wo'], 'L0_xattn_bo': _L0_xattn_in['bo'], 'L0_ffn_Wg': _L0_ffn_in['Wg'], 'L0_ffn_bg': _L0_ffn_in['bg'], 'L0_ffn_bias': _L0_ffn_in['bias'], 'L0_ffn_W1': _L0_ffn_in['W1'], 'L0_ffn_b1': _L0_ffn_in['b1'], 'L0_ffn_W2': _L0_ffn_in['W2'], 'L0_ffn_b2': _L0_ffn_in['b2'], 'L0_ffn_Ws1': _L0_ffn_in['Ws1'], 'L0_ffn_bs1': _L0_ffn_in['bs1'], 'L0_ffn_Ws2': _L0_ffn_in['Ws2'], 'L0_ffn_bs2': _L0_ffn_in['bs2'], 'L1_xattn_wq': _L1_xattn_in['wq'], 'L1_xattn_wk': _L1_xattn_in['wk'], 'L1_xattn_wv': _L1_xattn_in['wv'], 'L1_xattn_ln_gamma': _L1_xattn_in['ln_gamma'], 'L1_xattn_ln_beta': _L1_xattn_in['ln_beta'], 'L1_xattn_dense_w': _L1_xattn_in['dense_w'], 'L1_xattn_dense_b': _L1_xattn_in['dense_b'], 'L1_ffn_Wr': _L1_ffn_in['Wr'], 'L1_ffn_br': _L1_ffn_in['br'], 'L1_ffn_W1': _L1_ffn_in['W1'], 'L1_ffn_b1': _L1_ffn_in['b1'], 'L1_ffn_W2': _L1_ffn_in['W2'], 'L1_ffn_b2': _L1_ffn_in['b2'], 'L2_xattn_Wq': _L2_xattn_in['Wq'], 'L2_xattn_bq': _L2_xattn_in['bq'], 'L2_xattn_Wk': _L2_xattn_in['Wk'], 'L2_xattn_bk': _L2_xattn_in['bk'], 'L2_xattn_Wv': _L2_xattn_in['Wv'], 'L2_xattn_bv': _L2_xattn_in['bv'], 'L2_xattn_Wo': _L2_xattn_in['Wo'], 'L2_xattn_bo': _L2_xattn_in['bo'], 'L2_ffn_router_w': _L2_ffn_in['router_w'], 'L2_ffn_w1': _L2_ffn_in['w1'], 'L2_ffn_b1': _L2_ffn_in['b1'], 'L2_ffn_w2': _L2_ffn_in['w2'], 'L2_ffn_b2': _L2_ffn_in['b2'], 'L3_xattn_Wq': _L3_xattn_in['Wq'], 'L3_xattn_bq': _L3_xattn_in['bq'], 'L3_xattn_Wk': _L3_xattn_in['Wk'], 'L3_xattn_bk': _L3_xattn_in['bk'], 'L3_xattn_Wv': _L3_xattn_in['Wv'], 'L3_xattn_bv': _L3_xattn_in['bv'], 'L3_xattn_Wo': _L3_xattn_in['Wo'], 'L3_xattn_bo': _L3_xattn_in['bo'], 'L3_ffn_w1': _L3_ffn_in['w1'], 'L3_ffn_b1': _L3_ffn_in['b1'], 'L3_ffn_w2': _L3_ffn_in['w2'], 'L3_ffn_b2': _L3_ffn_in['b2']}

def reference(x, ctx_1024, mask_BxS2_ff1, mask_Bx1xS2_bf1, mask_1x1xSxS2_ff0, mask_BxS2_ik0, g_xattn, g_ffn, L0_xattn_Wq, L0_xattn_bq, L0_xattn_Wk, L0_xattn_bk, L0_xattn_Wv, L0_xattn_bv, L0_xattn_Wo, L0_xattn_bo, L0_ffn_Wg, L0_ffn_bg, L0_ffn_bias, L0_ffn_W1, L0_ffn_b1, L0_ffn_W2, L0_ffn_b2, L0_ffn_Ws1, L0_ffn_bs1, L0_ffn_Ws2, L0_ffn_bs2, L1_xattn_wq, L1_xattn_wk, L1_xattn_wv, L1_xattn_ln_gamma, L1_xattn_ln_beta, L1_xattn_dense_w, L1_xattn_dense_b, L1_ffn_Wr, L1_ffn_br, L1_ffn_W1, L1_ffn_b1, L1_ffn_W2, L1_ffn_b2, L2_xattn_Wq, L2_xattn_bq, L2_xattn_Wk, L2_xattn_bk, L2_xattn_Wv, L2_xattn_bv, L2_xattn_Wo, L2_xattn_bo, L2_ffn_router_w, L2_ffn_w1, L2_ffn_b1, L2_ffn_w2, L2_ffn_b2, L3_xattn_Wq, L3_xattn_bq, L3_xattn_Wk, L3_xattn_bk, L3_xattn_Wv, L3_xattn_bv, L3_xattn_Wo, L3_xattn_bo, L3_ffn_w1, L3_ffn_b1, L3_ffn_w2, L3_ffn_b2):
    import jax
    import jax.numpy as jnp

    def _L0_xattn_ref(query, key, value, Wq, bq, Wk, bk, Wv, bv, Wo, bo):
        import jax, jax.numpy as jnp
        import numpy as np
        HIDDEN = 128
        HEADS = 16
        HEAD_DIM = HIDDEN // HEADS
        B, S, _ = query.shape
        Q = query @ Wq.T + bq
        K = key @ Wk.T + bk
        V = value @ Wv.T + bv
        Q = Q.reshape(B, S, HEADS, HEAD_DIM).transpose(0, 2, 1, 3)
        K = K.reshape(B, S, HEADS, HEAD_DIM).transpose(0, 2, 1, 3)
        V = V.reshape(B, S, HEADS, HEAD_DIM).transpose(0, 2, 1, 3)
        scale = jnp.sqrt(jnp.float32(HEAD_DIM))
        energy = jnp.einsum('bhqd,bhkd->bhqk', Q, K) / scale
        attn = jax.nn.softmax(energy, axis=-1)
        x = jnp.einsum('bhqk,bhkd->bhqd', attn, V)
        x = x.transpose(0, 2, 1, 3).reshape(B, S, HIDDEN)
        return x @ Wo.T + bo

    def _L0_ffn_ref(x, Wg, bg, bias, W1, b1, W2, b2, Ws1, bs1, Ws2, bs2):
        import jax, jax.numpy as jnp
        import numpy as np
        B, S, D, E, TOP_K = (2, 128, 128, 8, 2)
        H = 4 * D
        b, s, d = x.shape
        xf = x.reshape(-1, d)
        T = xf.shape[0]
        scores = jax.nn.sigmoid(xf @ Wg.T + bg + bias)
        top_scores, top_idx = jax.lax.top_k(scores, TOP_K)
        weights = jnp.zeros((T, E), scores.dtype)
        weights = weights.at[jnp.arange(T)[:, None], top_idx].add(top_scores)
        h = jax.nn.gelu(jnp.einsum('td,ehd->teh', xf, W1) + b1, approximate=False)
        eo = jnp.einsum('teh,edh->ted', h, W2) + b2
        combined = jnp.einsum('ted,te->td', eo, weights)
        shared = jax.nn.gelu(xf @ Ws1.T + bs1, approximate=False) @ Ws2.T + bs2
        return (shared + combined).reshape(b, s, d)

    def _L1_xattn_ref(q, k, v, mask, wq, wk, wv, ln_gamma, ln_beta, dense_w, dense_b):
        import jax, jax.numpy as jnp
        import numpy as np
        D_MODEL = 128
        HEADS = 16
        DEPTH = D_MODEL // HEADS
        B, S = (4, 512)
        EPS_K = 1e-06
        EPS_LN = 1e-06

        def _layernorm(x, g, b):
            m = jnp.mean(x, axis=-1, keepdims=True)
            var = jnp.var(x, axis=-1, keepdims=True)
            return (x - m) * jax.lax.rsqrt(var + EPS_LN) * g + b

        def _split_heads(x):
            bsz, sl, _ = x.shape
            return x.reshape(bsz, sl, HEADS, DEPTH).transpose(0, 2, 1, 3)
        bsz = q.shape[0]
        em = mask[:, None, :, None]
        qh = _split_heads(_layernorm(q @ wq, ln_gamma, ln_beta))
        kh = _split_heads(_layernorm(k @ wk, ln_gamma, ln_beta))
        vh = _split_heads(_layernorm(v @ wv, ln_gamma, ln_beta))
        q_prime = jax.nn.relu(qh) + EPS_K
        k_prime = (jax.nn.relu(kh) + EPS_K) * em
        vh = vh * em
        kv = jnp.einsum('bhnd,bhne->bhde', k_prime, vh)
        z = 1.0 / (jnp.einsum('bhnd,bhd->bhn', q_prime, k_prime.sum(axis=-2)) + EPS_K)
        att = jnp.einsum('bhnd,bhde,bhn->bhne', q_prime, kv, z)
        att = att.reshape(bsz, -1, D_MODEL)
        out = att @ dense_w + dense_b
        return _layernorm(out, ln_gamma, ln_beta)

    def _L1_ffn_ref(x, Wr, br, W1, b1, W2, b2):
        import jax, jax.numpy as jnp
        import numpy as np
        B, S, D, H, E = (4, 256, 128, 256, 8)
        d = x.shape[-1]
        tokens = x.reshape(-1, d)
        logits = tokens @ Wr + br
        probs = jax.nn.softmax(logits, axis=-1)
        expert = jnp.argmax(probs, axis=-1)
        max_prob = jnp.take_along_axis(probs, expert[:, None], axis=-1)
        h = jax.nn.relu(jnp.einsum('td,edh->teh', tokens, W1) + b1[None])
        y = jnp.einsum('teh,ehd->ted', h, W2) + b2[None]
        out = jnp.take_along_axis(y, expert[:, None, None], axis=1)[:, 0, :]
        return (out * max_prob).reshape(x.shape)

    def _L2_xattn_ref(Q, K, V, mask, Wq, bq, Wk, bk, Wv, bv, Wo, bo):
        import jax, jax.numpy as jnp
        import numpy as np
        D_MODEL = 128
        N_HEADS = 16
        D_K = D_MODEL // N_HEADS
        B, S, D = Q.shape
        H, dk = (N_HEADS, D_K)
        q = (Q @ Wq + bq).reshape(B, S, H, dk).transpose(0, 2, 1, 3)
        k = (K @ Wk + bk).reshape(B, S, H, dk).transpose(0, 2, 1, 3)
        v = (V @ Wv + bv).reshape(B, S, H, dk).transpose(0, 2, 1, 3)
        scores = jnp.einsum('bhqd,bhkd->bhqk', q, k) / jnp.sqrt(jnp.float32(dk))
        m = mask[:, None, :, :]
        scores = jnp.where(m, scores, jnp.float32(-1000000000.0))
        att = jax.nn.softmax(scores, axis=-1)
        out = jnp.einsum('bhqk,bhkd->bhqd', att, v)
        out = out.transpose(0, 2, 1, 3).reshape(B, S, D)
        return out @ Wo + bo

    def _L2_ffn_ref(x, router_w, w1, b1, w2, b2):
        import math
        import jax, jax.numpy as jnp
        import numpy as np
        NUM_EXPERTS = 8
        CAPACITY_FACTOR = 1.5
        B, T, D = x.shape
        E = router_w.shape[0]
        N = B * T
        C = max(math.ceil(CAPACITY_FACTOR * N / E), 1)
        x_flat = x.reshape(N, D)
        logits = x_flat @ router_w.T
        probs = jax.nn.softmax(logits, axis=-1)
        chosen_e = jnp.argmax(probs, axis=-1)
        chosen_p = jnp.max(probs, axis=-1)
        onehot = jax.nn.one_hot(chosen_e, E, dtype=jnp.float32)
        pos = jnp.take_along_axis(jnp.cumsum(onehot, axis=0), chosen_e[:, None], axis=1)[:, 0] - 1.0
        pos = pos.astype(jnp.int32)
        kept = pos < C
        pos_c = jnp.clip(pos, 0, C - 1)
        buf = jnp.zeros((E, C, D), dtype=x.dtype).at[chosen_e, pos_c].add(x_flat * kept[:, None].astype(x.dtype))
        h = jax.nn.gelu(jnp.einsum('ecd,edf->ecf', buf, w1) + b1[:, None, :], approximate=False)
        eo = jnp.einsum('ecf,efd->ecd', h, w2) + b2[:, None, :]
        y = eo[chosen_e, pos_c] * (chosen_p * kept.astype(x.dtype))[:, None]
        return y.reshape(B, T, D)

    def _L3_xattn_ref(query, key_in, value, src_mask, pad_mask, Wq, bq, Wk, bk, Wv, bv, Wo, bo):
        import jax, jax.numpy as jnp
        import numpy as np
        H = 16
        D_MODEL = 128
        D_K = D_MODEL // H
        B, S = (4, 256)

        def _split_heads(x):
            b, s, _ = x.shape
            return x.reshape(b, s, H, D_K).transpose(0, 2, 1, 3)
        q = _split_heads(query @ Wq.T + bq)
        k = _split_heads(key_in @ Wk.T + bk)
        v = _split_heads(value @ Wv.T + bv)
        scores = jnp.einsum('bhqd,bhkd->bhqk', q, k) / jnp.sqrt(jnp.float32(D_K))
        pm = pad_mask[:, None, None, :]
        scores = jnp.where(pm == 0, jnp.float32(-1000000000.0), scores)
        scores = scores + src_mask
        p_attn = jax.nn.softmax(scores, axis=-1)
        x = jnp.einsum('bhqk,bhkd->bhqd', p_attn, v)
        x = x.transpose(0, 2, 1, 3).reshape(query.shape[0], -1, H * D_K)
        return x @ Wo.T + bo

    def _L3_ffn_ref(x, w1, b1, w2, b2):
        import jax, jax.numpy as jnp
        import numpy as np
        N_EMBD = 128
        N_STATE = 512
        h = jax.nn.gelu(jnp.einsum('bse,eh->bsh', x, w1) + b1, approximate=False)
        return jnp.einsum('bsh,he->bse', h, w2) + b2
    x = x + jnp.tanh(g_xattn[0]) * _L0_xattn_ref(_layernorm(x, axis=-1), ctx_1024, ctx_1024, L0_xattn_Wq, L0_xattn_bq, L0_xattn_Wk, L0_xattn_bk, L0_xattn_Wv, L0_xattn_bv, L0_xattn_Wo, L0_xattn_bo)
    x = x + jnp.tanh(g_ffn[0]) * _L0_ffn_ref(_layernorm(x, axis=-1), L0_ffn_Wg, L0_ffn_bg, L0_ffn_bias, L0_ffn_W1, L0_ffn_b1, L0_ffn_W2, L0_ffn_b2, L0_ffn_Ws1, L0_ffn_bs1, L0_ffn_Ws2, L0_ffn_bs2)
    x = x + jnp.tanh(g_xattn[1]) * _L1_xattn_ref(_layernorm(x, axis=-1), ctx_1024, ctx_1024, mask_BxS2_ff1, L1_xattn_wq, L1_xattn_wk, L1_xattn_wv, L1_xattn_ln_gamma, L1_xattn_ln_beta, L1_xattn_dense_w, L1_xattn_dense_b)
    x = x + jnp.tanh(g_ffn[1]) * _L1_ffn_ref(_layernorm(x, axis=-1), L1_ffn_Wr, L1_ffn_br, L1_ffn_W1, L1_ffn_b1, L1_ffn_W2, L1_ffn_b2)
    x = x + jnp.tanh(g_xattn[2]) * _L2_xattn_ref(_layernorm(x, axis=-1), ctx_1024, ctx_1024, mask_Bx1xS2_bf1, L2_xattn_Wq, L2_xattn_bq, L2_xattn_Wk, L2_xattn_bk, L2_xattn_Wv, L2_xattn_bv, L2_xattn_Wo, L2_xattn_bo)
    x = x + jnp.tanh(g_ffn[2]) * _L2_ffn_ref(_layernorm(x, axis=-1), L2_ffn_router_w, L2_ffn_w1, L2_ffn_b1, L2_ffn_w2, L2_ffn_b2)
    x = x + jnp.tanh(g_xattn[3]) * _L3_xattn_ref(_layernorm(x, axis=-1), ctx_1024, ctx_1024, mask_1x1xSxS2_ff0, mask_BxS2_ik0, L3_xattn_Wq, L3_xattn_bq, L3_xattn_Wk, L3_xattn_bk, L3_xattn_Wv, L3_xattn_bv, L3_xattn_Wo, L3_xattn_bo)
    x = x + jnp.tanh(g_ffn[3]) * _L3_ffn_ref(_layernorm(x, axis=-1), L3_ffn_w1, L3_ffn_b1, L3_ffn_w2, L3_ffn_b2)
    return x

_drawn_inputs = setup_inputs


def setup_inputs(seed=0):
    import zlib

    import numpy as np

    out = dict(_drawn_inputs(seed))
    spreads = {'L0_xattn_bq': (0.0, 0.495),
     'L0_xattn_bk': (0.0, 2.0),
     'L0_xattn_bv': (0.0, 0.1),
     'L0_xattn_bo': (0.0, 0.1),
     'L0_ffn_bg': (0.0, 0.325),
     'L0_ffn_bias': (0.0, 0.1),
     'L0_ffn_b1': (0.0, 0.661),
     'L0_ffn_b2': (0.0, 0.1),
     'L0_ffn_bs1': (0.0, 0.539),
     'L0_ffn_bs2': (0.0, 0.1),
     'L1_xattn_ln_gamma': (1.0, 0.2),
     'L1_xattn_ln_beta': (0.0, 0.1),
     'L1_xattn_dense_b': (0.0, 0.1),
     'L1_ffn_br': (0.0, 0.8),
     'L1_ffn_b1': (0.0, 0.8),
     'L1_ffn_b2': (0.0, 0.75),
     'L2_xattn_bq': (0.0, 0.714),
     'L2_xattn_bk': (0.0, 2.0),
     'L2_xattn_bv': (0.0, 0.1),
     'L2_xattn_bo': (0.0, 0.1),
     'L2_ffn_b1': (0.0, 0.8),
     'L2_ffn_b2': (0.0, 0.8),
     'L3_xattn_bq': (0.0, 0.576),
     'L3_xattn_bk': (0.0, 2.0),
     'L3_xattn_bv': (0.0, 0.322),
     'L3_xattn_bo': (0.0, 0.332)}
    factors = {'g_ffn': 32.256,
     'L1_ffn_Wr': 5.091,
     'L1_ffn_W1': 8.0,
     'L1_ffn_W2': 8.0,
     'L2_ffn_router_w': 6.295,
     'L2_ffn_w1': 8.0,
     'L2_ffn_w2': 8.0,
     'L3_ffn_b1': 8.0,
     'L3_ffn_b2': 5.501}
    for name, (base, spread) in spreads.items():
        noise = np.random.default_rng([zlib.crc32(name.encode()), seed]).standard_normal(out[name].shape)
        drawn = base * np.exp(spread * noise) if base else spread * noise
        out[name] = jnp.asarray(drawn.astype(out[name].dtype))
    for name, factor in factors.items():
        out[name] = (out[name] * factor).astype(out[name].dtype)
    return out
```

```python
import numpy as np
import concourse.bass as bass
from concourse import mybir
from contextlib import ExitStack

F32 = mybir.dt.float32
I32 = mybir.dt.int32
U8 = mybir.dt.uint8
ALU = mybir.AluOpType
ACT = mybir.ActivationFunctionType
AX = mybir.AxisListType.X

P = 128
D = 128
NB = 32
HEADS = 16
HD = D // HEADS
GROUPS = 4
PER = HEADS // GROUPS
E = 8
BLOCK = 4
NBLK = NB // BLOCK
CAPACITY = 768
EPS = 1e-5
EPS_LN1 = 1e-6
EPS_K = 1e-6
NEG = 1e9


class Batch:

    def __init__(self, i, c):
        self.i, self.c = i, c
        self.n = i * 2 + c if not isinstance(i, int) else 2 * i + c
        self.slot = c % 2
        self.turn = i + c // 2

    def shift(self, k):
        return Batch(self.i, self.c + k)


def wait(eng, sem, value):
    if isinstance(value, int) and value <= 0:
        return
    eng.wait_ge(sem, value)


def pipelined(eng, step):
    step(Batch(0, -1), False, False, True)
    step(Batch(0, 0), False, True, True)
    step(Batch(0, 1), True, True, True)
    step(Batch(0, 2), True, True, True)
    with eng.Fori(0, (NB - 4) // 2) as i:
        for u in (0, 1):
            step(Batch(i, 3 + u), True, True, True)
    step(Batch(0, NB - 1), True, True, False)
    step(Batch(0, NB), True, False, False)


def tile_of(t, n, w=D):
    if isinstance(n, int):
        return t[:, n * w:(n + 1) * w]
    return t[:, bass.ds(n * w, w)]


def moments(nc, dve, chain, base, stats, mean, var, total, gap):
    s = stats.rearrange("p (n c) -> p n c", c=6)
    nc.vector.tensor_tensor(mean, s[:, :, 1], s[:, :, 4], ALU.add)
    nc.vector.tensor_tensor(gap, s[:, :, 1], s[:, :, 4], ALU.subtract)
    nc.vector.tensor_tensor(total, s[:, :, 2], s[:, :, 5], ALU.add).then_inc(chain, 1)
    dve.wait_ge(chain, base + 1)
    nc.vector.tensor_scalar(mean, mean, 0.5, None, ALU.mult)
    nc.vector.scalar_tensor_tensor(out=gap, in0=gap, scalar=0.25, in1=gap, op0=ALU.mult, op1=ALU.mult).then_inc(chain, 1)
    dve.wait_ge(chain, base + 2)
    nc.vector.scalar_tensor_tensor(out=var, in0=total, scalar=1.0 / D, in1=gap, op0=ALU.mult, op1=ALU.add).then_inc(chain, 1)
    dve.wait_ge(chain, base + 3)


def rebuild_norm_scale(nc, sem, core, eps):
    chain, ready, root = sem("chain"), sem("var_ready"), sem("root_ready")
    done = sem("rstd_ready")
    with nc.Block() as block:
        @block.vector
        def _(dve):
            moments(nc, dve, chain, 0, core.stats[:], core.mean[:], core.var[:], core.half_sum[:], core.half_gap[:])
            nc.vector.tensor_scalar(core.rstd[:], core.var[:], eps, None, ALU.add).then_inc(ready, 1)
            dve.wait_ge(root, 1)
            nc.vector.reciprocal(core.rstd[:], core.root[:]).then_inc(done, 1)
            dve.wait_ge(done, 1)

        @block.scalar
        def _(act):
            act.wait_ge(ready, 1)
            nc.scalar.activation(core.root[:], core.rstd[:], ACT.Sqrt).then_inc(root, 1)


def softmax_attention(nc, sem, core, w, masked, src):
    ctx_in = [sem("ctx_in0"), sem("ctx_in1")]
    xn_ready = sem("xn_ready")
    xnT_ready, xnT_out = sem("xnT_ready"), sem("xnT_out")
    proj = sem("proj")
    q_out, k_out, v_out = sem("q_out"), sem("k_out"), sem("v_out")
    k_plain, bias_ready = sem("k_plain"), sem("bias_ready")
    scores, biased, top, shifted, expd = sem("scores"), sem("biased"), sem("top"), sem("shifted"), sem("expd")
    turned, probs_out, mixed = sem("turned"), sem("probs_out"), sem("mixed")
    recip, normed = sem("recip"), sem("normed")
    oT_ready, oT_out, y_ready = sem("oT_ready"), sem("oT_out"), sem("y_ready")
    y_read, x_new, stats_new = sem("y_read"), sem("x_new"), sem("stats_new")
    A, S, T, O = core.bankA, core.bankS, core.bankT, core.bankO
    q_norm = float(HD) ** -0.5

    with nc.Block() as block:
        @block.sync
        def _(sp):
            def load(b):
                wait(sp, proj, b.n - 1)
                sp.dma_start(core.ctxT[b.slot][:], core.ctxT_dram[bass.ds(b.n, 1) if not isinstance(b.n, int) else slice(b.n, b.n + 1)]
                             .rearrange("o d t -> d (o t)")).then_inc(ctx_in[b.slot], 16)
            load(Batch(0, 0))
            load(Batch(0, 1))
            with sp.Fori(0, (NB - 2) // 2) as i:
                for u in (0, 1):
                    load(Batch(i, 2 + u))

        @block.vector
        def _(dve):
            def step(b, back, middle, front):
                n, c = b.shift(1), b.shift(-1)
                if front:
                    wait(dve, xnT_ready, n.n - 1)
                    nc.vector.tensor_scalar(core.xn[n.slot][:], tile_of(core.x, n.n), tile_of(core.mean, n.n, 1),
                                            tile_of(core.rstd, n.n, 1), ALU.subtract, ALU.mult).then_inc(xn_ready, 1)
                if middle and masked:
                    if src is None:
                        nc.vector.tensor_copy(core.bias[:], tile_of(core.key_neg, b.n)).then_inc(bias_ready, 1)
                    else:
                        nc.vector.tensor_tensor(core.bias[:], tile_of(core.key_neg, b.n), src[:], ALU.add).then_inc(bias_ready, 1)
                    wait(dve, bias_ready, b.n + 1)
                if middle:
                    for hf in range(2):
                        wait(dve, scores, b.n * 2 + hf + 1)
                        wait(dve, turned, b.n * 4 - 4)
                        half = core.probs[b.slot][:, hf * 1024:(hf + 1) * 1024]
                        source = S[hf][:]
                        if masked:
                            nc.vector.tensor_tensor(half.rearrange("p (h k) -> p h k", k=P), source.rearrange("p (h k) -> p h k", k=P),
                                                    core.bias[:].rearrange("p (o k) -> p o k", o=1).to_broadcast([P, 8, P]), ALU.add).then_inc(biased, 1)
                            wait(dve, biased, b.n * 2 + hf + 1)
                            source = half
                        m = core.top[:, hf * 8:hf * 8 + 8]
                        nc.vector.tensor_reduce(out=m, in_=source.rearrange("p (h k) -> p h k", k=P), op=ALU.max,
                                                axis=AX).then_inc(top, 1)
                        wait(dve, top, b.n * 2 + hf + 1)
                        nc.vector.tensor_tensor(half.rearrange("p (h k) -> p h k", k=P), source.rearrange("p (h k) -> p h k", k=P),
                                                m.rearrange("p (h o) -> p h o", o=1).to_broadcast([P, 8, P]), ALU.subtract).then_inc(shifted, 1)
                if back:
                    o = O[:, 0:HEADS * (HD + 1)].rearrange("p (h c) -> p h c", c=HD + 1)
                    wait(dve, mixed, c.n * 4 + 4)
                    nc.vector.reciprocal(core.recip[:], o[:, :, HD]).then_inc(recip, 1)
                    wait(dve, recip, c.n + 1)
                    wait(dve, oT_ready, c.n)
                    nc.vector.tensor_tensor(core.o[:].rearrange("p (h c) -> p h c", c=HD), o[:, :, 0:HD],
                                            core.recip[:].rearrange("p (h o) -> p h o", o=1).to_broadcast([P, HEADS, HD]), ALU.mult).then_inc(normed, 1)
                if front:
                    wait(dve, proj, n.n + 1)
                    wait(dve, scores, n.n * 2)
                    kz = core.kz[:].rearrange("p (s k) -> p s k", k=P)
                    ms = core.head_of4[:].rearrange("p (s k) -> p s k", k=P)
                    if masked:
                        nc.vector.scalar_tensor_tensor(out=core.k[:], in0=A[:, 256:384], scalar=w.bk[:, 0:1],
                                                       in1=tile_of(core.key_on, n.n), op0=ALU.add, op1=ALU.mult).then_inc(k_plain, 1)
                        wait(dve, k_plain, n.n + 1)
                        nc.vector.tensor_tensor(kz, core.k[:].rearrange("p (o k) -> p o k", o=1).to_broadcast([P, PER, P]),
                                                ms, ALU.mult).then_inc(k_out, 1)
                    else:
                        nc.vector.scalar_tensor_tensor(out=kz, in0=A[:, 256:384].rearrange("p (o k) -> p o k", o=1).to_broadcast([P, PER, P]),
                                                       scalar=w.bk[:, 0:1], in1=ms, op0=ALU.add, op1=ALU.mult).then_inc(k_out, 1)
                    wait(dve, mixed, n.n * 4 - 4)
                    nc.vector.tensor_tensor(core.v[n.slot][:].rearrange("p (h c) -> p h c", c=HD + 1)[:, :, 0:HD],
                                            A[:, 384:512].rearrange("p (h c) -> p h c", c=HD),
                                            w.bv[:].rearrange("p (h c) -> p h c", c=HD), ALU.add).then_inc(v_out, 1)
                if back:
                    xt = tile_of(core.x, c.n)
                    wait(dve, x_new, c.n)
                    wait(dve, y_ready, c.n + 1)
                    nc.vector.tensor_tensor(core.y[:], O[:, 384:512], w.bo[:], ALU.add).then_inc(y_read, 1)
                    wait(dve, y_read, c.n + 1)
                    nc.vector.scalar_tensor_tensor(out=xt, in0=core.y[:], scalar=core.gate[:, w.gate:w.gate + 1], in1=xt,
                                                   op0=ALU.mult, op1=ALU.add).then_inc(x_new, 1)
                    if not (isinstance(c.n, int) and c.n == 0):
                        nc.vector.bn_stats(tile_of(core.stats, c.n - 1, 6), tile_of(core.x, c.n - 1)).then_inc(stats_new, 1)
            pipelined(dve, step)
            dve.wait_ge(x_new, NB)
            nc.vector.bn_stats(tile_of(core.stats, NB - 1, 6), tile_of(core.x, NB - 1)).then_inc(stats_new, 1)
            dve.wait_ge(stats_new, NB)

        @block.scalar
        def _(act):
            def step(b, back, middle, front):
                n, c = b.shift(1), b.shift(-1)
                if back:
                    for g in range(GROUPS):
                        wait(act, turned, c.n * 4 + g + 1)
                        wait(act, mixed, c.n * 4 + g - 1)
                        nc.scalar.activation(core.probsT[g % 2][:], T[g % 2][:], ACT.Copy).then_inc(probs_out, 1)
                if front:
                    wait(act, xnT_ready, n.n + 1)
                    nc.scalar.activation(core.xnT1[:], A[:, 0:128], ACT.Copy).then_inc(xnT_out, 1)
                if back:
                    wait(act, oT_ready, c.n + 1)
                    nc.scalar.activation(core.oT[:], O[:, 256:384], ACT.Copy).then_inc(oT_out, 1)
                if middle:
                    for hf in range(2):
                        wait(act, shifted, b.n * 2 + hf + 1)
                        half = core.probs[b.slot][:, hf * 1024:(hf + 1) * 1024]
                        nc.scalar.activation(half, half, ACT.Exp).then_inc(expd, 1)
                if front:
                    wait(act, v_out, n.n + 1)
                    wait(act, scores, n.n * 2)
                    for g in range(GROUPS):
                        r = slice(32 * g, 32 * g + 32)
                        nc.scalar.activation(core.qz[r, g * P:(g + 1) * P], A[r, 128:256], ACT.Identity,
                                             bias=w.bq[r, 0:1], scale=q_norm).then_inc(q_out, 1)
            pipelined(act, step)

        @block.tensor
        def _(pe):
            def step(b, back, middle, front):
                n, c = b.shift(1), b.shift(-1)
                if middle:
                    wait(pe, q_out, b.n * 4 + 4)
                    wait(pe, k_out, b.n + 1)
                    for hf in range(2):
                        wait(pe, shifted, b.n * 2 + hf - 1)
                        for g in (2 * hf, 2 * hf + 1):
                            last = nc.tensor.matmul(S[hf][:, (g % 2) * 512:(g % 2) * 512 + 512], core.qz[:, g * P:(g + 1) * P],
                                                    core.kz[:], start=True, stop=True)
                        last.then_inc(scores, 1)

                def turn(g):
                    wait(pe, expd, c.n * 2 + g // 2 + 1)
                    wait(pe, probs_out, c.n * 4 + g - 1)
                    for s in range(PER):
                        h = g * PER + s
                        last = nc.tensor.transpose(T[g % 2][:, s * P:(s + 1) * P], core.probs[c.slot][:, h * P:(h + 1) * P], core.ident[:])
                    last.then_inc(turned, 1)

                def mix(g):
                    wait(pe, probs_out, c.n * 4 + g + 1)
                    for s in range(PER):
                        h = g * PER + s
                        last = nc.tensor.matmul(O[:, h * 9:h * 9 + 9], core.probsT[g % 2][:, s * P:(s + 1) * P],
                                                core.v[c.slot][:, h * 9:h * 9 + 9], start=True, stop=True)
                    last.then_inc(mixed, 1)
                if back:
                    wait(pe, v_out, c.n + 1)
                    wait(pe, y_read, c.n)
                    turn(0), turn(1), mix(0), turn(2), mix(1), turn(3), mix(2), mix(3)
                if front:
                    wait(pe, q_out, n.n * 4)
                    wait(pe, v_out, n.n)
                    wait(pe, xn_ready, n.n + 1)
                    nc.tensor.transpose(A[:, 0:128], core.xn[n.slot][:], core.ident[:]).then_inc(xnT_ready, 1)
                if back:
                    wait(pe, normed, c.n + 1)
                    nc.tensor.transpose(O[:, 256:384], core.o[:], core.ident[:]).then_inc(oT_ready, 1)
                if front:
                    wait(pe, ctx_in[n.slot], (n.turn + 1) * 16)
                    wait(pe, xnT_out, n.n + 1)
                    nc.tensor.matmul(A[:, 128:256], w.wq[:], core.xnT1[:], start=True, stop=True)
                    nc.tensor.matmul(A[:, 256:384], w.wk[:], core.ctxT[n.slot][:], start=True, stop=True)
                    nc.tensor.matmul(A[:, 384:512], core.ctxT[n.slot][:], w.wv[:], start=True, stop=True).then_inc(proj, 1)
                if back:
                    wait(pe, oT_out, c.n + 1)
                    nc.tensor.matmul(O[:, 384:512], core.oT[:], w.wo[:], start=True, stop=True).then_inc(y_ready, 1)
            pipelined(pe, step)


def linear_attention(nc, sem, core, w):
    ctx_in, xn_ready, xnT_ready, xnT_out = sem("ctx_in"), sem("xn_ready"), sem("xnT_ready"), sem("xnT_out")
    proj, chain, var_ready, root_ready = sem("proj"), sem("chain"), sem("var_ready"), sem("root_ready")
    kv_in, kv_ready, qT_ready, qT_out, kv_out = sem("kv_in"), sem("kv_ready"), sem("qT_ready"), sem("qT_out"), sem("kv_out")
    att_ready, att_out, attT_ready, attT_out, y_ready = sem("att_ready"), sem("att_out"), sem("attT_ready"), sem("attT_out"), sem("y_ready")
    S, T, A, O = core.bankS, core.bankT, core.bankA, core.bankO
    B4 = BLOCK
    where = [S[0][:, 0:512], S[0][:, 512:1024], S[1][:, 0:512]]
    L = core.lin
    STEPS = 25

    with nc.Block() as block:
        @block.sync
        def _(sp):
            with sp.Fori(0, NB // B4) as r:
                wait(sp, proj, r)
                sp.dma_start(L.ctxT[:].rearrange("d (b t) -> d b t", b=B4),
                             core.ctxT_dram[bass.ds(r * B4, B4)].rearrange("b d t -> d b t")).then_inc(ctx_in, 16)

        @block.vector
        def _(dve):
            with dve.Fori(0, NB // B4) as r:
                done = [0]

                def link(ins):
                    done[0] += 1
                    ins.then_inc(chain, 1)
                    dve.wait_ge(chain, r * STEPS + done[0])

                for j in range(B4):
                    n = r * B4 + j
                    ins = nc.vector.tensor_scalar(L.xn[:, j * D:(j + 1) * D], tile_of(core.x, n), tile_of(core.mean, n, 1),
                                                  tile_of(core.rstd, n, 1), ALU.subtract, ALU.mult)
                ins.then_inc(xn_ready, 1)
                dve.wait_ge(proj, r + 1)
                for t in range(3):
                    for j in range(B4):
                        i = t * B4 + j
                        last = nc.vector.bn_stats(L.stat6[:, i * 6:i * 6 + 6], where[t][:, j * D:(j + 1) * D])
                link(last)
                moments(nc, dve, chain, r * STEPS + done[0], L.stat6[:, 0:72], L.mean[:, 0:12], L.var[:, 0:12], L.total[:, 0:12], L.gap[:, 0:12])
                done[0] += 3
                nc.vector.tensor_scalar(L.var[:, 0:12], L.var[:, 0:12], EPS_LN1, None, ALU.add).then_inc(var_ready, 1)
                dve.wait_ge(root_ready, r * 2 + 1)
                link(nc.vector.reciprocal(L.rs[:, 0:12], L.root[:, 0:12]))
                for t in range(3):
                    for j in range(B4):
                        i = t * B4 + j
                        last = nc.vector.tensor_scalar(L.qkv[:, i * D:(i + 1) * D], where[t][:, j * D:(j + 1) * D], L.mean[:, i:i + 1],
                                                       L.rs[:, i:i + 1], ALU.subtract, ALU.mult)
                link(last)
                every = L.qkv[:].rearrange("p (i d) -> p i d", d=D)
                bc = lambda a, k: a[:].rearrange("p (o d) -> p o d", o=1).to_broadcast([P, k, D])
                link(nc.vector.tensor_tensor(every, every, bc(w.gamma, 12), ALU.mult))
                link(nc.vector.tensor_tensor(every, every, bc(w.beta, 12), ALU.add))
                link(nc.vector.tensor_scalar(L.qkv[:, 0:8 * D], L.qkv[:, 0:8 * D], 0.0, EPS_K, ALU.max, ALU.add))
                for j in range(B4):
                    n = r * B4 + j
                    k = L.qkv[:, (4 + j) * D:(5 + j) * D]
                    nc.vector.tensor_scalar(k, k, tile_of(w.em, n, 1), None, ALU.mult)
                    last = nc.vector.tensor_scalar(L.vx[:, j * 129:j * 129 + D], L.qkv[:, (8 + j) * D:(9 + j) * D], tile_of(w.em, n, 1), None, ALU.mult)
                last.then_inc(kv_in, 1)
                dve.wait_ge(kv_ready, r + 1)
                for j in range(B4):
                    src = (A if j < 2 else O)[:, (j % 2) * 256:(j % 2) * 256 + 129]
                    nc.vector.tensor_tensor(L.kvm[:, j * 144:j * 144 + D], src[:, 0:D], core.own_block[:], ALU.mult)
                    last = nc.vector.tensor_scalar(L.kvm[:, j * 144 + D:(j + 1) * 144], core.own_head[:], src[:, D:D + 1], None, ALU.mult)
                last.then_inc(kv_out, 1)
                dve.wait_ge(att_ready, r + 1)
                for j in range(B4):
                    z = T[j // 2][:, (j % 2) * 256 + D:(j % 2) * 256 + 144]
                    last = nc.vector.tensor_scalar(L.z[:, j * 16:(j + 1) * 16], z, EPS_K, None, ALU.add)
                link(last)
                link(nc.vector.reciprocal(L.zr[:], L.z[:]))
                for j in range(B4):
                    a = T[j // 2][:, (j % 2) * 256:(j % 2) * 256 + D].rearrange("p (h c) -> p c h", c=HD)
                    z = L.zr[:, j * 16:(j + 1) * 16].rearrange("p (o h) -> p o h", o=1).to_broadcast([P, HD, HEADS])
                    to = L.twice[:, j * 256:(j + 1) * 256].rearrange("p (c x h) -> p c x h", x=2, h=HEADS)
                    for x in range(2):
                        last = nc.vector.tensor_tensor(to[:, :, x, :], a, z, ALU.mult)
                link(last)
                link(nc.vector.transpose(L.turned[:], L.twice[:]))
                for j in range(B4):
                    tv = L.turned[:, j * 256:(j + 1) * 256].rearrange("p (c x m) -> p x c m", x=2, m=HEADS)
                    last = nc.vector.tensor_scalar(L.part[:, j * D:(j + 1) * D].rearrange("p (c m) -> p c m", c=HD), tv[:, 0], core.even16[:, 0:1], None, ALU.mult)
                link(last)
                for j in range(B4):
                    tv = L.turned[:, j * 256:(j + 1) * 256].rearrange("p (c x m) -> p x c m", x=2, m=HEADS)
                    last = nc.vector.scalar_tensor_tensor(out=L.att[:, j * D:(j + 1) * D].rearrange("p (m c) -> p c m", c=HD), in0=tv[:, 1],
                                                          scalar=core.even16[:, 1:2], in1=L.part[:, j * D:(j + 1) * D].rearrange("p (c m) -> p c m", c=HD),
                                                          op0=ALU.mult, op1=ALU.add)
                last.then_inc(att_out, 1)
                dve.wait_ge(y_ready, r + 1)
                y = S[1][:, 512:1024].rearrange("p (j d) -> p j d", d=D)
                yb = L.y[:].rearrange("p (j d) -> p j d", d=D)
                link(nc.vector.tensor_tensor(yb, y, bc(w.bd, B4), ALU.add))
                for j in range(B4):
                    last = nc.vector.bn_stats(L.stat6[:, j * 6:j * 6 + 6], L.y[:, j * D:(j + 1) * D])
                link(last)
                moments(nc, dve, chain, r * STEPS + done[0], L.stat6[:, 0:24], L.mean[:, 0:B4], L.var[:, 0:B4], L.total[:, 0:B4], L.gap[:, 0:B4])
                done[0] += 3
                nc.vector.tensor_scalar(L.var[:, 0:B4], L.var[:, 0:B4], EPS_LN1, None, ALU.add).then_inc(var_ready, 1)
                dve.wait_ge(root_ready, r * 2 + 2)
                link(nc.vector.reciprocal(L.rs[:, 0:B4], L.root[:, 0:B4]))
                for j in range(B4):
                    last = nc.vector.tensor_scalar(L.y[:, j * D:(j + 1) * D], L.y[:, j * D:(j + 1) * D], L.mean[:, j:j + 1],
                                                   L.rs[:, j:j + 1], ALU.subtract, ALU.mult)
                link(last)
                link(nc.vector.tensor_tensor(yb, yb, bc(w.gamma, B4), ALU.mult))
                link(nc.vector.tensor_tensor(yb, yb, bc(w.beta, B4), ALU.add))
                xt = core.x[:, bass.ds(r * (B4 * D), B4 * D)]
                link(nc.vector.scalar_tensor_tensor(out=L.y[:], in0=L.y[:], scalar=core.gate[:, w.gate:w.gate + 1], in1=xt, op0=ALU.mult, op1=ALU.add))
                nc.vector.tensor_scalar(xt, L.y[:], 1.0, None, ALU.mult)
                for j in range(B4):
                    last = nc.vector.bn_stats(tile_of(core.stats, r * B4 + j, 6), L.y[:, j * D:(j + 1) * D])
                link(last)
                assert done[0] == STEPS, done[0]

        @block.scalar
        def _(act):
            with act.Fori(0, NB // B4) as r:
                act.wait_ge(xnT_ready, r + 1)
                nc.scalar.activation(L.xnT[:], A[:, 0:512], ACT.Copy).then_inc(xnT_out, 1)
                act.wait_ge(var_ready, r * 2 + 1)
                nc.scalar.activation(L.root[:, 0:12], L.var[:, 0:12], ACT.Sqrt).then_inc(root_ready, 1)
                act.wait_ge(qT_ready, r + 1)
                nc.scalar.activation(L.qT[:], S[1][:, 512:1024], ACT.Copy).then_inc(qT_out, 1)
                act.wait_ge(attT_ready, r + 1)
                nc.scalar.activation(L.attT[:], A[:, 0:512], ACT.Copy).then_inc(attT_out, 1)
                act.wait_ge(var_ready, r * 2 + 2)
                nc.scalar.activation(L.root[:, 0:B4], L.var[:, 0:B4], ACT.Sqrt).then_inc(root_ready, 1)

        @block.tensor
        def _(pe):
            with pe.Fori(0, NB // B4) as r:
                pe.wait_ge(xn_ready, r + 1)
                for j in range(B4):
                    last = nc.tensor.transpose(A[:, j * P:(j + 1) * P], L.xn[:, j * D:(j + 1) * D], core.ident[:])
                last.then_inc(xnT_ready, 1)
                pe.wait_ge(ctx_in, r * 16 + 16)
                pe.wait_ge(xnT_out, r + 1)
                for t, (left, right) in enumerate(((L.xnT, w.wq), (L.ctxT, w.wk), (L.ctxT, w.wv))):
                    for j in range(B4):
                        last = nc.tensor.matmul(where[t][:, j * D:(j + 1) * D], left[:, j * P:(j + 1) * P], right[:], start=True, stop=True)
                last.then_inc(proj, 1)
                pe.wait_ge(kv_in, r + 1)
                for j in range(B4):
                    last = nc.tensor.matmul((A if j < 2 else O)[:, (j % 2) * 256:(j % 2) * 256 + 129], L.qkv[:, (4 + j) * D:(5 + j) * D],
                                            L.vx[:, j * 129:(j + 1) * 129], start=True, stop=True)
                last.then_inc(kv_ready, 1)
                for j in range(B4):
                    last = nc.tensor.transpose(S[1][:, 512 + j * P:512 + (j + 1) * P], L.qkv[:, j * D:(j + 1) * D], core.ident[:])
                last.then_inc(qT_ready, 1)
                pe.wait_ge(qT_out, r + 1)
                pe.wait_ge(kv_out, r + 1)
                for j in range(B4):
                    last = nc.tensor.matmul(T[j // 2][:, (j % 2) * 256:(j % 2) * 256 + 144], L.qT[:, j * P:(j + 1) * P],
                                            L.kvm[:, j * 144:(j + 1) * 144], start=True, stop=True)
                last.then_inc(att_ready, 1)
                pe.wait_ge(att_out, r + 1)
                for j in range(B4):
                    last = nc.tensor.transpose(A[:, j * P:(j + 1) * P], L.att[:, j * D:(j + 1) * D], core.perm[:])
                last.then_inc(attT_ready, 1)
                pe.wait_ge(attT_out, r + 1)
                for j in range(B4):
                    last = nc.tensor.matmul(S[1][:, 512 + j * D:512 + (j + 1) * D], L.attT[:, j * P:(j + 1) * P], w.wd[:], start=True, stop=True)
                last.then_inc(y_ready, 1)


def norm_and_route(nc, sem, core, w):
    xn_ready, xnT_ready, xnT_out, logit_ready, logit_out = (sem("xn_ready"), sem("xnT_ready"), sem("xnT_out"), sem("logit_ready"), sem("logit_out"))
    T, A = core.bankT, [core.bankA, core.bankO]
    routed = w.router is not None
    per = 2 if routed else 1
    with nc.Block() as block:
        @block.vector
        def _(dve):
            with dve.Fori(0, NB // 2) as i:
                for u in (0, 1):
                    n = Batch(i, u)
                    wait(dve, xnT_ready, n.n - 1) if u else wait(dve, xnT_ready, n.i * 2)
                    nc.vector.tensor_scalar(core.xn[u][:], tile_of(core.x, n.n), tile_of(core.mean, n.n, 1),
                                            tile_of(core.rstd, n.n, 1), ALU.subtract, ALU.mult).then_inc(xn_ready, 1)
                if routed:
                    for u in (0, 1):
                        n = Batch(i, u)
                        dve.wait_ge(logit_ready, n.n + 1)
                        nc.vector.tensor_tensor(tile_of(core.logits, n.n, E), A[u][:, 0:E], w.router_bias[:], ALU.add).then_inc(logit_out, 1)

        @block.scalar
        def _(act):
            with act.Fori(0, NB // 2) as i:
                for u in (0, 1):
                    n = Batch(i, u)
                    act.wait_ge(xnT_ready, n.n + 1)
                    if routed:
                        act.wait_ge(logit_ready, i * 2)
                        nc.scalar.activation(core.xnTs[u][:], T[u][:, 0:P], ACT.Copy).then_inc(xnT_out, 1)
                    nc.scalar.activation(tile_of(core.xnT, n.n), T[u][:, 0:P], ACT.Copy).then_inc(xnT_out, 1)

        @block.tensor
        def _(pe):
            with pe.Fori(0, NB // 2) as i:
                for u in (0, 1):
                    n = Batch(i, u)
                    pe.wait_ge(xn_ready, n.n + 1)
                    pe.wait_ge(xnT_out, i * (2 * per))
                    nc.tensor.transpose(T[u][:, 0:P], core.xn[u][:], core.ident[:]).then_inc(xnT_ready, 1)
                if routed:
                    for u in (0, 1):
                        n = Batch(i, u)
                        pe.wait_ge(xnT_out, n.n * 2 + 1)
                        pe.wait_ge(logit_out, i * 2)
                        nc.tensor.matmul(A[u][:, 0:E], core.xnTs[u][:], w.router[:], start=True, stop=True).then_inc(logit_ready, 1)


def route(nc, sem, core, kind, gate):
    chain, act_in, act_out, rank_in, rank_ready = sem("chain"), sem("act_in"), sem("act_out"), sem("rank_in"), sem("rank_ready")
    R = core.route
    N = NB * E
    v3 = lambda a: a[:].rearrange("p (n e) -> p n e", e=E)
    row = lambda a: a[:].rearrange("p (n o) -> p n o", o=1).to_broadcast([P, NB, E])
    tg = core.gate[:, gate:gate + 1]
    with nc.Block() as block:
        @block.vector
        def _(dve):
            done = [0]

            def link(ins):
                done[0] += 1
                ins.then_inc(chain, 1)
                dve.wait_ge(chain, done[0])

            def first_of_largest(out, values, top, mark, best):
                link(nc.vector.tensor_reduce(out=top[:], in_=v3(values), op=ALU.max, axis=AX))
                link(nc.vector.tensor_tensor(v3(mark), v3(values), row(top), ALU.is_equal))
                link(nc.vector.tensor_tensor(mark[:], mark[:], core.countdown[:], ALU.mult))
                link(nc.vector.tensor_reduce(out=best[:], in_=v3(mark), op=ALU.max, axis=AX))
                link(nc.vector.tensor_tensor(v3(out), v3(mark), row(best), ALU.is_equal))

            if kind == "top2":
                dve.wait_ge(act_out, 1)
                first_of_largest(R.one, R.prob, R.top, R.mark, R.best)
                link(nc.vector.tensor_scalar(R.left[:], R.one[:], -1.0, 1.0, ALU.mult, ALU.add))
                link(nc.vector.tensor_tensor(R.left[:], R.prob[:], R.left[:], ALU.mult))
                link(nc.vector.tensor_tensor(R.left[:], R.left[:], R.one[:], ALU.subtract))
                first_of_largest(R.two, R.left, R.top, R.mark, R.best)
                link(nc.vector.tensor_tensor(R.one[:], R.one[:], R.two[:], ALU.add))
                link(nc.vector.tensor_tensor(R.one[:], R.one[:], R.prob[:], ALU.mult))
            else:
                link(nc.vector.tensor_reduce(out=R.top[:], in_=v3(core.logits), op=ALU.max, axis=AX))
                nc.vector.tensor_tensor(v3(R.left), v3(core.logits), row(R.top), ALU.subtract).then_inc(act_in, 1)
                dve.wait_ge(act_out, 1)
                link(nc.vector.tensor_reduce(out=R.best[:], in_=v3(R.prob), op=ALU.add, axis=AX))
                link(nc.vector.reciprocal(R.top[:], R.best[:]))
                link(nc.vector.tensor_tensor(v3(R.prob), v3(R.prob), row(R.top), ALU.mult))
                first_of_largest(R.one, R.prob, R.top, R.mark, R.best)
                if kind == "capacity":
                    nc.vector.engine_nop().then_inc(rank_in, 1)
                    dve.wait_ge(rank_ready, 1)
                    link(nc.vector.memset(R.two[:], 0.0))
                    link(nc.vector.tensor_copy(R.two[:, E:N], core.bankT[1][:, 0:N - E]))
                    a, b = R.two, R.mark
                    for shift in (1, 2, 4, 8, 16):
                        k = shift * E
                        nc.vector.tensor_copy(b[:, 0:k], a[:, 0:k]).then_inc(chain, 1)
                        done[0] += 1
                        link(nc.vector.tensor_tensor(b[:, k:N], a[:, k:N], a[:, 0:N - k], ALU.add))
                        a, b = b, a
                    link(nc.vector.tensor_tensor(a[:], a[:], core.bankT[0][:, 0:N], ALU.add))
                    link(nc.vector.tensor_scalar(a[:], a[:], float(CAPACITY), None, ALU.is_le))
                    link(nc.vector.tensor_tensor(R.one[:], R.one[:], a[:], ALU.mult))
                link(nc.vector.tensor_tensor(R.one[:], R.one[:], R.prob[:], ALU.mult))
            link(nc.vector.tensor_scalar(core.weight[:], R.one[:], tg, None, ALU.mult))

        @block.scalar
        def _(act):
            if kind == "top2":
                nc.scalar.activation(R.prob[:], core.logits[:], ACT.Sigmoid).then_inc(act_out, 1)
            else:
                act.wait_ge(act_in, 1)
                nc.scalar.activation(R.prob[:], R.left[:], ACT.Exp).then_inc(act_out, 1)

        @block.tensor
        def _(pe):
            if kind == "capacity":
                pe.wait_ge(rank_in, 1)
                nc.tensor.matmul(core.bankT[0][:, 0:N], core.upper[:], R.one[:], start=True, stop=True)
                nc.tensor.matmul(core.bankT[1][:, 0:N], core.ones[:], R.one[:], start=True, stop=True).then_inc(rank_ready, 1)


def feed_forward(nc, sem, core, w):
    hidden, hidden_out, y_ready, y_read, added, stats_new = (
        sem("hidden"), sem("hidden_out"), sem("y_ready"), sem("y_read"), sem("added"), sem("stats_new"))
    C, X = w.chunks, w.experts
    H = core.bankS
    Y = core.bankT
    W = BLOCK * P
    tiles_at = BLOCK // C if C < BLOCK else 1

    def steps():
        return range(2 * X)

    with nc.Block() as block:
        @block.tensor
        def _(pe):
            with pe.Fori(0, NBLK // 2) as i:
                for j in range(2 * X + 1):
                    e, half = j % X, j // X
                    for c in range(C):
                        if j < 2 * X:
                            k = j * C + c
                            if k >= 2:
                                pe.wait_ge(hidden_out, i * (2 * X * C) + k - 1)
                            else:
                                pe.wait_ge(hidden_out, i * (2 * X * C))
                            nc.tensor.matmul(H[k % 2][:, 0:W], w.w1[:, (e * C + c) * P:(e * C + c + 1) * P],
                                             core.xnT[:, bass.ds(i * (2 * W) + half * W, W)], start=True, stop=True).then_inc(hidden, 1)
                        if j >= 1:
                            t = j - 1
                            f = t % X
                            if c == 0:
                                pe.wait_ge(hidden_out, i * (2 * X * C) + (t + 1) * C)
                                if t >= 2:
                                    pe.wait_ge(y_read, i * (2 * X) + t - 1)
                                else:
                                    pe.wait_ge(y_read, i * (2 * X))
                            for q in range(c * tiles_at, (c + 1) * tiles_at):
                                for cc in range(C):
                                    last = nc.tensor.matmul(Y[t % 2][:, q * D:(q + 1) * D], core.hidden[t % 2][:, cc * W + q * P:cc * W + (q + 1) * P],
                                                            w.w2[:, (f * C + cc) * D:(f * C + cc + 1) * D], start=(cc == 0), stop=(cc == C - 1))
                            if c == C - 1:
                                last.then_inc(y_ready, 1)

        @block.scalar
        def _(act):
            with act.Fori(0, NBLK // 2) as i:
                for j in steps():
                    e = j % X
                    if j >= 2:
                        act.wait_ge(y_ready, i * (2 * X) + j - 1)
                    else:
                        act.wait_ge(y_ready, i * (2 * X))
                    for c in range(C):
                        k = j * C + c
                        act.wait_ge(hidden, i * (2 * X * C) + k + 1)
                        nc.scalar.activation(core.hidden[j % 2][:, c * W:(c + 1) * W], H[k % 2][:, 0:W], w.act,
                                             bias=w.b1[:, e * C + c:e * C + c + 1]).then_inc(hidden_out, 1)

        @block.vector
        def _(dve):
            with dve.Fori(0, NBLK // 2) as i:
                for j in steps():
                    e, half = j % X, j // X
                    dve.wait_ge(y_ready, i * (2 * X) + j + 1)
                    tiles = [i * (2 * BLOCK) + half * BLOCK + q for q in range(BLOCK)]

                    def weight(q):
                        if e >= w.routed:
                            return core.gate[:, w.gate:w.gate + 1]
                        return core.weight[:, bass.ds(tiles[q] * E + e, 1)]
                    if j:
                        dve.wait_ge(added, i * (2 * X) + j)
                    for q in range(BLOCK):
                        xt = tile_of(core.x, tiles[q])
                        last = nc.vector.scalar_tensor_tensor(out=xt, in0=Y[j % 2][:, q * D:(q + 1) * D], scalar=weight(q), in1=xt,
                                                              op0=ALU.mult, op1=ALU.add)
                    last.then_inc(y_read, 1)
                    dve.wait_ge(y_read, i * (2 * X) + j + 1)
                    for q in range(BLOCK):
                        xt = tile_of(core.x, tiles[q])
                        last = nc.vector.scalar_tensor_tensor(out=xt, in0=w.b2[:, e * D:(e + 1) * D], scalar=weight(q), in1=xt,
                                                              op0=ALU.mult, op1=ALU.add)
                    last.then_inc(added, 1)
                    if e == X - 1:
                        dve.wait_ge(added, i * (2 * X) + j + 1)
                        nc.vector.memset(core.pause[:], 0.0)
                        for q in range(BLOCK):
                            last = nc.vector.bn_stats(tile_of(core.stats, tiles[q], 6), tile_of(core.x, tiles[q]))
                        last.then_inc(stats_new, 1)
            dve.wait_ge(stats_new, NBLK)


class Named:
    pass


def program(nc, a, out):
    ctx = ExitStack()
    with ctx:
        phase = [""]

        def sb(name, cols, dt=F32):
            return ctx.enter_context(nc.sbuf_tensor(name, [P, cols], dt))

        taken = []

        def sem(name):
            taken.append(nc.alloc_semaphore(name=f"{phase[0]}_{name}"))
            return taken[-1]

        def give_back():
            with nc.Block() as block:
                @block.sync
                def _(sp):
                    for s in taken:
                        sp.sem_clear(s)
            for s in taken:
                nc.release_semaphore(s)
            taken.clear()

        core = Named()
        core.ctxT_dram = a["ctxT"]
        core.bankA = ctx.enter_context(nc.psum_tensor("bankA", [P, 512], F32))
        core.bankS = [ctx.enter_context(nc.psum_tensor(f"bankS{h}", [P, 1024], F32)) for h in range(2)]
        core.bankT = [ctx.enter_context(nc.psum_tensor(f"bankT{h}", [P, 512], F32)) for h in range(2)]
        core.bankO = ctx.enter_context(nc.psum_tensor("bankO", [P, 512], F32))
        core.x = sb("x", NB * D)
        core.xnT = sb("xnT", NB * P)
        core.key_on = sb("key_on", NB * P)
        core.key_neg = sb("key_neg", NB * P)
        core.stats, core.rstd, core.root = sb("stats", NB * 6), sb("rstd", NB), sb("root", NB)
        core.mean, core.var, core.half_sum, core.half_gap, core.pause = sb("mean", NB), sb("var", NB), sb("half_sum", NB), sb("half_gap", NB), sb("pause", 1)
        core.gate = sb("gate", 8)
        core.ident, core.ones, core.upper = sb("ident", P), sb("ones", P), sb("upper", P)
        core.head_of4, core.own_block, core.own_head = sb("head_of4", PER * P), sb("own_block", D), sb("own_head", HEADS)
        core.perm, core.even16 = sb("perm", P), sb("even16", 2)
        core.countdown = sb("countdown", NB * E)
        core.ctxT = [sb(f"ctxT{s}", P) for s in range(2)]
        core.xn = [sb(f"xn{s}", D) for s in range(2)]
        core.xnT1, core.bias, core.top, core.recip = sb("xnT1", P), sb("bias", P), sb("top", HEADS), sb("recip", HEADS)
        core.xnTs = [sb(f"xnTs{s}", P) for s in range(2)]
        core.k, core.kz, core.qz = sb("k", P), sb("kz", PER * P), sb("qz", GROUPS * P)
        core.v = [sb(f"v{s}", HEADS * (HD + 1)) for s in range(2)]
        core.o, core.oT, core.y = sb("o", D), sb("oT", P), sb("y", D)
        big = sb("big", 2 * HEADS * P + 2 * PER * P)
        core.probs = [big[:, s * HEADS * P:(s + 1) * HEADS * P] for s in range(2)]
        core.probsT = [big[:, 2 * HEADS * P + s * PER * P:2 * HEADS * P + (s + 1) * PER * P] for s in range(2)]
        core.hidden = core.probs
        L = core.lin = Named()
        L.xn, L.xnT, L.qkv, L.vx, L.kvm, L.qT = cut(big, (512, 512, 1536, 4 * 129, 4 * 144, 512))
        lin = sb("lin", 3 * 512 + 72 + 36 + 12 + 12 + 12 + 64 + 64)
        L.ctxT, L.attT, L.y, L.stat6, L.mean, L.total, L.gap, L.var, L.root, L.rs, L.z, L.zr = cut(
            lin, (512, 512, 512, 72, 12, 12, 12, 12, 12, 12, 64, 64))
        L.twice, L.turned, L.part, L.att = core.key_on[:, 0:1024], core.key_on[:, 1024:2048], core.key_on[:, 2048:2560], core.key_on[:, 2560:3072]
        core.logits, core.weight = sb("logits", NB * E), sb("weight", NB * E)
        R = core.route = Named()
        R.prob, R.one, R.two, R.mark, R.left = (sb("route_" + name, NB * E) for name in ("prob", "one", "two", "mark", "left"))
        R.top, R.best = sb("route_top", NB), sb("route_best", NB)
        w1_big = sb("w1_big", 9 * 4 * P)
        w2_big = sb("w2_big", 9 * 4 * D)
        b2_big = sb("b2_big", 9 * D)

        phase[0] = "setup"
        loaded, const0, const1, const2, gate_done = sem("loaded"), sem("const0"), sem("const1"), sem("const2"), sem("gate_done")
        first, chain, own1 = sem("first"), sem("chain"), sem("own1")
        W = {}
        loads = []

        def weight_tile(name, cols, src):
            t = sb(name, cols)
            loads.append((t[:], src))
            return t

        for l in (0, 2, 3):
            w = W[l] = Named()
            w.gate = l
            w.wq, w.wk, w.wv, w.wo = (weight_tile(f"w{k}{l}", D, a[f"w{k}{l}"]) for k in "qkvo")
            w.bq, w.bk = (weight_tile(f"b{k}{l}", 1, a[f"b{k}{l}"].rearrange("(p o) -> p o", o=1)) for k in "qk")
            w.bv, w.bo = (weight_tile(f"b{k}{l}", D, a[f"b{k}{l}"].partition_broadcast(P)) for k in "vo")
        w = W[1] = Named()
        w.gate = 1
        w.wq, w.wk, w.wv, w.wd = (weight_tile(f"w{k}1", D, a[f"w{k}1"]) for k in "qkvd")
        w.gamma, w.beta, w.bd = (weight_tile(n, D, a[n].partition_broadcast(P)) for n in ("gamma", "beta", "bd1"))
        w.em = weight_tile("em", NB, a["em"])
        src = weight_tile("src", P, a["src"])
        ffn = {}
        for l, X, C, router, act in ((0, 9, 4, "wr0", ACT.Gelu), (1, 8, 2, "wr1", ACT.Relu), (2, 8, 4, "wr2", ACT.Gelu), (3, 1, 4, None, ACT.Gelu)):
            f = ffn[l] = Named()
            f.experts, f.chunks, f.act, f.gate, f.routed = X, C, act, 4 + l, (0 if l == 3 else E)
            f.w1, f.w2, f.b2 = w1_big, w2_big, b2_big
            f.b1 = weight_tile(f"b1_{l}", X * C, a[f"b1_{l}"])
            f.router = weight_tile(router, E, a[router]) if router else None
            f.router_bias = sb(f"router_bias{l}", E)
        extra = sb("extra_bias", E)
        loads.append((ffn[0].router_bias[:], a["bg0"].partition_broadcast(P)))
        loads.append((extra[:], a["bias0"].partition_broadcast(P)))
        loads.append((ffn[1].router_bias[:], a["br1"].partition_broadcast(P)))
        loads.append((core.gate[:, 0:4], a["g_xattn"].partition_broadcast(P)))
        loads.append((core.gate[:, 4:8], a["g_ffn"].partition_broadcast(P)))
        loads.append((core.x[:].rearrange("p (n d) -> p n d", d=D), a["x"].rearrange("n p d -> p n d")))

        with nc.Block() as block:
            @block.sync
            def _(sp):
                for dst, s in loads:
                    sp.dma_start(dst, s).then_inc(loaded, 16)
                sp.wait_ge(loaded, 16 * len(loads))

            @block.gpsimd
            def _(pool):
                pool.memset(core.ones[:], 1.0)
                pool.memset(core.ident[:], 0.0)
                pool.memset(core.qz[:], 0.0)
                pool.memset(core.perm[:], 0.0)
                pool.memset(core.v[0][:], 1.0)
                pool.memset(core.v[1][:], 1.0)
                pool.memset(core.head_of4[:], 1.0)
                pool.memset(core.own_block[:], 1.0)
                pool.memset(core.own_head[:], 1.0)
                pool.iota(core.countdown[:], pattern=[[0, NB], [-1, E]], base=E, channel_multiplier=0,
                          allow_small_or_imprecise_dtypes=True).then_inc(const0, 1)
                pool.wait_ge(const0, 1)
                pool.affine_select(out=core.ident[:], in_=core.ident[:], compare_op=ALU.not_equal, fill=1.0, base=0,
                                   pattern=[[-1, P]], channel_multiplier=1).then_inc(const1, 1)
                pv = core.perm[:].rearrange("p (h a) -> p h a", h=HEADS)
                pool.affine_select(out=pv, in_=pv, compare_op=ALU.not_equal, fill=1.0, base=0,
                                   pattern=[[-1, HEADS], [-HEADS, P // HEADS]], channel_multiplier=1).then_inc(const1, 1)
                pool.affine_select(out=core.upper[:], in_=core.ones[:], compare_op=ALU.is_ge, fill=0.0, base=0,
                                   pattern=[[1, P]], channel_multiplier=-1).then_inc(const1, 1)
                for t, pat in ((core.own_head[:], [[-HD, HEADS]]), (core.own_block[:].rearrange("p (h c) -> p h c", c=HD), [[-HD, HEADS], [0, HD]])):
                    pool.affine_select(out=t, in_=t, compare_op=ALU.is_ge, fill=0.0, base=0, pattern=pat,
                                       channel_multiplier=1).then_inc(const1, 1)
                pool.wait_ge(const1, 5)
                for t, pat in ((core.own_head[:], [[HD, HEADS]]), (core.own_block[:].rearrange("p (h c) -> p h c", c=HD), [[HD, HEADS], [0, HD]])):
                    pool.affine_select(out=t, in_=t, compare_op=ALU.is_ge, fill=0.0, base=HD - 1, pattern=pat,
                                       channel_multiplier=-1).then_inc(const2, 1)

            @block.vector
            def _(dve):
                dve.wait_ge(const2, 2)
                hs = core.own_head[:].rearrange("p (g s) -> p s g", s=PER)
                nc.vector.tensor_reduce(out=core.top[:, 0:PER], in_=hs, op=ALU.max, axis=AX).then_inc(chain, 1)
                nc.vector.tensor_reduce(out=core.even16[:], in_=core.own_head[:].rearrange("p (q r s) -> p r q s", r=2, s=2), op=ALU.max,
                                        axis=mybir.AxisListType.XY).then_inc(chain, 1)
                dve.wait_ge(chain, 1)
                nc.vector.tensor_tensor(core.head_of4[:].rearrange("p (s k) -> p s k", k=P), core.head_of4[:].rearrange("p (s k) -> p s k", k=P),
                                        core.top[:, 0:PER].rearrange("p (s o) -> p s o", o=1).to_broadcast([P, PER, P]), ALU.mult).then_inc(chain, 1)
                dve.wait_ge(loaded, 16 * len(loads))
                nc.vector.tensor_tensor(ffn[0].router_bias[:], ffn[0].router_bias[:], extra[:], ALU.add).then_inc(chain, 1)
                nc.vector.memset(ffn[2].router_bias[:], 0.0).then_inc(chain, 1)
                for l in (0, 2, 3):
                    nc.vector.tensor_scalar(W[l].bq[:], W[l].bq[:], float(HD) ** -0.5, None, ALU.mult).then_inc(chain, 1)
                with dve.Fori(0, NB) as n:
                    nc.vector.bn_stats(tile_of(core.stats, n, 6), tile_of(core.x, n)).then_inc(first, 1)
                dve.wait_ge(first, NB)
                dve.wait_ge(chain, 8)

            @block.scalar
            def _(act):
                act.wait_ge(loaded, 16 * len(loads))
                nc.scalar.activation(core.gate[:], core.gate[:], ACT.Tanh).then_inc(gate_done, 1)

        def load_weights(l):
            f = ffn[l]
            phase[0] = f"load{l}"
            landed = sem("landed")
            parts = [(w1_big[:, 0:f.experts * f.chunks * P], a[f"w1_{l}"]),
                     (w2_big[:, 0:f.experts * f.chunks * D], a[f"w2_{l}"]),
                     (b2_big[:, 0:f.experts * D], a[f"b2_{l}"].partition_broadcast(P))]
            with nc.Block() as block:
                @block.sync
                def _(sp):
                    for dst, s in parts:
                        sp.dma_start(dst, s).then_inc(landed, 16)
                    sp.wait_ge(landed, 16 * len(parts))

        def load_mask(l):
            phase[0] = f"mask{l}"
            landed, on, neg = sem("landed"), sem("on"), sem("neg")
            raw = core.xnT[:].bitcast(I32) if l == 3 else core.xnT[:, 0:NB * P // 4].bitcast(U8)
            with nc.Block() as block:
                @block.sync
                def _(sp):
                    sp.dma_start(raw, a[f"mask{l}"].partition_broadcast(P)).then_inc(landed, 16)

                @block.vector
                def _(dve):
                    dve.wait_ge(landed, 16)
                    nc.vector.tensor_scalar(core.key_on[:], raw, 0.0, None, ALU.not_equal).then_inc(on, 1)
                    dve.wait_ge(on, 1)
                    nc.vector.tensor_scalar(core.key_neg[:], core.key_on[:], -1.0, NEG, ALU.add, ALU.mult).then_inc(neg, 1)
                    dve.wait_ge(neg, 1)

        for l in range(4):
            load_weights(l)
            phase[0] = f"norm{l}a"
            rebuild_norm_scale(nc, sem, core, EPS)
            if l == 1:
                phase[0] = "lin1"
                linear_attention_setup(nc, sem, core)
                linear_attention(nc, sem, core, W[1])
                phase[0] = "v1"
            else:
                if l >= 2:
                    load_mask(l)
                phase[0] = f"att{l}"
                softmax_attention(nc, sem, core, W[l], l >= 2, src if l == 3 else None)
            phase[0] = f"norm{l}f"
            rebuild_norm_scale(nc, sem, core, EPS)
            phase[0] = f"xnT{l}"
            norm_and_route(nc, sem, core, ffn[l])
            if l < 3:
                phase[0] = f"route{l}"
                route(nc, sem, core, ("top2", "top1", "capacity")[l], 4 + l)
            phase[0] = f"ffn{l}"
            feed_forward(nc, sem, core, ffn[l])
            give_back()
        phase[0] = "store"
        stored = sem("stored")
        with nc.Block() as block:
            @block.sync
            def _(sp):
                sp.dma_start(out.rearrange("n p d -> p n d"), core.x[:].rearrange("p (n d) -> p n d", d=D)).then_inc(stored, 16)
                sp.wait_ge(stored, 16)


def cut(buffer, widths):
    ends = [sum(widths[:k + 1]) for k in range(len(widths))]
    return [buffer[:, end - width:end] for end, width in zip(ends, widths)]


def linear_attention_setup(nc, sem, core):
    done = sem("ones_column")
    with nc.Block() as block:
        @block.vector
        def _(dve):
            nc.vector.memset(core.lin.vx[:], 1.0).then_inc(done, 1)
            dve.wait_ge(done, 1)


def laid_out(inputs):
    v = {k: np.asarray(x) for k, x in inputs.items()}
    g = {}
    g["x"] = v["x"]
    g["ctxT"] = v["ctx_1024"].transpose(0, 2, 1)
    for l in (0, 2, 3):
        for k in "qkvo":
            m = v[f"L{l}_xattn_W{k}"]
            g[f"w{k}{l}"] = m if l == 2 else m.T
            g[f"b{k}{l}"] = v[f"L{l}_xattn_b{k}"]
    g["wq1"], g["wk1"], g["wv1"], g["wd1"] = v["L1_xattn_wq"], v["L1_xattn_wk"], v["L1_xattn_wv"], v["L1_xattn_dense_w"]
    g["gamma"], g["beta"], g["bd1"] = v["L1_xattn_ln_gamma"], v["L1_xattn_ln_beta"], v["L1_xattn_dense_b"]
    g["em"] = v["mask_BxS2_ff1"].T
    g["src"] = v["mask_1x1xSxS2_ff0"].reshape(P, P)
    g["mask2"] = v["mask_Bx1xS2_bf1"].view(np.uint8).reshape(-1)
    g["mask3"] = v["mask_BxS2_ik0"].reshape(-1)
    g["g_xattn"], g["g_ffn"] = v["g_xattn"], v["g_ffn"]

    def first(m):
        return m.transpose(1, 0, 2).reshape(D, -1)

    def second(m):
        e, h, d = m.shape
        return m.reshape(e, h // P, P, d).transpose(2, 0, 1, 3).reshape(P, -1)

    def bias(m):
        e, h = m.shape
        return m.reshape(e, h // P, P).transpose(2, 0, 1).reshape(P, -1)

    g["w1_0"] = first(np.concatenate([v["L0_ffn_W1"], v["L0_ffn_Ws1"][None]]).transpose(0, 2, 1))
    g["w2_0"] = second(np.concatenate([v["L0_ffn_W2"], v["L0_ffn_Ws2"][None]]).transpose(0, 2, 1))
    g["b1_0"] = bias(np.concatenate([v["L0_ffn_b1"], v["L0_ffn_bs1"][None]]))
    g["b2_0"] = np.concatenate([v["L0_ffn_b2"], v["L0_ffn_bs2"][None]]).reshape(-1)
    g["wr0"], g["bg0"], g["bias0"] = v["L0_ffn_Wg"].T, v["L0_ffn_bg"], v["L0_ffn_bias"]
    g["w1_1"], g["w2_1"], g["b1_1"], g["b2_1"] = first(v["L1_ffn_W1"]), second(v["L1_ffn_W2"]), bias(v["L1_ffn_b1"]), v["L1_ffn_b2"].reshape(-1)
    g["wr1"], g["br1"] = v["L1_ffn_Wr"], v["L1_ffn_br"]
    g["w1_2"], g["w2_2"], g["b1_2"], g["b2_2"] = first(v["L2_ffn_w1"]), second(v["L2_ffn_w2"]), bias(v["L2_ffn_b1"]), v["L2_ffn_b2"].reshape(-1)
    g["wr2"] = v["L2_ffn_router_w"].T
    g["w1_3"], g["w2_3"] = v["L3_ffn_w1"], second(v["L3_ffn_w2"][None])
    g["b1_3"], g["b2_3"] = bias(v["L3_ffn_b1"][None]), v["L3_ffn_b2"]

    return g


def kernel(**inputs):
    import concourse.bacc as _bacc
    from concourse.bass_utils import run_bass_kernel_spmd as _run

    g = laid_out(inputs)
    nc = _bacc.Bacc("TRN2", target_bir_lowering=False, num_devices=1)
    arrays, args = {}, {}
    for name, m in g.items():
        m = np.ascontiguousarray(m)
        arrays[f"in_{name}"] = m
        args[name] = nc.dram_tensor(f"in_{name}", m.shape, mybir.dt.from_np(m.dtype), kind="ExternalInput").ap()
    out = nc.dram_tensor("out_x", (NB, P, D), F32, kind="ExternalOutput").ap()
    program(nc, args, out)
    r = _run(nc, [arrays], core_ids=[0])
    return r.results[0]["out_x"]
```

```python
import numpy as np
import concourse.bass as bass
from concourse import mybir
from contextlib import ExitStack

F32 = mybir.dt.float32
I32 = mybir.dt.int32
U8 = mybir.dt.uint8
ALU = mybir.AluOpType
ACT = mybir.ActivationFunctionType
AX = mybir.AxisListType.X

P = 128
D = 128
NB = 32
HEADS = 16
HD = D // HEADS
GROUPS = 4
PER = HEADS // GROUPS
VW = HEADS * (HD + 1)
E = 8
BLOCK = 4
NBLK = NB // BLOCK
CAPACITY = 768
EPS = 1e-5
EPS_LN1 = 1e-6
EPS_K = 1e-6
NEG = 1e9


class Batch:

    def __init__(self, i, c):
        self.i, self.c = i, c
        self.n = i * 2 + c if not isinstance(i, int) else 2 * i + c
        self.slot = c % 2
        self.turn = i + c // 2

    def shift(self, k):
        return Batch(self.i, self.c + k)


def wait(eng, sem, value):
    if isinstance(value, int) and value <= 0:
        return
    eng.wait_ge(sem, value)


def pipelined(eng, step):
    for c in range(-2, 4):
        step(Batch(0, c))
    with eng.Fori(0, (NB - 6) // 2) as i:
        for u in (0, 1):
            step(Batch(i, 4 + u))
    for c in range(NB - 2, NB + 2):
        step(Batch(0, c))


def exists(b):
    return not isinstance(b.n, int) or 0 <= b.n < NB


def own_strips(v):
    return v[:, 0:HEADS * (VW + HD + 1)].rearrange("p (h c) -> p h c", c=VW + HD + 1)[:, :, 0:HD + 1]


def tile_of(t, n, w=D):
    if isinstance(n, int):
        return t[:, n * w:(n + 1) * w]
    return t[:, bass.ds(n * w, w)]


def moments(nc, dve, chain, base, stats, mean, var, total, gap):
    s = stats.rearrange("p (n c) -> p n c", c=6)
    nc.vector.tensor_tensor(mean, s[:, :, 1], s[:, :, 4], ALU.add)
    nc.vector.tensor_tensor(gap, s[:, :, 1], s[:, :, 4], ALU.subtract)
    nc.vector.tensor_tensor(total, s[:, :, 2], s[:, :, 5], ALU.add).then_inc(chain, 1)
    dve.wait_ge(chain, base + 1)
    nc.vector.tensor_scalar(mean, mean, 0.5, None, ALU.mult)
    nc.vector.scalar_tensor_tensor(out=gap, in0=gap, scalar=0.25, in1=gap, op0=ALU.mult, op1=ALU.mult).then_inc(chain, 1)
    dve.wait_ge(chain, base + 2)
    nc.vector.scalar_tensor_tensor(out=var, in0=total, scalar=1.0 / D, in1=gap, op0=ALU.mult, op1=ALU.add).then_inc(chain, 1)
    dve.wait_ge(chain, base + 3)


def rebuild_norm_scale(nc, sem, core, eps):
    chain, ready, root = sem("chain"), sem("var_ready"), sem("root_ready")
    done = sem("rstd_ready")
    with nc.Block() as block:
        @block.vector
        def _(dve):
            moments(nc, dve, chain, 0, core.stats[:], core.mean[:], core.var[:], core.half_sum[:], core.half_gap[:])
            nc.vector.tensor_scalar(core.rstd[:], core.var[:], eps, None, ALU.add).then_inc(ready, 1)
            dve.wait_ge(root, 1)
            nc.vector.reciprocal(core.rstd[:], core.root[:]).then_inc(done, 1)
            dve.wait_ge(done, 1)

        @block.scalar
        def _(act):
            act.wait_ge(ready, 1)
            nc.scalar.activation(core.root[:], core.rstd[:], ACT.Sqrt).then_inc(root, 1)


def softmax_attention(nc, sem, core, w, masked, src):
    ctx_in = [sem("ctx_in0"), sem("ctx_in1")]
    xn_ready = sem("xn_ready")
    xnT_ready, xnT_out = sem("xnT_ready"), sem("xnT_out")
    proj = sem("proj")
    q_out, k_out, v_out, v_placed = sem("q_out"), sem("k_out"), sem("v_out"), sem("v_placed")
    k_plain, bias_ready = sem("k_plain"), sem("bias_ready")
    scores, biased, top, shifted, expd = sem("scores"), sem("biased"), sem("top"), sem("shifted"), sem("expd")
    turned, probs_out, mixed = sem("turned"), sem("probs_out"), sem("mixed")
    recip, normed = sem("recip"), sem("normed")
    oT_ready, oT_out, y_ready = sem("oT_ready"), sem("oT_out"), sem("y_ready")
    y_read, x_new, stats_new = sem("y_read"), sem("x_new"), sem("stats_new")
    A, S, T, O = core.bankA, core.bankS, core.bankT, core.bankO
    q_norm = float(HD) ** -0.5
    heads8 = lambda a: a.rearrange("p (h k) -> p h k", k=P)

    with nc.Block() as block:
        @block.sync
        def _(sp):
            def load(b):
                wait(sp, proj, b.n - 1)
                sp.dma_start(core.ctxT[b.slot][:], core.ctxT_dram[bass.ds(b.n, 1) if not isinstance(b.n, int) else slice(b.n, b.n + 1)]
                             .rearrange("o d t -> d (o t)")).then_inc(ctx_in[b.slot], 16)
            load(Batch(0, 0))
            load(Batch(0, 1))
            with sp.Fori(0, (NB - 2) // 2) as i:
                for u in (0, 1):
                    load(Batch(i, 2 + u))

        @block.vector
        def _(dve):
            def norm_x(n):
                wait(dve, xnT_ready, n.n - 1)
                nc.vector.tensor_scalar(core.xn[n.slot][:], tile_of(core.x, n.n), tile_of(core.mean, n.n, 1),
                                        tile_of(core.rstd, n.n, 1), ALU.subtract, ALU.mult).then_inc(xn_ready, 1)

            def norm_o(n):
                o = O[:, 0:VW].rearrange("p (h c) -> p h c", c=HD + 1)
                wait(dve, mixed, n.n * 4 + 4)
                nc.vector.reciprocal(core.recip[:], o[:, :, HD]).then_inc(recip, 1)
                wait(dve, recip, n.n + 1)
                wait(dve, oT_ready, n.n)
                nc.vector.tensor_tensor(core.o[:].rearrange("p (h c) -> p h c", c=HD), o[:, :, 0:HD],
                                        core.recip[:].rearrange("p (h o) -> p h o", o=1).to_broadcast([P, HEADS, HD]), ALU.mult).then_inc(normed, 1)

            def keys_values(n):
                wait(dve, proj, n.n + 1)
                wait(dve, scores, n.n * 2 - 2)
                kz = core.kz[n.slot][:].rearrange("p (s k) -> p s k", k=P)
                ms = core.head_of4[:].rearrange("p (s k) -> p s k", k=P)
                if masked:
                    nc.vector.scalar_tensor_tensor(out=core.k[:], in0=T[0][:, 0:P], scalar=w.bk[:, 0:1],
                                                   in1=tile_of(core.key_on, n.n), op0=ALU.add, op1=ALU.mult).then_inc(k_plain, 1)
                    wait(dve, k_plain, n.n + 1)
                    nc.vector.tensor_tensor(kz, core.k[:].rearrange("p (o k) -> p o k", o=1).to_broadcast([P, PER, P]),
                                            ms, ALU.mult).then_inc(k_out, 1)
                else:
                    nc.vector.scalar_tensor_tensor(out=kz, in0=T[0][:, 0:P].rearrange("p (o k) -> p o k", o=1).to_broadcast([P, PER, P]),
                                                   scalar=w.bk[:, 0:1], in1=ms, op0=ALU.add, op1=ALU.mult).then_inc(k_out, 1)
                wait(dve, v_placed, n.n)
                nc.vector.tensor_copy(core.v_early[:], T[0][:, P:2 * P]).then_inc(v_out, 1)

            def softmax(n, hf):
                if hf == 0 and masked:
                    if src is None:
                        nc.vector.tensor_copy(core.bias[:], tile_of(core.key_neg, n.n)).then_inc(bias_ready, 1)
                    else:
                        nc.vector.tensor_tensor(core.bias[:], tile_of(core.key_neg, n.n), src[:], ALU.add).then_inc(bias_ready, 1)
                    wait(dve, bias_ready, n.n + 1)
                wait(dve, scores, n.n * 2 + hf + 1)
                wait(dve, turned, n.n * 4 - 4)
                half = core.probs[n.slot][:, hf * 1024:(hf + 1) * 1024]
                source = S[hf][:]
                if masked:
                    nc.vector.tensor_tensor(heads8(half), heads8(source), core.bias[:].rearrange("p (o k) -> p o k", o=1).to_broadcast([P, 8, P]),
                                            ALU.add).then_inc(biased, 1)
                    wait(dve, biased, n.n * 2 + hf + 1)
                    source = half
                m = core.top[:, hf * 8:hf * 8 + 8]
                nc.vector.tensor_reduce(out=m, in_=heads8(source), op=ALU.max, axis=AX).then_inc(top, 1)
                wait(dve, top, n.n * 2 + hf + 1)
                nc.vector.tensor_tensor(heads8(half), heads8(source), m.rearrange("p (h o) -> p h o", o=1).to_broadcast([P, 8, P]),
                                        ALU.subtract).then_inc(shifted, 1)

            def add_to_x(n):
                xt = tile_of(core.x, n.n)
                wait(dve, x_new, n.n)
                wait(dve, y_ready, n.n + 1)
                nc.vector.tensor_tensor(core.y[:], O[:, 384:512], w.bo[:], ALU.add).then_inc(y_read, 1)
                wait(dve, y_read, n.n + 1)
                nc.vector.scalar_tensor_tensor(out=xt, in0=core.y[:], scalar=core.gate[:, w.gate:w.gate + 1], in1=xt,
                                               op0=ALU.mult, op1=ALU.add).then_inc(x_new, 1)
                if not (isinstance(n.n, int) and n.n == 0):
                    nc.vector.bn_stats(tile_of(core.stats, n.n - 1, 6), tile_of(core.x, n.n - 1)).then_inc(stats_new, 1)

            def step(b):
                if exists(b.shift(2)):
                    norm_x(b.shift(2))
                if exists(b.shift(-2)):
                    norm_o(b.shift(-2))
                if exists(b.shift(1)):
                    keys_values(b.shift(1))
                if exists(b):
                    softmax(b, 0)
                if exists(b.shift(-2)):
                    add_to_x(b.shift(-2))
                if exists(b):
                    softmax(b, 1)
            pipelined(dve, step)
            dve.wait_ge(x_new, NB)
            nc.vector.bn_stats(tile_of(core.stats, NB - 1, 6), tile_of(core.x, NB - 1)).then_inc(stats_new, 1)
            dve.wait_ge(stats_new, NB)

        @block.gpsimd
        def _(pool):
            def place(b):
                wait(pool, v_out, b.n + 1)
                wait(pool, mixed, b.n * 4 - 4)
                nc.gpsimd.tensor_tensor(own_strips(core.v[b.slot])[:, :, 0:HD], core.v_early[:].rearrange("p (h c) -> p h c", c=HD),
                                        w.bv[:].rearrange("p (h c) -> p h c", c=HD), ALU.add).then_inc(v_placed, 1)
            place(Batch(0, 0))
            place(Batch(0, 1))
            with pool.Fori(0, (NB - 2) // 2) as i:
                for u in (0, 1):
                    place(Batch(i, 2 + u))

        @block.scalar
        def _(act):
            def step(b):
                first, n, c, o = b.shift(2), b.shift(1), b.shift(-1), b.shift(-2)
                if exists(n):
                    wait(act, proj, n.n + 1)
                    wait(act, scores, n.n * 2 - 2)
                    if exists(first):
                        wait(act, xnT_ready, first.n + 1)
                    for g in range(GROUPS):
                        r = slice(32 * g, 32 * g + 32)
                        nc.scalar.activation(core.qz[n.slot][r, g * P:(g + 1) * P], A[r, 128:256], ACT.Identity,
                                             bias=w.bq[r, 0:1], scale=q_norm).then_inc(q_out, 1)
                if exists(first):
                    wait(act, xnT_ready, first.n + 1)
                    wait(act, proj, first.n - 1)
                    nc.scalar.activation(core.xnTs[first.slot][:], A[:, 0:128], ACT.Copy).then_inc(xnT_out, 1)
                if exists(o):
                    wait(act, oT_ready, o.n + 1)
                    wait(act, y_ready, o.n)
                    nc.scalar.activation(core.oT[:], A[:, 256:384], ACT.Copy).then_inc(oT_out, 1)
                if exists(c):
                    for g in range(GROUPS):
                        wait(act, turned, c.n * 4 + g + 1)
                        wait(act, mixed, c.n * 4 + g - 1)
                        nc.scalar.activation(core.probsT[g % 2][:], T[g % 2][:], ACT.Copy).then_inc(probs_out, 1)
                if exists(b):
                    for hf in range(2):
                        wait(act, shifted, b.n * 2 + hf + 1)
                        half = core.probs[b.slot][:, hf * 1024:(hf + 1) * 1024]
                        nc.scalar.activation(half, half, ACT.Exp).then_inc(expd, 1)
            pipelined(act, step)

        @block.tensor
        def _(pe):
            def project(n):
                wait(pe, ctx_in[n.slot], (n.turn + 1) * 16)
                wait(pe, xnT_out, n.n + 1)
                wait(pe, oT_out, n.n - 3)
                wait(pe, probs_out, n.n * 4 - 8)
                wait(pe, v_out, n.n)
                nc.tensor.matmul(A[:, 128:256], w.wq[:], core.xnTs[n.slot][:], start=True, stop=True)
                nc.tensor.matmul(T[0][:, 0:P], w.wk[:], core.ctxT[n.slot][:], start=True, stop=True)
                nc.tensor.matmul(T[0][:, P:2 * P], core.ctxT[n.slot][:], w.wv[:], start=True, stop=True).then_inc(proj, 1)

            def turn_x(n):
                wait(pe, xn_ready, n.n + 1)
                wait(pe, oT_out, n.n - 4)
                wait(pe, q_out, n.n * 4 - 4)
                nc.tensor.transpose(A[:, 0:128], core.xn[n.slot][:], core.ident[:]).then_inc(xnT_ready, 1)

            def score(n, g):
                if g == 0:
                    wait(pe, q_out, n.n * 4 + 4)
                    wait(pe, k_out, n.n + 1)
                if g % 2 == 0:
                    wait(pe, shifted, n.n * 2 + g // 2 - 1)
                last = nc.tensor.matmul(S[g // 2][:, (g % 2) * 512:(g % 2) * 512 + 512], core.qz[n.slot][:, g * P:(g + 1) * P],
                                        core.kz[n.slot][:], start=True, stop=True)
                if g % 2:
                    last.then_inc(scores, 1)

            def turn(n, g):
                if g == 0:
                    wait(pe, v_out, n.n + 3 if exists(n.shift(2)) else NB)
                wait(pe, expd, n.n * 2 + g // 2 + 1)
                wait(pe, probs_out, n.n * 4 + g - 1)
                for s in range(PER):
                    h = g * PER + s
                    last = nc.tensor.transpose(T[g % 2][:, s * P:(s + 1) * P], core.probs[n.slot][:, h * P:(h + 1) * P], core.ident[:])
                last.then_inc(turned, 1)

            def mix(n, g):
                wait(pe, probs_out, n.n * 4 + g + 1)
                if g == 0:
                    wait(pe, y_read, n.n)
                    wait(pe, v_placed, n.n + 1)
                for s in range(PER):
                    h = g * PER + s
                    last = nc.tensor.matmul(O[:, 0:VW], core.probsT[g % 2][:, s * P:(s + 1) * P],
                                            core.v[n.slot][:, h * VW:(h + 1) * VW], start=(h == 0), stop=(h == HEADS - 1))
                last.then_inc(mixed, 1)

            def step(b):
                first, n, c, o = b.shift(2), b.shift(1), b.shift(-1), b.shift(-2)
                if exists(n):
                    project(n)
                if exists(first):
                    turn_x(first)
                if exists(b):
                    score(b, 0)
                    score(b, 1)
                if exists(o):
                    wait(pe, normed, o.n + 1)
                    if exists(n):
                        wait(pe, q_out, n.n * 4 + 4)
                    if exists(first):
                        wait(pe, xnT_out, first.n + 1)
                    nc.tensor.transpose(A[:, 256:384], core.o[:], core.ident[:]).then_inc(oT_ready, 1)
                if exists(b):
                    score(b, 2)
                if exists(o):
                    wait(pe, oT_out, o.n + 1)
                    nc.tensor.matmul(O[:, 384:512], core.oT[:], w.wo[:], start=True, stop=True).then_inc(y_ready, 1)
                if exists(b):
                    score(b, 3)
                if exists(c):
                    turn(c, 0), turn(c, 1), mix(c, 0), turn(c, 2), mix(c, 1), turn(c, 3), mix(c, 2), mix(c, 3)
            pipelined(pe, step)


def linear_attention(nc, sem, core, w):
    ctx_in, xn_ready, xnT_ready, xnT_out = sem("ctx_in"), sem("xn_ready"), sem("xnT_ready"), sem("xnT_out")
    proj, chain, var_ready, root_ready = sem("proj"), sem("chain"), sem("var_ready"), sem("root_ready")
    kv_in, kv_ready, qT_ready, qT_out, kv_out = sem("kv_in"), sem("kv_ready"), sem("qT_ready"), sem("qT_out"), sem("kv_out")
    att_ready, att_out, attT_ready, attT_out, y_ready = sem("att_ready"), sem("att_out"), sem("attT_ready"), sem("attT_out"), sem("y_ready")
    S, T, A, O = core.bankS, core.bankT, core.bankA, core.bankO
    B4 = BLOCK
    where = [S[0][:, 0:512], S[0][:, 512:1024], S[1][:, 0:512]]
    L = core.lin
    STEPS = 25

    with nc.Block() as block:
        @block.sync
        def _(sp):
            with sp.Fori(0, NB // B4) as r:
                wait(sp, proj, r)
                sp.dma_start(L.ctxT[:].rearrange("d (b t) -> d b t", b=B4),
                             core.ctxT_dram[bass.ds(r * B4, B4)].rearrange("b d t -> d b t")).then_inc(ctx_in, 16)

        @block.vector
        def _(dve):
            with dve.Fori(0, NB // B4) as r:
                done = [0]

                def link(ins):
                    done[0] += 1
                    ins.then_inc(chain, 1)
                    dve.wait_ge(chain, r * STEPS + done[0])

                for j in range(B4):
                    n = r * B4 + j
                    ins = nc.vector.tensor_scalar(L.xn[:, j * D:(j + 1) * D], tile_of(core.x, n), tile_of(core.mean, n, 1),
                                                  tile_of(core.rstd, n, 1), ALU.subtract, ALU.mult)
                ins.then_inc(xn_ready, 1)
                dve.wait_ge(proj, r + 1)
                for t in range(3):
                    for j in range(B4):
                        i = t * B4 + j
                        last = nc.vector.bn_stats(L.stat6[:, i * 6:i * 6 + 6], where[t][:, j * D:(j + 1) * D])
                link(last)
                moments(nc, dve, chain, r * STEPS + done[0], L.stat6[:, 0:72], L.mean[:, 0:12], L.var[:, 0:12], L.total[:, 0:12], L.gap[:, 0:12])
                done[0] += 3
                nc.vector.tensor_scalar(L.var[:, 0:12], L.var[:, 0:12], EPS_LN1, None, ALU.add).then_inc(var_ready, 1)
                dve.wait_ge(root_ready, r * 2 + 1)
                link(nc.vector.reciprocal(L.rs[:, 0:12], L.root[:, 0:12]))
                for t in range(3):
                    for j in range(B4):
                        i = t * B4 + j
                        last = nc.vector.tensor_scalar(L.qkv[:, i * D:(i + 1) * D], where[t][:, j * D:(j + 1) * D], L.mean[:, i:i + 1],
                                                       L.rs[:, i:i + 1], ALU.subtract, ALU.mult)
                link(last)
                every = L.qkv[:].rearrange("p (i d) -> p i d", d=D)
                bc = lambda a, k: a[:].rearrange("p (o d) -> p o d", o=1).to_broadcast([P, k, D])
                link(nc.vector.tensor_tensor(every, every, bc(w.gamma, 12), ALU.mult))
                link(nc.vector.tensor_tensor(every, every, bc(w.beta, 12), ALU.add))
                link(nc.vector.tensor_scalar(L.qkv[:, 0:8 * D], L.qkv[:, 0:8 * D], 0.0, EPS_K, ALU.max, ALU.add))
                for j in range(B4):
                    n = r * B4 + j
                    k = L.qkv[:, (4 + j) * D:(5 + j) * D]
                    nc.vector.tensor_scalar(k, k, tile_of(w.em, n, 1), None, ALU.mult)
                    last = nc.vector.tensor_scalar(L.vx[:, j * 129:j * 129 + D], L.qkv[:, (8 + j) * D:(9 + j) * D], tile_of(w.em, n, 1), None, ALU.mult)
                last.then_inc(kv_in, 1)
                dve.wait_ge(kv_ready, r + 1)
                for j in range(B4):
                    src = (A if j < 2 else O)[:, (j % 2) * 256:(j % 2) * 256 + 129]
                    nc.vector.tensor_tensor(L.kvm[:, j * 144:j * 144 + D], src[:, 0:D], core.own_block[:], ALU.mult)
                    last = nc.vector.tensor_scalar(L.kvm[:, j * 144 + D:(j + 1) * 144], core.own_head[:], src[:, D:D + 1], None, ALU.mult)
                last.then_inc(kv_out, 1)
                dve.wait_ge(att_ready, r + 1)
                for j in range(B4):
                    z = T[j // 2][:, (j % 2) * 256 + D:(j % 2) * 256 + 144]
                    last = nc.vector.tensor_scalar(L.z[:, j * 16:(j + 1) * 16], z, EPS_K, None, ALU.add)
                link(last)
                link(nc.vector.reciprocal(L.zr[:], L.z[:]))
                for j in range(B4):
                    a = T[j // 2][:, (j % 2) * 256:(j % 2) * 256 + D].rearrange("p (h c) -> p c h", c=HD)
                    z = L.zr[:, j * 16:(j + 1) * 16].rearrange("p (o h) -> p o h", o=1).to_broadcast([P, HD, HEADS])
                    to = L.twice[:, j * 256:(j + 1) * 256].rearrange("p (c x h) -> p c x h", x=2, h=HEADS)
                    for x in range(2):
                        last = nc.vector.tensor_tensor(to[:, :, x, :], a, z, ALU.mult)
                link(last)
                link(nc.vector.transpose(L.turned[:], L.twice[:]))
                for j in range(B4):
                    tv = L.turned[:, j * 256:(j + 1) * 256].rearrange("p (c x m) -> p x c m", x=2, m=HEADS)
                    last = nc.vector.tensor_scalar(L.part[:, j * D:(j + 1) * D].rearrange("p (c m) -> p c m", c=HD), tv[:, 0], core.even16[:, 0:1], None, ALU.mult)
                link(last)
                for j in range(B4):
                    tv = L.turned[:, j * 256:(j + 1) * 256].rearrange("p (c x m) -> p x c m", x=2, m=HEADS)
                    last = nc.vector.scalar_tensor_tensor(out=L.att[:, j * D:(j + 1) * D].rearrange("p (m c) -> p c m", c=HD), in0=tv[:, 1],
                                                          scalar=core.even16[:, 1:2], in1=L.part[:, j * D:(j + 1) * D].rearrange("p (c m) -> p c m", c=HD),
                                                          op0=ALU.mult, op1=ALU.add)
                last.then_inc(att_out, 1)
                dve.wait_ge(y_ready, r + 1)
                y = S[1][:, 512:1024].rearrange("p (j d) -> p j d", d=D)
                yb = L.y[:].rearrange("p (j d) -> p j d", d=D)
                link(nc.vector.tensor_tensor(yb, y, bc(w.bd, B4), ALU.add))
                for j in range(B4):
                    last = nc.vector.bn_stats(L.stat6[:, j * 6:j * 6 + 6], L.y[:, j * D:(j + 1) * D])
                link(last)
                moments(nc, dve, chain, r * STEPS + done[0], L.stat6[:, 0:24], L.mean[:, 0:B4], L.var[:, 0:B4], L.total[:, 0:B4], L.gap[:, 0:B4])
                done[0] += 3
                nc.vector.tensor_scalar(L.var[:, 0:B4], L.var[:, 0:B4], EPS_LN1, None, ALU.add).then_inc(var_ready, 1)
                dve.wait_ge(root_ready, r * 2 + 2)
                link(nc.vector.reciprocal(L.rs[:, 0:B4], L.root[:, 0:B4]))
                for j in range(B4):
                    last = nc.vector.tensor_scalar(L.y[:, j * D:(j + 1) * D], L.y[:, j * D:(j + 1) * D], L.mean[:, j:j + 1],
                                                   L.rs[:, j:j + 1], ALU.subtract, ALU.mult)
                link(last)
                link(nc.vector.tensor_tensor(yb, yb, bc(w.gamma, B4), ALU.mult))
                link(nc.vector.tensor_tensor(yb, yb, bc(w.beta, B4), ALU.add))
                xt = core.x[:, bass.ds(r * (B4 * D), B4 * D)]
                link(nc.vector.scalar_tensor_tensor(out=L.y[:], in0=L.y[:], scalar=core.gate[:, w.gate:w.gate + 1], in1=xt, op0=ALU.mult, op1=ALU.add))
                nc.vector.tensor_scalar(xt, L.y[:], 1.0, None, ALU.mult)
                for j in range(B4):
                    last = nc.vector.bn_stats(tile_of(core.stats, r * B4 + j, 6), L.y[:, j * D:(j + 1) * D])
                link(last)
                assert done[0] == STEPS, done[0]

        @block.scalar
        def _(act):
            with act.Fori(0, NB // B4) as r:
                act.wait_ge(xnT_ready, r + 1)
                nc.scalar.activation(L.xnT[:], A[:, 0:512], ACT.Copy).then_inc(xnT_out, 1)
                act.wait_ge(var_ready, r * 2 + 1)
                nc.scalar.activation(L.root[:, 0:12], L.var[:, 0:12], ACT.Sqrt).then_inc(root_ready, 1)
                act.wait_ge(qT_ready, r + 1)
                nc.scalar.activation(L.qT[:], S[1][:, 512:1024], ACT.Copy).then_inc(qT_out, 1)
                act.wait_ge(attT_ready, r + 1)
                nc.scalar.activation(L.attT[:], A[:, 0:512], ACT.Copy).then_inc(attT_out, 1)
                act.wait_ge(var_ready, r * 2 + 2)
                nc.scalar.activation(L.root[:, 0:B4], L.var[:, 0:B4], ACT.Sqrt).then_inc(root_ready, 1)

        @block.tensor
        def _(pe):
            with pe.Fori(0, NB // B4) as r:
                pe.wait_ge(xn_ready, r + 1)
                for j in range(B4):
                    last = nc.tensor.transpose(A[:, j * P:(j + 1) * P], L.xn[:, j * D:(j + 1) * D], core.ident[:])
                last.then_inc(xnT_ready, 1)
                pe.wait_ge(ctx_in, r * 16 + 16)
                pe.wait_ge(xnT_out, r + 1)
                for t, (left, right) in enumerate(((L.xnT, w.wq), (L.ctxT, w.wk), (L.ctxT, w.wv))):
                    for j in range(B4):
                        last = nc.tensor.matmul(where[t][:, j * D:(j + 1) * D], left[:, j * P:(j + 1) * P], right[:], start=True, stop=True)
                last.then_inc(proj, 1)
                pe.wait_ge(kv_in, r + 1)
                for j in range(B4):
                    last = nc.tensor.matmul((A if j < 2 else O)[:, (j % 2) * 256:(j % 2) * 256 + 129], L.qkv[:, (4 + j) * D:(5 + j) * D],
                                            L.vx[:, j * 129:(j + 1) * 129], start=True, stop=True)
                last.then_inc(kv_ready, 1)
                for j in range(B4):
                    last = nc.tensor.transpose(S[1][:, 512 + j * P:512 + (j + 1) * P], L.qkv[:, j * D:(j + 1) * D], core.ident[:])
                last.then_inc(qT_ready, 1)
                pe.wait_ge(qT_out, r + 1)
                pe.wait_ge(kv_out, r + 1)
                for j in range(B4):
                    last = nc.tensor.matmul(T[j // 2][:, (j % 2) * 256:(j % 2) * 256 + 144], L.qT[:, j * P:(j + 1) * P],
                                            L.kvm[:, j * 144:(j + 1) * 144], start=True, stop=True)
                last.then_inc(att_ready, 1)
                pe.wait_ge(att_out, r + 1)
                for j in range(B4):
                    last = nc.tensor.transpose(A[:, j * P:(j + 1) * P], L.att[:, j * D:(j + 1) * D], core.perm[:])
                last.then_inc(attT_ready, 1)
                pe.wait_ge(attT_out, r + 1)
                for j in range(B4):
                    last = nc.tensor.matmul(S[1][:, 512 + j * D:512 + (j + 1) * D], L.attT[:, j * P:(j + 1) * P], w.wd[:], start=True, stop=True)
                last.then_inc(y_ready, 1)


def norm_and_route(nc, sem, core, w):
    xn_ready, xnT_ready, xnT_out, logit_ready, logit_out = (sem("xn_ready"), sem("xnT_ready"), sem("xnT_out"), sem("logit_ready"), sem("logit_out"))
    T, A = core.bankT, [core.bankA, core.bankO]
    routed = w.router is not None
    per = 2 if routed else 1
    with nc.Block() as block:
        @block.vector
        def _(dve):
            with dve.Fori(0, NB // 2) as i:
                for u in (0, 1):
                    n = Batch(i, u)
                    wait(dve, xnT_ready, n.n - 1) if u else wait(dve, xnT_ready, n.i * 2)
                    nc.vector.tensor_scalar(core.xn[u][:], tile_of(core.x, n.n), tile_of(core.mean, n.n, 1),
                                            tile_of(core.rstd, n.n, 1), ALU.subtract, ALU.mult).then_inc(xn_ready, 1)
                if routed:
                    for u in (0, 1):
                        n = Batch(i, u)
                        dve.wait_ge(logit_ready, n.n + 1)
                        nc.vector.tensor_tensor(tile_of(core.logits, n.n, E), A[u][:, 0:E], w.router_bias[:], ALU.add).then_inc(logit_out, 1)

        @block.scalar
        def _(act):
            with act.Fori(0, NB // 2) as i:
                for u in (0, 1):
                    n = Batch(i, u)
                    act.wait_ge(xnT_ready, n.n + 1)
                    if routed:
                        act.wait_ge(logit_ready, i * 2)
                        nc.scalar.activation(core.xnTs[u][:], T[u][:, 0:P], ACT.Copy).then_inc(xnT_out, 1)
                    nc.scalar.activation(tile_of(core.xnT, n.n), T[u][:, 0:P], ACT.Copy).then_inc(xnT_out, 1)

        @block.tensor
        def _(pe):
            with pe.Fori(0, NB // 2) as i:
                for u in (0, 1):
                    n = Batch(i, u)
                    pe.wait_ge(xn_ready, n.n + 1)
                    pe.wait_ge(xnT_out, i * (2 * per))
                    nc.tensor.transpose(T[u][:, 0:P], core.xn[u][:], core.ident[:]).then_inc(xnT_ready, 1)
                if routed:
                    for u in (0, 1):
                        n = Batch(i, u)
                        pe.wait_ge(xnT_out, n.n * 2 + 1)
                        pe.wait_ge(logit_out, i * 2)
                        nc.tensor.matmul(A[u][:, 0:E], core.xnTs[u][:], w.router[:], start=True, stop=True).then_inc(logit_ready, 1)


def route(nc, sem, core, kind, gate):
    chain, act_in, act_out, rank_in, rank_ready = sem("chain"), sem("act_in"), sem("act_out"), sem("rank_in"), sem("rank_ready")
    R = core.route
    N = NB * E
    v3 = lambda a: a[:].rearrange("p (n e) -> p n e", e=E)
    row = lambda a: a[:].rearrange("p (n o) -> p n o", o=1).to_broadcast([P, NB, E])
    tg = core.gate[:, gate:gate + 1]
    with nc.Block() as block:
        @block.vector
        def _(dve):
            done = [0]

            def link(ins):
                done[0] += 1
                ins.then_inc(chain, 1)
                dve.wait_ge(chain, done[0])

            def first_of_largest(out, values, top, mark, best):
                link(nc.vector.tensor_reduce(out=top[:], in_=v3(values), op=ALU.max, axis=AX))
                link(nc.vector.tensor_tensor(v3(mark), v3(values), row(top), ALU.is_equal))
                link(nc.vector.tensor_tensor(mark[:], mark[:], core.countdown[:], ALU.mult))
                link(nc.vector.tensor_reduce(out=best[:], in_=v3(mark), op=ALU.max, axis=AX))
                link(nc.vector.tensor_tensor(v3(out), v3(mark), row(best), ALU.is_equal))

            if kind == "top2":
                dve.wait_ge(act_out, 1)
                first_of_largest(R.one, R.prob, R.top, R.mark, R.best)
                link(nc.vector.tensor_scalar(R.left[:], R.one[:], -1.0, 1.0, ALU.mult, ALU.add))
                link(nc.vector.tensor_tensor(R.left[:], R.prob[:], R.left[:], ALU.mult))
                link(nc.vector.tensor_tensor(R.left[:], R.left[:], R.one[:], ALU.subtract))
                first_of_largest(R.two, R.left, R.top, R.mark, R.best)
                link(nc.vector.tensor_tensor(R.one[:], R.one[:], R.two[:], ALU.add))
                link(nc.vector.tensor_tensor(R.one[:], R.one[:], R.prob[:], ALU.mult))
            else:
                link(nc.vector.tensor_reduce(out=R.top[:], in_=v3(core.logits), op=ALU.max, axis=AX))
                nc.vector.tensor_tensor(v3(R.left), v3(core.logits), row(R.top), ALU.subtract).then_inc(act_in, 1)
                dve.wait_ge(act_out, 1)
                link(nc.vector.tensor_reduce(out=R.best[:], in_=v3(R.prob), op=ALU.add, axis=AX))
                link(nc.vector.reciprocal(R.top[:], R.best[:]))
                link(nc.vector.tensor_tensor(v3(R.prob), v3(R.prob), row(R.top), ALU.mult))
                first_of_largest(R.one, R.prob, R.top, R.mark, R.best)
                if kind == "capacity":
                    nc.vector.engine_nop().then_inc(rank_in, 1)
                    dve.wait_ge(rank_ready, 1)
                    link(nc.vector.memset(R.two[:], 0.0))
                    link(nc.vector.tensor_copy(R.two[:, E:N], core.bankT[1][:, 0:N - E]))
                    a, b = R.two, R.mark
                    for shift in (1, 2, 4, 8, 16):
                        k = shift * E
                        nc.vector.tensor_copy(b[:, 0:k], a[:, 0:k]).then_inc(chain, 1)
                        done[0] += 1
                        link(nc.vector.tensor_tensor(b[:, k:N], a[:, k:N], a[:, 0:N - k], ALU.add))
                        a, b = b, a
                    link(nc.vector.tensor_tensor(a[:], a[:], core.bankT[0][:, 0:N], ALU.add))
                    link(nc.vector.tensor_scalar(a[:], a[:], float(CAPACITY), None, ALU.is_le))
                    link(nc.vector.tensor_tensor(R.one[:], R.one[:], a[:], ALU.mult))
                link(nc.vector.tensor_tensor(R.one[:], R.one[:], R.prob[:], ALU.mult))
            link(nc.vector.tensor_scalar(core.weight[:], R.one[:], tg, None, ALU.mult))

        @block.scalar
        def _(act):
            if kind == "top2":
                nc.scalar.activation(R.prob[:], core.logits[:], ACT.Sigmoid).then_inc(act_out, 1)
            else:
                act.wait_ge(act_in, 1)
                nc.scalar.activation(R.prob[:], R.left[:], ACT.Exp).then_inc(act_out, 1)

        @block.tensor
        def _(pe):
            if kind == "capacity":
                pe.wait_ge(rank_in, 1)
                nc.tensor.matmul(core.bankT[0][:, 0:N], core.upper[:], R.one[:], start=True, stop=True)
                nc.tensor.matmul(core.bankT[1][:, 0:N], core.ones[:], R.one[:], start=True, stop=True).then_inc(rank_ready, 1)


def feed_forward(nc, sem, core, w):
    hidden, hidden_out, y_ready, y_read, added, stats_new = (
        sem("hidden"), sem("hidden_out"), sem("y_ready"), sem("y_read"), sem("added"), sem("stats_new"))
    C, X = w.chunks, w.experts
    H = core.bankS
    Y = core.bankT
    W = BLOCK * P
    tiles_at = BLOCK // C if C < BLOCK else 1

    def steps():
        return range(2 * X)

    with nc.Block() as block:
        @block.tensor
        def _(pe):
            with pe.Fori(0, NBLK // 2) as i:
                for j in range(2 * X + 1):
                    e, half = j % X, j // X
                    for c in range(C):
                        if j < 2 * X:
                            k = j * C + c
                            if k >= 2:
                                pe.wait_ge(hidden_out, i * (2 * X * C) + k - 1)
                            else:
                                pe.wait_ge(hidden_out, i * (2 * X * C))
                            nc.tensor.matmul(H[k % 2][:, 0:W], w.w1[:, (e * C + c) * P:(e * C + c + 1) * P],
                                             core.xnT[:, bass.ds(i * (2 * W) + half * W, W)], start=True, stop=True).then_inc(hidden, 1)
                        if j >= 1:
                            t = j - 1
                            f = t % X
                            if c == 0:
                                pe.wait_ge(hidden_out, i * (2 * X * C) + (t + 1) * C)
                                if t >= 2:
                                    pe.wait_ge(y_read, i * (2 * X) + t - 1)
                                else:
                                    pe.wait_ge(y_read, i * (2 * X))
                            for q in range(c * tiles_at, (c + 1) * tiles_at):
                                for cc in range(C):
                                    last = nc.tensor.matmul(Y[t % 2][:, q * D:(q + 1) * D], core.hidden[t % 2][:, cc * W + q * P:cc * W + (q + 1) * P],
                                                            w.w2[:, (f * C + cc) * D:(f * C + cc + 1) * D], start=(cc == 0), stop=(cc == C - 1))
                            if c == C - 1:
                                last.then_inc(y_ready, 1)

        @block.scalar
        def _(act):
            with act.Fori(0, NBLK // 2) as i:
                for j in steps():
                    e = j % X
                    if j >= 2:
                        act.wait_ge(y_ready, i * (2 * X) + j - 1)
                    else:
                        act.wait_ge(y_ready, i * (2 * X))
                    for c in range(C):
                        k = j * C + c
                        act.wait_ge(hidden, i * (2 * X * C) + k + 1)
                        nc.scalar.activation(core.hidden[j % 2][:, c * W:(c + 1) * W], H[k % 2][:, 0:W], w.act,
                                             bias=w.b1[:, e * C + c:e * C + c + 1]).then_inc(hidden_out, 1)

        @block.vector
        def _(dve):
            with dve.Fori(0, NBLK // 2) as i:
                for j in steps():
                    e, half = j % X, j // X
                    dve.wait_ge(y_ready, i * (2 * X) + j + 1)
                    tiles = [i * (2 * BLOCK) + half * BLOCK + q for q in range(BLOCK)]

                    def weight(q):
                        if e >= w.routed:
                            return core.gate[:, w.gate:w.gate + 1]
                        return core.weight[:, bass.ds(tiles[q] * E + e, 1)]
                    if j:
                        dve.wait_ge(added, i * (2 * X) + j)
                    for q in range(BLOCK):
                        xt = tile_of(core.x, tiles[q])
                        last = nc.vector.scalar_tensor_tensor(out=xt, in0=Y[j % 2][:, q * D:(q + 1) * D], scalar=weight(q), in1=xt,
                                                              op0=ALU.mult, op1=ALU.add)
                    last.then_inc(y_read, 1)
                    dve.wait_ge(y_read, i * (2 * X) + j + 1)
                    for q in range(BLOCK):
                        xt = tile_of(core.x, tiles[q])
                        last = nc.vector.scalar_tensor_tensor(out=xt, in0=w.b2[:, e * D:(e + 1) * D], scalar=weight(q), in1=xt,
                                                              op0=ALU.mult, op1=ALU.add)
                    last.then_inc(added, 1)
                    if e == X - 1:
                        dve.wait_ge(added, i * (2 * X) + j + 1)
                        nc.vector.memset(core.pause[:], 0.0)
                        for q in range(BLOCK):
                            last = nc.vector.bn_stats(tile_of(core.stats, tiles[q], 6), tile_of(core.x, tiles[q]))
                        last.then_inc(stats_new, 1)
            dve.wait_ge(stats_new, NBLK)


class Named:
    pass


def program(nc, a, out):
    ctx = ExitStack()
    with ctx:
        phase = [""]

        def sb(name, cols, dt=F32):
            return ctx.enter_context(nc.sbuf_tensor(name, [P, cols], dt))

        taken = []

        def sem(name):
            taken.append(nc.alloc_semaphore(name=f"{phase[0]}_{name}"))
            return taken[-1]

        def give_back():
            with nc.Block() as block:
                @block.sync
                def _(sp):
                    for s in taken:
                        sp.sem_clear(s)
            for s in taken:
                nc.release_semaphore(s)
            taken.clear()

        core = Named()
        core.ctxT_dram = a["ctxT"]
        core.bankA = ctx.enter_context(nc.psum_tensor("bankA", [P, 512], F32))
        core.bankS = [ctx.enter_context(nc.psum_tensor(f"bankS{h}", [P, 1024], F32)) for h in range(2)]
        core.bankT = [ctx.enter_context(nc.psum_tensor(f"bankT{h}", [P, 512], F32)) for h in range(2)]
        core.bankO = ctx.enter_context(nc.psum_tensor("bankO", [P, 512], F32))
        core.x = sb("x", NB * D)
        core.xnT = sb("xnT", NB * P)
        core.key_on = sb("key_on", NB * P)
        core.key_neg = sb("key_neg", NB * P)
        core.stats, core.rstd, core.root = sb("stats", NB * 6), sb("rstd", NB), sb("root", NB)
        core.mean, core.var, core.half_sum, core.half_gap, core.pause = sb("mean", NB), sb("var", NB), sb("half_sum", NB), sb("half_gap", NB), sb("pause", 1)
        core.gate = sb("gate", 8)
        core.ident, core.ones, core.upper = sb("ident", P), sb("ones", P), sb("upper", P)
        core.head_of4, core.own_block, core.own_head = sb("head_of4", PER * P), sb("own_block", D), sb("own_head", HEADS)
        core.perm, core.even16 = sb("perm", P), sb("even16", 2)
        core.countdown = sb("countdown", NB * E)
        core.ctxT = [sb(f"ctxT{s}", P) for s in range(2)]
        core.xn = [sb(f"xn{s}", D) for s in range(2)]
        core.bias, core.top, core.recip = sb("bias", P), sb("top", HEADS), sb("recip", HEADS)
        core.xnTs = [sb(f"xnTs{s}", P) for s in range(2)]
        core.k = sb("k", P)
        core.v_early = sb("v_early", D)
        core.kz, core.qz = [sb(f"kz{s}", PER * P) for s in range(2)], [sb(f"qz{s}", GROUPS * P) for s in range(2)]
        core.v = [sb(f"v{s}", HEADS * VW + VW) for s in range(2)]
        core.o, core.oT, core.y = sb("o", D), sb("oT", P), sb("y", D)
        big = sb("big", 2 * HEADS * P + 2 * PER * P)
        core.probs = [big[:, s * HEADS * P:(s + 1) * HEADS * P] for s in range(2)]
        core.probsT = [big[:, 2 * HEADS * P + s * PER * P:2 * HEADS * P + (s + 1) * PER * P] for s in range(2)]
        core.hidden = core.probs
        L = core.lin = Named()
        L.xn, L.xnT, L.qkv, L.vx, L.kvm, L.qT = cut(big, (512, 512, 1536, 4 * 129, 4 * 144, 512))
        lin = sb("lin", 3 * 512 + 72 + 36 + 12 + 12 + 12 + 64 + 64)
        L.ctxT, L.attT, L.y, L.stat6, L.mean, L.total, L.gap, L.var, L.root, L.rs, L.z, L.zr = cut(
            lin, (512, 512, 512, 72, 12, 12, 12, 12, 12, 12, 64, 64))
        L.twice, L.turned, L.part, L.att = core.key_on[:, 0:1024], core.key_on[:, 1024:2048], core.key_on[:, 2048:2560], core.key_on[:, 2560:3072]
        core.logits, core.weight = sb("logits", NB * E), sb("weight", NB * E)
        R = core.route = Named()
        R.prob, R.one, R.two, R.mark, R.left = (sb("route_" + name, NB * E) for name in ("prob", "one", "two", "mark", "left"))
        R.top, R.best = sb("route_top", NB), sb("route_best", NB)
        w1_big = sb("w1_big", 9 * 4 * P)
        w2_big = sb("w2_big", 9 * 4 * D)
        b2_big = sb("b2_big", 9 * D)

        phase[0] = "setup"
        loaded, const0, const1, const2, gate_done = sem("loaded"), sem("const0"), sem("const1"), sem("const2"), sem("gate_done")
        first, chain, zeroed = sem("first"), sem("chain"), sem("zeroed")
        W = {}
        loads = []

        def weight_tile(name, cols, src):
            t = sb(name, cols)
            loads.append((t[:], src))
            return t

        for l in (0, 2, 3):
            w = W[l] = Named()
            w.gate = l
            w.wq, w.wk, w.wv, w.wo = (weight_tile(f"w{k}{l}", D, a[f"w{k}{l}"]) for k in "qkvo")
            w.bq, w.bk = (weight_tile(f"b{k}{l}", 1, a[f"b{k}{l}"].rearrange("(p o) -> p o", o=1)) for k in "qk")
            w.bv, w.bo = (weight_tile(f"b{k}{l}", D, a[f"b{k}{l}"].partition_broadcast(P)) for k in "vo")
        w = W[1] = Named()
        w.gate = 1
        w.wq, w.wk, w.wv, w.wd = (weight_tile(f"w{k}1", D, a[f"w{k}1"]) for k in "qkvd")
        w.gamma, w.beta, w.bd = (weight_tile(n, D, a[n].partition_broadcast(P)) for n in ("gamma", "beta", "bd1"))
        w.em = weight_tile("em", NB, a["em"])
        src = weight_tile("src", P, a["src"])
        ffn = {}
        for l, X, C, router, act in ((0, 9, 4, "wr0", ACT.Gelu), (1, 8, 2, "wr1", ACT.Relu), (2, 8, 4, "wr2", ACT.Gelu), (3, 1, 4, None, ACT.Gelu)):
            f = ffn[l] = Named()
            f.experts, f.chunks, f.act, f.gate, f.routed = X, C, act, 4 + l, (0 if l == 3 else E)
            f.w1, f.w2, f.b2 = w1_big, w2_big, b2_big
            f.b1 = weight_tile(f"b1_{l}", X * C, a[f"b1_{l}"])
            f.router = weight_tile(router, E, a[router]) if router else None
            f.router_bias = sb(f"router_bias{l}", E)
        extra = sb("extra_bias", E)
        loads.append((ffn[0].router_bias[:], a["bg0"].partition_broadcast(P)))
        loads.append((extra[:], a["bias0"].partition_broadcast(P)))
        loads.append((ffn[1].router_bias[:], a["br1"].partition_broadcast(P)))
        loads.append((core.gate[:, 0:4], a["g_xattn"].partition_broadcast(P)))
        loads.append((core.gate[:, 4:8], a["g_ffn"].partition_broadcast(P)))
        loads.append((core.x[:].rearrange("p (n d) -> p n d", d=D), a["x"].rearrange("n p d -> p n d")))

        with nc.Block() as block:
            @block.sync
            def _(sp):
                for dst, s in loads:
                    sp.dma_start(dst, s).then_inc(loaded, 16)
                sp.wait_ge(loaded, 16 * len(loads))

            @block.gpsimd
            def _(pool):
                pool.memset(core.ones[:], 1.0)
                pool.memset(core.ident[:], 0.0)
                pool.memset(core.qz[0][:], 0.0)
                pool.memset(core.qz[1][:], 0.0)
                pool.memset(core.perm[:], 0.0)
                pool.memset(core.v[0][:], 0.0)
                pool.memset(core.v[1][:], 0.0).then_inc(zeroed, 1)
                pool.wait_ge(zeroed, 1)
                pool.memset(own_strips(core.v[0])[:, :, HD:HD + 1], 1.0)
                pool.memset(own_strips(core.v[1])[:, :, HD:HD + 1], 1.0)
                pool.memset(core.head_of4[:], 1.0)
                pool.memset(core.own_block[:], 1.0)
                pool.memset(core.own_head[:], 1.0)
                pool.iota(core.countdown[:], pattern=[[0, NB], [-1, E]], base=E, channel_multiplier=0,
                          allow_small_or_imprecise_dtypes=True).then_inc(const0, 1)
                pool.wait_ge(const0, 1)
                pool.affine_select(out=core.ident[:], in_=core.ident[:], compare_op=ALU.not_equal, fill=1.0, base=0,
                                   pattern=[[-1, P]], channel_multiplier=1).then_inc(const1, 1)
                pv = core.perm[:].rearrange("p (h a) -> p h a", h=HEADS)
                pool.affine_select(out=pv, in_=pv, compare_op=ALU.not_equal, fill=1.0, base=0,
                                   pattern=[[-1, HEADS], [-HEADS, P // HEADS]], channel_multiplier=1).then_inc(const1, 1)
                pool.affine_select(out=core.upper[:], in_=core.ones[:], compare_op=ALU.is_ge, fill=0.0, base=0,
                                   pattern=[[1, P]], channel_multiplier=-1).then_inc(const1, 1)
                for t, pat in ((core.own_head[:], [[-HD, HEADS]]), (core.own_block[:].rearrange("p (h c) -> p h c", c=HD), [[-HD, HEADS], [0, HD]])):
                    pool.affine_select(out=t, in_=t, compare_op=ALU.is_ge, fill=0.0, base=0, pattern=pat,
                                       channel_multiplier=1).then_inc(const1, 1)
                pool.wait_ge(const1, 5)
                for t, pat in ((core.own_head[:], [[HD, HEADS]]), (core.own_block[:].rearrange("p (h c) -> p h c", c=HD), [[HD, HEADS], [0, HD]])):
                    pool.affine_select(out=t, in_=t, compare_op=ALU.is_ge, fill=0.0, base=HD - 1, pattern=pat,
                                       channel_multiplier=-1).then_inc(const2, 1)

            @block.vector
            def _(dve):
                dve.wait_ge(const2, 2)
                hs = core.own_head[:].rearrange("p (g s) -> p s g", s=PER)
                nc.vector.tensor_reduce(out=core.top[:, 0:PER], in_=hs, op=ALU.max, axis=AX).then_inc(chain, 1)
                nc.vector.tensor_reduce(out=core.even16[:], in_=core.own_head[:].rearrange("p (q r s) -> p r q s", r=2, s=2), op=ALU.max,
                                        axis=mybir.AxisListType.XY).then_inc(chain, 1)
                dve.wait_ge(chain, 1)
                nc.vector.tensor_tensor(core.head_of4[:].rearrange("p (s k) -> p s k", k=P), core.head_of4[:].rearrange("p (s k) -> p s k", k=P),
                                        core.top[:, 0:PER].rearrange("p (s o) -> p s o", o=1).to_broadcast([P, PER, P]), ALU.mult).then_inc(chain, 1)
                dve.wait_ge(loaded, 16 * len(loads))
                nc.vector.tensor_tensor(ffn[0].router_bias[:], ffn[0].router_bias[:], extra[:], ALU.add).then_inc(chain, 1)
                nc.vector.memset(ffn[2].router_bias[:], 0.0).then_inc(chain, 1)
                for l in (0, 2, 3):
                    nc.vector.tensor_scalar(W[l].bq[:], W[l].bq[:], float(HD) ** -0.5, None, ALU.mult).then_inc(chain, 1)
                with dve.Fori(0, NB) as n:
                    nc.vector.bn_stats(tile_of(core.stats, n, 6), tile_of(core.x, n)).then_inc(first, 1)
                dve.wait_ge(first, NB)
                dve.wait_ge(chain, 8)

            @block.scalar
            def _(act):
                act.wait_ge(loaded, 16 * len(loads))
                nc.scalar.activation(core.gate[:], core.gate[:], ACT.Tanh).then_inc(gate_done, 1)

        def load_weights(l):
            f = ffn[l]
            phase[0] = f"load{l}"
            landed = sem("landed")
            parts = [(w1_big[:, 0:f.experts * f.chunks * P], a[f"w1_{l}"]),
                     (w2_big[:, 0:f.experts * f.chunks * D], a[f"w2_{l}"]),
                     (b2_big[:, 0:f.experts * D], a[f"b2_{l}"].partition_broadcast(P))]
            with nc.Block() as block:
                @block.sync
                def _(sp):
                    for dst, s in parts:
                        sp.dma_start(dst, s).then_inc(landed, 16)
                    sp.wait_ge(landed, 16 * len(parts))

        def load_mask(l):
            phase[0] = f"mask{l}"
            landed, on, neg = sem("landed"), sem("on"), sem("neg")
            raw = core.xnT[:].bitcast(I32) if l == 3 else core.xnT[:, 0:NB * P // 4].bitcast(U8)
            with nc.Block() as block:
                @block.sync
                def _(sp):
                    sp.dma_start(raw, a[f"mask{l}"].partition_broadcast(P)).then_inc(landed, 16)

                @block.vector
                def _(dve):
                    dve.wait_ge(landed, 16)
                    nc.vector.tensor_scalar(core.key_on[:], raw, 0.0, None, ALU.not_equal).then_inc(on, 1)
                    dve.wait_ge(on, 1)
                    nc.vector.tensor_scalar(core.key_neg[:], core.key_on[:], -1.0, NEG, ALU.add, ALU.mult).then_inc(neg, 1)
                    dve.wait_ge(neg, 1)

        for l in range(4):
            load_weights(l)
            phase[0] = f"norm{l}a"
            rebuild_norm_scale(nc, sem, core, EPS)
            if l == 1:
                phase[0] = "lin1"
                linear_attention_setup(nc, sem, core)
                linear_attention(nc, sem, core, W[1])
                phase[0] = "v1"
            else:
                if l >= 2:
                    load_mask(l)
                phase[0] = f"att{l}"
                softmax_attention(nc, sem, core, W[l], l >= 2, src if l == 3 else None)
            phase[0] = f"norm{l}f"
            rebuild_norm_scale(nc, sem, core, EPS)
            phase[0] = f"xnT{l}"
            norm_and_route(nc, sem, core, ffn[l])
            if l < 3:
                phase[0] = f"route{l}"
                route(nc, sem, core, ("top2", "top1", "capacity")[l], 4 + l)
            phase[0] = f"ffn{l}"
            feed_forward(nc, sem, core, ffn[l])
            give_back()
        phase[0] = "store"
        stored = sem("stored")
        with nc.Block() as block:
            @block.sync
            def _(sp):
                sp.dma_start(out.rearrange("n p d -> p n d"), core.x[:].rearrange("p (n d) -> p n d", d=D)).then_inc(stored, 16)
                sp.wait_ge(stored, 16)


def cut(buffer, widths):
    ends = [sum(widths[:k + 1]) for k in range(len(widths))]
    return [buffer[:, end - width:end] for end, width in zip(ends, widths)]


def linear_attention_setup(nc, sem, core):
    done = sem("ones_column")
    with nc.Block() as block:
        @block.vector
        def _(dve):
            nc.vector.memset(core.lin.vx[:], 1.0).then_inc(done, 1)
            dve.wait_ge(done, 1)


def laid_out(inputs):
    v = {k: np.asarray(x) for k, x in inputs.items()}
    g = {}
    g["x"] = v["x"]
    g["ctxT"] = v["ctx_1024"].transpose(0, 2, 1)
    for l in (0, 2, 3):
        for k in "qkvo":
            m = v[f"L{l}_xattn_W{k}"]
            g[f"w{k}{l}"] = m if l == 2 else m.T
            g[f"b{k}{l}"] = v[f"L{l}_xattn_b{k}"]
    g["wq1"], g["wk1"], g["wv1"], g["wd1"] = v["L1_xattn_wq"], v["L1_xattn_wk"], v["L1_xattn_wv"], v["L1_xattn_dense_w"]
    g["gamma"], g["beta"], g["bd1"] = v["L1_xattn_ln_gamma"], v["L1_xattn_ln_beta"], v["L1_xattn_dense_b"]
    g["em"] = v["mask_BxS2_ff1"].T
    g["src"] = v["mask_1x1xSxS2_ff0"].reshape(P, P)
    g["mask2"] = v["mask_Bx1xS2_bf1"].view(np.uint8).reshape(-1)
    g["mask3"] = v["mask_BxS2_ik0"].reshape(-1)
    g["g_xattn"], g["g_ffn"] = v["g_xattn"], v["g_ffn"]

    def first(m):
        return m.transpose(1, 0, 2).reshape(D, -1)

    def second(m):
        e, h, d = m.shape
        return m.reshape(e, h // P, P, d).transpose(2, 0, 1, 3).reshape(P, -1)

    def bias(m):
        e, h = m.shape
        return m.reshape(e, h // P, P).transpose(2, 0, 1).reshape(P, -1)

    g["w1_0"] = first(np.concatenate([v["L0_ffn_W1"], v["L0_ffn_Ws1"][None]]).transpose(0, 2, 1))
    g["w2_0"] = second(np.concatenate([v["L0_ffn_W2"], v["L0_ffn_Ws2"][None]]).transpose(0, 2, 1))
    g["b1_0"] = bias(np.concatenate([v["L0_ffn_b1"], v["L0_ffn_bs1"][None]]))
    g["b2_0"] = np.concatenate([v["L0_ffn_b2"], v["L0_ffn_bs2"][None]]).reshape(-1)
    g["wr0"], g["bg0"], g["bias0"] = v["L0_ffn_Wg"].T, v["L0_ffn_bg"], v["L0_ffn_bias"]
    g["w1_1"], g["w2_1"], g["b1_1"], g["b2_1"] = first(v["L1_ffn_W1"]), second(v["L1_ffn_W2"]), bias(v["L1_ffn_b1"]), v["L1_ffn_b2"].reshape(-1)
    g["wr1"], g["br1"] = v["L1_ffn_Wr"], v["L1_ffn_br"]
    g["w1_2"], g["w2_2"], g["b1_2"], g["b2_2"] = first(v["L2_ffn_w1"]), second(v["L2_ffn_w2"]), bias(v["L2_ffn_b1"]), v["L2_ffn_b2"].reshape(-1)
    g["wr2"] = v["L2_ffn_router_w"].T
    g["w1_3"], g["w2_3"] = v["L3_ffn_w1"], second(v["L3_ffn_w2"][None])
    g["b1_3"], g["b2_3"] = bias(v["L3_ffn_b1"][None]), v["L3_ffn_b2"]

    return g


def kernel(**inputs):
    import concourse.bacc as _bacc
    from concourse.bass_utils import run_bass_kernel_spmd as _run

    g = laid_out(inputs)
    nc = _bacc.Bacc("TRN2", target_bir_lowering=False, num_devices=1)
    arrays, args = {}, {}
    for name, m in g.items():
        m = np.ascontiguousarray(m)
        arrays[f"in_{name}"] = m
        args[name] = nc.dram_tensor(f"in_{name}", m.shape, mybir.dt.from_np(m.dtype), kind="ExternalInput").ap()
    out = nc.dram_tensor("out_x", (NB, P, D), F32, kind="ExternalOutput").ap()
    program(nc, args, out)
    r = _run(nc, [arrays], core_ids=[0])
    return r.results[0]["out_x"]
```

```python
import numpy as np
import concourse.bass as bass
from concourse import mybir
from contextlib import ExitStack

F32 = mybir.dt.float32
I32 = mybir.dt.int32
U8 = mybir.dt.uint8
ALU = mybir.AluOpType
ACT = mybir.ActivationFunctionType
AX = mybir.AxisListType.X

P = 128
D = 128
NB = 32
HEADS = 16
HD = D // HEADS
GROUPS = 4
PER = HEADS // GROUPS
SIDE = HEADS // 2
VW = 96
E = 8
TILES1 = 40
TILES2 = 72
BLOCK = 4
NBLK = NB // BLOCK
CAPACITY = 768
CREDIT = 2
RW = D + 1
T_ALL = NB * P
EMPTY = 24
EPS = 1e-5
EPS_LN1 = 1e-6
EPS_K = 1e-6
NEG = 1e9


class Batch:

    def __init__(self, i, c):
        self.i, self.c = i, c
        self.n = i * 2 + c if not isinstance(i, int) else 2 * i + c
        self.slot = c % 2
        self.turn = i + c // 2

    def shift(self, k):
        return Batch(self.i, self.c + k)


class Tile:

    def __init__(self, i, c):
        self.i, self.c = i, c
        self.n, self.n_key = i * 8 + c, c
        self.slot, self.in8, self.four = c % 2, c % 8, c // 4 % 2
        self.turn = i + c // 8
        self.fours = i * 2 + c // 4

    def shift(self, k):
        return Tile(self.i, self.c + k)


def wait(eng, sem, value):
    if isinstance(value, int) and value <= 0:
        return
    eng.wait_ge(sem, value)


def pipelined(eng, step):
    for c in range(-2, 4):
        step(Batch(0, c))
    with eng.Fori(0, (NB - 8) // 2) as i:
        for u in (0, 1):
            step(Batch(i, 4 + u))
    for c in range(NB - 4, NB + 2):
        step(Batch(0, c))


def exists(b):
    return not isinstance(b.n, int) or 0 <= b.n < NB


def own_strips(v):
    return v[:].rearrange("p (a h c) -> p a h c", a=2, h=SIDE)[:, :, :, 0:HD + 1]


def strip(v, h):
    at = h // SIDE * SIDE * (VW + HD + 1) + h % SIDE * VW
    return v[:, at:at + VW]


def sides(a, c):
    return a[:].rearrange("p (a h c) -> p a h c", a=2, c=c)


def tile_of(t, n, w=D):
    if isinstance(n, int):
        return t[:, n * w:(n + 1) * w]
    return t[:, bass.ds(n * w, w)]


def moments(nc, dve, chain, base, stats, mean, var, total, gap):
    s = stats.rearrange("p (n c) -> p n c", c=6)
    nc.vector.tensor_tensor(mean, s[:, :, 1], s[:, :, 4], ALU.add)
    nc.vector.tensor_tensor(gap, s[:, :, 1], s[:, :, 4], ALU.subtract)
    nc.vector.tensor_tensor(total, s[:, :, 2], s[:, :, 5], ALU.add).then_inc(chain, 1)
    dve.wait_ge(chain, base + 1)
    nc.vector.tensor_scalar(mean, mean, 0.5, None, ALU.mult)
    nc.vector.scalar_tensor_tensor(out=gap, in0=gap, scalar=0.25, in1=gap, op0=ALU.mult, op1=ALU.mult).then_inc(chain, 1)
    dve.wait_ge(chain, base + 2)
    nc.vector.scalar_tensor_tensor(out=var, in0=total, scalar=1.0 / D, in1=gap, op0=ALU.mult, op1=ALU.add).then_inc(chain, 1)
    dve.wait_ge(chain, base + 3)


def rebuild_norm_scale(nc, sem, core, eps, ended):
    chain, ready, root, done = sem("chain"), sem("var_ready"), sem("root_ready"), sem("rstd_ready")
    with nc.Block() as block:
        @block.vector
        def _(dve):
            moments(nc, dve, chain, 0, core.stats[:], core.mean[:], core.var[:], core.half_sum[:], core.half_gap[:])
            nc.vector.tensor_scalar(core.rstd[:], core.var[:], eps, None, ALU.add).then_inc(ready, 1)
            dve.wait_ge(root, 1)
            nc.vector.reciprocal(core.rstd[:], core.root[:]).then_inc(done, 1)
            dve.wait_ge(done, 1)

        @block.scalar
        def _(act):
            act.wait_ge(ready, 1)
            nc.scalar.activation(core.root[:], core.rstd[:], ACT.Sqrt).then_inc(root, 1)

        @block.sync
        def _(sp):
            for s in ended:
                sp.sem_clear(s)


def softmax_attention(nc, sem, core, w, masked, src, later):
    ctx_in = [sem("ctx_in0"), sem("ctx_in1")]
    xn_ready = sem("xn_ready")
    xnT_ready, xnT_out = sem("xnT_ready"), sem("xnT_out")
    proj = sem("proj")
    q_out, k_out, v_out, v_placed = sem("q_out"), sem("k_out"), sem("v_out"), sem("v_placed")
    k_plain, bias_ready = sem("k_plain"), sem("bias_ready")
    scores, biased, top, shifted, expd = sem("scores"), sem("biased"), sem("top"), sem("shifted"), sem("expd")
    turned, probs_out, mixed = sem("turned"), sem("probs_out"), sem("mixed")
    recip, normed = sem("recip"), sem("normed")
    oT_ready, oT_out, y_ready = sem("oT_ready"), sem("oT_out"), sem("y_ready")
    y_read, x_new, stats_new = sem("y_read"), sem("x_new"), sem("stats_new")
    later_in = sem("later_in")
    A, S, T, O = core.bankA, core.bankS, core.bankT, core.bankO
    q_norm = float(HD) ** -0.5
    heads8 = lambda a: a.rearrange("p (h k) -> p h k", k=P)

    with nc.Block() as block:
        @block.sync
        def _(sp):
            def load(b):
                wait(sp, proj, b.n - 1)
                sp.dma_start(core.ctxT[b.slot][:], core.ctxT_dram[bass.ds(b.n, 1) if not isinstance(b.n, int) else slice(b.n, b.n + 1)]
                             .rearrange("o d t -> d (o t)")).then_inc(ctx_in[b.slot], 16)
            peeled = 2 + (len(later) + 3) // 4 * 2
            for c in range(peeled):
                load(Batch(0, c))
                for to, source in later[max(c - 2, 0) * 2:max(c - 1, 0) * 2]:
                    sp.dma_start(to, source).then_inc(later_in, 16)
            with sp.Fori(0, (NB - peeled) // 2) as i:
                for u in (0, 1):
                    load(Batch(i, peeled + u))
            sp.wait_ge(later_in, 16 * len(later))

        @block.vector
        def _(dve):
            def norm_x(n):
                wait(dve, xnT_ready, n.n - 1)
                nc.vector.tensor_scalar(core.xn[n.slot][:], tile_of(core.x, n.n), tile_of(core.mean, n.n, 1),
                                        tile_of(core.rstd, n.n, 1), ALU.subtract, ALU.mult).then_inc(xn_ready, 1)

            def norm_o(n):
                o = O[:, 0:2 * VW].rearrange("p (a w) -> p a w", a=2)[:, :, 0:SIDE * (HD + 1)].rearrange("p a (h c) -> p a h c", c=HD + 1)
                wait(dve, mixed, n.n * 4 + 4)
                nc.vector.reciprocal(core.recip[:].rearrange("p (a h) -> p a h", a=2), o[:, :, :, HD]).then_inc(recip, 1)
                wait(dve, recip, n.n + 1)
                wait(dve, oT_ready, n.n)
                nc.vector.tensor_tensor(sides(core.o, HD), o[:, :, :, 0:HD], sides(core.recip, 1).to_broadcast([P, 2, SIDE, HD]), ALU.mult).then_inc(normed, 1)

            def keys_values(n):
                wait(dve, proj, n.n + 1)
                kz = core.kz[n.slot][:].rearrange("p (s k) -> p s k", k=P)
                ms = core.head_of4[:].rearrange("p (s k) -> p s k", k=P)
                if masked:
                    wait(dve, k_out, n.n)
                    nc.vector.scalar_tensor_tensor(out=core.k[:], in0=T[0][:, 0:P], scalar=w.bk[:, 0:1],
                                                   in1=tile_of(core.key_on, n.n), op0=ALU.add, op1=ALU.mult).then_inc(k_plain, 1)
                else:
                    wait(dve, scores, n.n * 2 - 2)
                    nc.vector.scalar_tensor_tensor(out=kz, in0=T[0][:, 0:P].rearrange("p (o k) -> p o k", o=1).to_broadcast([P, PER, P]),
                                                   scalar=w.bk[:, 0:1], in1=ms, op0=ALU.add, op1=ALU.mult).then_inc(k_out, 1)
                wait(dve, v_placed, n.n)
                nc.vector.tensor_copy(core.v_early[:], T[0][:, P:2 * P]).then_inc(v_out, 1)

            def softmax(n, hf, between):
                if hf == 0 and masked:
                    if src is not None:
                        nc.vector.tensor_tensor(core.bias[:], tile_of(core.key_neg, n.n), src[:], ALU.add).then_inc(bias_ready, 1)
                        wait(dve, bias_ready, n.n + 1)
                wait(dve, scores, n.n * 2 + hf + 1)
                wait(dve, turned, n.n * 4 - 4)
                half = core.probs[n.slot][:, hf * 1024:(hf + 1) * 1024]
                source = S[hf][:]
                if masked:
                    bias = core.bias[:] if src is not None else tile_of(core.key_neg, n.n)
                    nc.vector.tensor_tensor(heads8(half), heads8(source), bias.rearrange("p (o k) -> p o k", o=1).to_broadcast([P, 8, P]),
                                            ALU.add).then_inc(biased, 1)
                    wait(dve, biased, n.n * 2 + hf + 1)
                    source = half
                m = core.top[:, hf * 8:hf * 8 + 8]
                if masked:
                    between()
                nc.vector.tensor_reduce(out=m, in_=heads8(source), op=ALU.max, axis=AX).then_inc(top, 1)
                if not masked:
                    between()
                if hf == 1 and exists(n.shift(-1)):
                    norm_o(n.shift(-1))
                wait(dve, top, n.n * 2 + hf + 1)
                nc.vector.tensor_tensor(heads8(half), heads8(source), m.rearrange("p (h o) -> p h o", o=1).to_broadcast([P, 8, P]),
                                        ALU.subtract).then_inc(shifted, 1)

            def read_y(n):
                wait(dve, x_new, n.n)
                wait(dve, y_ready, n.n + 1)
                nc.vector.tensor_tensor(core.y[:], O[:, 384:512], w.bo[:], ALU.add).then_inc(y_read, 1)

            def add_to_x(n):
                xt = tile_of(core.x, n.n)
                wait(dve, y_read, n.n + 1)
                nc.vector.scalar_tensor_tensor(out=xt, in0=core.y[:], scalar=core.gate[:, w.gate:w.gate + 1], in1=xt,
                                               op0=ALU.mult, op1=ALU.add).then_inc(x_new, 1)
                if not (isinstance(n.n, int) and n.n == 0):
                    nc.vector.bn_stats(tile_of(core.stats, n.n - 1, 6), tile_of(core.x, n.n - 1)).then_inc(stats_new, 1)

            def step(b):
                if not exists(b) and exists(b.shift(3)):
                    norm_x(b.shift(3))
                if exists(b.shift(1)):
                    keys_values(b.shift(1))
                if exists(b):
                    softmax(b, 0, lambda: read_y(b.shift(-2)) if exists(b.shift(-2)) else None)
                elif exists(b.shift(-2)):
                    read_y(b.shift(-2))
                if exists(b.shift(-2)):
                    add_to_x(b.shift(-2))
                if not exists(b) and exists(b.shift(-1)):
                    norm_o(b.shift(-1))
                if exists(b):
                    softmax(b, 1, lambda: norm_x(b.shift(3)) if exists(b.shift(3)) else None)
            norm_x(Batch(0, 0))
            pipelined(dve, step)
            dve.wait_ge(x_new, NB)
            nc.vector.bn_stats(tile_of(core.stats, NB - 1, 6), tile_of(core.x, NB - 1)).then_inc(stats_new, 1)
            dve.wait_ge(stats_new, NB)

        @block.gpsimd
        def _(pool):
            def spread(b):
                wait(pool, k_plain, b.n + 1)
                wait(pool, scores, b.n * 2 - 2)
                nc.gpsimd.tensor_tensor(core.kz[b.slot][:].rearrange("p (s k) -> p s k", k=P),
                                        core.k[:].rearrange("p (o k) -> p o k", o=1).to_broadcast([P, PER, P]),
                                        core.head_of4[:].rearrange("p (s k) -> p s k", k=P), ALU.mult).then_inc(k_out, 1)

            def place(b):
                wait(pool, v_out, b.n + 1)
                wait(pool, mixed, b.n * 4 - 4)
                nc.gpsimd.tensor_tensor(own_strips(core.v[b.slot])[:, :, :, 0:HD], sides(core.v_early, HD), sides(w.bv, HD), ALU.add).then_inc(v_placed, 1)
            def both(b):
                if masked:
                    spread(b)
                place(b)
            both(Batch(0, 0))
            both(Batch(0, 1))
            with pool.Fori(0, (NB - 2) // 2) as i:
                for u in (0, 1):
                    both(Batch(i, 2 + u))

        @block.scalar
        def _(act):
            def exponentials(n, hf):
                wait(act, shifted, n.n * 2 + hf + 1)
                half = core.probs[n.slot][:, hf * 1024:(hf + 1) * 1024]
                nc.scalar.activation(half, half, ACT.Exp).then_inc(expd, 1)

            def step(b):
                first, n, c, o = b.shift(2), b.shift(1), b.shift(-1), b.shift(-2)
                if exists(n):
                    wait(act, proj, n.n + 1)
                    wait(act, scores, n.n * 2 - 2)
                    if exists(first):
                        wait(act, xnT_ready, first.n + 1)
                    for g in range(GROUPS):
                        r = slice(32 * g, 32 * g + 32)
                        nc.scalar.activation(core.qz[n.slot][r, g * P:(g + 1) * P], A[r, 128:256], ACT.Identity,
                                             bias=w.bq[r, 0:1], scale=q_norm).then_inc(q_out, 1)
                if exists(first):
                    wait(act, xnT_ready, first.n + 1)
                    wait(act, proj, first.n - 1)
                    nc.scalar.activation(core.xnTs[first.slot][:], A[:, 0:128], ACT.Copy).then_inc(xnT_out, 1)
                if exists(o):
                    wait(act, oT_ready, o.n + 1)
                    wait(act, y_ready, o.n)
                    nc.scalar.activation(core.oT[:], A[:, 256:384], ACT.Copy).then_inc(oT_out, 1)
                if exists(c):
                    exponentials(c, 1)
                if exists(c):
                    for g in range(GROUPS):
                        wait(act, turned, c.n * 4 + g + 1)
                        wait(act, mixed, c.n * 4 + g - 1)
                        nc.scalar.activation(core.probsT[g % 2][:], T[g % 2][:], ACT.Copy).then_inc(probs_out, 1)
                if exists(b):
                    exponentials(b, 0)
            pipelined(act, step)

        @block.tensor
        def _(pe):
            def project(n):
                wait(pe, ctx_in[n.slot], (n.turn + 1) * 16)
                wait(pe, xnT_out, n.n + 1)
                wait(pe, oT_out, n.n - 3)
                wait(pe, probs_out, n.n * 4 - 8)
                wait(pe, v_out, n.n)
                nc.tensor.matmul(A[:, 128:256], w.wq[:], core.xnTs[n.slot][:], start=True, stop=True)
                nc.tensor.matmul(T[0][:, 0:P], w.wk[:], core.ctxT[n.slot][:], start=True, stop=True)
                nc.tensor.matmul(T[0][:, P:2 * P], core.ctxT[n.slot][:], w.wv[:], start=True, stop=True).then_inc(proj, 1)

            def turn_x(n):
                wait(pe, xn_ready, n.n + 1)
                wait(pe, oT_out, n.n - 4)
                wait(pe, q_out, n.n * 4 - 4)
                nc.tensor.transpose(A[:, 0:128], core.xn[n.slot][:], core.ident[:]).then_inc(xnT_ready, 1)

            def score(n, g):
                if g == 0:
                    wait(pe, q_out, n.n * 4 + 4)
                    wait(pe, k_out, n.n + 1)
                if g % 2 == 0:
                    wait(pe, shifted, n.n * 2 + g // 2 - 1)
                last = nc.tensor.matmul(S[g // 2][:, (g % 2) * 512:(g % 2) * 512 + 512], core.qz[n.slot][:, g * P:(g + 1) * P],
                                        core.kz[n.slot][:], start=True, stop=True)
                if g % 2:
                    last.then_inc(scores, 1)

            def turn(n, g):
                if g == 0:
                    wait(pe, v_out, n.n + 3 if exists(n.shift(2)) else NB)
                wait(pe, expd, n.n * 2 + g // 2 + 1)
                wait(pe, probs_out, n.n * 4 + g - 1)
                for s in range(PER):
                    h = g * PER + s
                    last = nc.tensor.transpose(T[g % 2][:, s * P:(s + 1) * P], core.probs[n.slot][:, h * P:(h + 1) * P], core.ident[:])
                last.then_inc(turned, 1)

            def mix(n, g):
                wait(pe, probs_out, n.n * 4 + g + 1)
                if g == 0:
                    wait(pe, y_read, n.n)
                    wait(pe, v_placed, n.n + 1)
                for s in range(PER):
                    h = g * PER + s
                    last = nc.tensor.matmul(O[:, h // SIDE * VW:(h // SIDE + 1) * VW], core.probsT[g % 2][:, s * P:(s + 1) * P],
                                            strip(core.v[n.slot], h), start=(h % SIDE == 0), stop=(h % SIDE == SIDE - 1))
                last.then_inc(mixed, 1)

            def step(b):
                first, n, c, o = b.shift(2), b.shift(1), b.shift(-1), b.shift(-2)
                if exists(n):
                    project(n)
                if exists(first):
                    turn_x(first)
                if exists(b):
                    score(b, 0)
                    score(b, 1)
                if exists(o):
                    wait(pe, normed, o.n + 1)
                    if exists(n):
                        wait(pe, q_out, n.n * 4 + 4)
                    if exists(first):
                        wait(pe, xnT_out, first.n + 1)
                    nc.tensor.transpose(A[:, 256:384], core.o[:], core.ident[:]).then_inc(oT_ready, 1)
                if exists(b):
                    score(b, 2)
                if exists(o):
                    wait(pe, oT_out, o.n + 1)
                    nc.tensor.matmul(O[:, 384:512], core.oT[:], w.wo[:], start=True, stop=True).then_inc(y_ready, 1)
                if exists(c):
                    turn(c, 0)
                if exists(b):
                    score(b, 3)
                if exists(c):
                    turn(c, 1), mix(c, 0), turn(c, 2), mix(c, 1), turn(c, 3), mix(c, 2), mix(c, 3)
            pipelined(pe, step)


def linear_attention(nc, sem, core, w, later):
    end_chain, end_var, end_root = sem("end_chain"), sem("end_var"), sem("end_root")
    proj_read, norm_in, norm_out = sem("proj_read"), sem("norm_in"), sem("norm_out")
    v_scaled, v_ready, ones_column = sem("v_scaled"), sem("v_ready"), sem("ones_column")
    later_in = sem("later_in")
    ctx_in, xn_ready, xnT_ready, xnT_out = sem("ctx_in"), sem("xn_ready"), sem("xnT_ready"), sem("xnT_out")
    proj, chain, var_ready, root_ready = sem("proj"), sem("chain"), sem("var_ready"), sem("root_ready")
    kv_in, kv_ready, qT_ready, qT_out, kv_out = sem("kv_in"), sem("kv_ready"), sem("qT_ready"), sem("qT_out"), sem("kv_out")
    att_ready, att_out, attT_ready, attT_out, y_ready = sem("att_ready"), sem("att_out"), sem("attT_ready"), sem("attT_out"), sem("y_ready")
    y_out = sem("y_out")
    S, T, A, O = core.bankS, core.bankT, core.bankA, core.bankO
    B4 = BLOCK
    where = [S[0][:, 0:512], S[0][:, 512:1024], S[1][:, 0:512]]
    L = core.lin
    STEPS, END_STEPS = 13, 10
    ROUNDS = NB // B4

    def rounds(eng, front, back, end):
        front(0)
        back(0, lambda: front(1), lambda: None)
        with eng.Fori(1, ROUNDS - 1) as r:
            back(r, lambda: front(r + 1), lambda: end(r - 1))
        back(ROUNDS - 1, lambda: None, lambda: end(ROUNDS - 2))
        end(ROUNDS - 1)

    with nc.Block() as block:
        @block.sync
        def _(sp):
            def load(r):
                sp.dma_start(L.ctxT[:].rearrange("d (b t) -> d b t", b=B4),
                             core.ctxT_dram[bass.ds(r * B4, B4) if not isinstance(r, int) else slice(r * B4, (r + 1) * B4)]
                             .rearrange("b d t -> d b t")).then_inc(ctx_in, 16)
            load(0)
            for to, source in later:
                sp.dma_start(to, source).then_inc(later_in, 16)
            with sp.Fori(1, NB // B4) as r:
                sp.wait_ge(proj, r)
                load(r)
            sp.wait_ge(later_in, 16 * len(later))

        @block.vector
        def _(dve):
            bc = lambda a, k: a[:].rearrange("p (o d) -> p o d", o=1).to_broadcast([P, k, D])

            def front(r):
                for j in range(B4):
                    n = r * B4 + j
                    ins = nc.vector.tensor_scalar(L.xn[:, j * D:(j + 1) * D], tile_of(core.x, n), tile_of(core.mean, n, 1),
                                                  tile_of(core.rstd, n, 1), ALU.subtract, ALU.mult)
                ins.then_inc(xn_ready, 1)

            def back(r, next_front, last_end):
                done = [0]

                def link(ins):
                    done[0] += 1
                    ins.then_inc(chain, 1)
                    dve.wait_ge(chain, r * STEPS + done[0])

                dve.wait_ge(proj, r + 1)
                for t in range(3):
                    for j in range(B4):
                        i = t * B4 + j
                        last = nc.vector.bn_stats(L.stat6[:, i * 6:i * 6 + 6], where[t][:, j * D:(j + 1) * D])
                link(last)
                moments(nc, dve, chain, r * STEPS + done[0], L.stat6[:, 0:72], L.mean[:, 0:12], L.var[:, 0:12], L.total[:, 0:12], L.gap[:, 0:12])
                done[0] += 3
                nc.vector.tensor_scalar(L.var[:, 0:12], L.var[:, 0:12], EPS_LN1, None, ALU.add).then_inc(var_ready, 1)
                dve.wait_ge(root_ready, r + 1)
                link(nc.vector.reciprocal(L.rs[:, 0:12], L.root[:, 0:12]))
                nc.vector.scalar_tensor_tensor(out=L.total[:, 0:12], in0=L.mean[:, 0:12], scalar=-1.0, in1=L.rs[:, 0:12],
                                               op0=ALU.mult, op1=ALU.mult).then_inc(norm_in, 1)
                for j in range(B4):
                    i = B4 + j
                    last = nc.vector.tensor_scalar(L.qkv[:, i * D:(i + 1) * D], where[1][:, j * D:(j + 1) * D], L.mean[:, i:i + 1],
                                                   L.rs[:, i:i + 1], ALU.subtract, ALU.mult)
                last.then_inc(proj_read, 1)
                dve.wait_ge(proj_read, r + 1)
                dve.wait_ge(norm_out, r + 1)
                every = L.qkv[:].rearrange("p (i d) -> p i d", d=D)
                qk = every[:, 0:8]
                link(nc.vector.tensor_tensor(qk, qk, bc(w.gamma, 8), ALU.mult))
                link(nc.vector.tensor_tensor(qk, qk, bc(w.beta, 8), ALU.add))
                link(nc.vector.tensor_scalar(L.qkv[:, 0:8 * D], L.qkv[:, 0:8 * D], 0.0, EPS_K, ALU.max, ALU.add))
                for j in range(B4):
                    k = L.qkv[:, (4 + j) * D:(5 + j) * D]
                    nc.vector.tensor_scalar(k, k, tile_of(w.em, r * B4 + j, 1), None, ALU.mult)
                dve.wait_ge(v_ready, r + 1)
                for j in range(B4):
                    n = r * B4 + j
                    last = nc.vector.tensor_scalar(L.vx[:, j * 129:j * 129 + D], L.qkv[:, (8 + j) * D:(9 + j) * D], tile_of(w.em, n, 1), None, ALU.mult)
                last.then_inc(kv_in, 1)
                next_front()
                last_end()
                dve.wait_ge(kv_ready, r + 1)
                for j in range(B4):
                    src = T[j // 2][:, (j % 2) * 256:(j % 2) * 256 + 129]
                    nc.vector.tensor_tensor(L.kvm[:, j * 144:j * 144 + D], src[:, 0:D], core.own_block[:], ALU.mult)
                    last = nc.vector.tensor_scalar(L.kvm[:, j * 144 + D:(j + 1) * 144], core.own_head[:], src[:, D:D + 1], None, ALU.mult)
                last.then_inc(kv_out, 1)
                dve.wait_ge(att_ready, r + 1)
                for j in range(B4):
                    z = T[j // 2][:, (j % 2) * 256 + D:(j % 2) * 256 + 144]
                    last = nc.vector.tensor_scalar(L.z[:, j * 16:(j + 1) * 16], z, EPS_K, None, ALU.add)
                link(last)
                link(nc.vector.reciprocal(L.zr[:], L.z[:]))
                for j in range(B4):
                    a = T[j // 2][:, (j % 2) * 256:(j % 2) * 256 + D].rearrange("p (h c) -> p c h", c=HD)
                    z = L.zr[:, j * 16:(j + 1) * 16].rearrange("p (o h) -> p o h", o=1).to_broadcast([P, HD, HEADS])
                    to = L.twice[:, j * 256:(j + 1) * 256].rearrange("p (c x h) -> p c x h", x=2, h=HEADS)
                    for x in range(2):
                        last = nc.vector.tensor_tensor(to[:, :, x, :], a, z, ALU.mult)
                link(last)
                link(nc.vector.transpose(L.turned[:], L.twice[:]))
                tv = L.turned[:].rearrange("p (j c x m) -> p x (j c) m", j=B4, x=2, m=HEADS)
                part = L.part[:].rearrange("p (a m) -> p a m", m=HEADS)
                link(nc.vector.tensor_scalar(part, tv[:, 0], core.even16[:, 0:1], None, ALU.mult))
                for j in range(B4):
                    own = slice(j * HD, (j + 1) * HD)
                    last = nc.vector.scalar_tensor_tensor(out=L.att[:, j * D:(j + 1) * D].rearrange("p (m c) -> p c m", c=HD), in0=tv[:, 1, own],
                                                          scalar=core.even16[:, 1:2], in1=part[:, own], op0=ALU.mult, op1=ALU.add)
                last.then_inc(att_out, 1)
                assert done[0] == STEPS, done[0]

            def end(r):
                done = [0]

                def link(ins):
                    done[0] += 1
                    ins.then_inc(end_chain, 1)
                    dve.wait_ge(end_chain, r * END_STEPS + done[0])

                dve.wait_ge(y_ready, r + 1)
                y = O[:, 0:512].rearrange("p (j d) -> p j d", d=D)
                yb = L.y[:].rearrange("p (j d) -> p j d", d=D)
                nc.vector.tensor_tensor(yb, y, bc(w.bd, B4), ALU.add).then_inc(y_out, 1)
                dve.wait_ge(y_out, r + 1)
                for j in range(B4):
                    last = nc.vector.bn_stats(L.stat6[:, j * 6:j * 6 + 6], L.y[:, j * D:(j + 1) * D])
                link(last)
                moments(nc, dve, end_chain, r * END_STEPS + done[0], L.stat6[:, 0:24], L.mean[:, 0:B4], L.var[:, 0:B4], L.total[:, 0:B4], L.gap[:, 0:B4])
                done[0] += 3
                nc.vector.tensor_scalar(L.var[:, 0:B4], L.var[:, 0:B4], EPS_LN1, None, ALU.add).then_inc(end_var, 1)
                dve.wait_ge(end_root, r + 1)
                link(nc.vector.reciprocal(L.rs[:, 0:B4], L.root[:, 0:B4]))
                for j in range(B4):
                    last = nc.vector.tensor_scalar(L.y[:, j * D:(j + 1) * D], L.y[:, j * D:(j + 1) * D], L.mean[:, j:j + 1],
                                                   L.rs[:, j:j + 1], ALU.subtract, ALU.mult)
                link(last)
                link(nc.vector.tensor_tensor(yb, yb, bc(w.gamma, B4), ALU.mult))
                link(nc.vector.tensor_tensor(yb, yb, bc(w.beta, B4), ALU.add))
                xt = core.x[:, bass.ds(r * (B4 * D), B4 * D)]
                link(nc.vector.scalar_tensor_tensor(out=L.y[:], in0=L.y[:], scalar=core.gate[:, w.gate:w.gate + 1], in1=xt, op0=ALU.mult, op1=ALU.add))
                nc.vector.tensor_scalar(xt, L.y[:], 1.0, None, ALU.mult)
                for j in range(B4):
                    last = nc.vector.bn_stats(tile_of(core.stats, r * B4 + j, 6), L.y[:, j * D:(j + 1) * D])
                link(last)
                assert done[0] == END_STEPS, done[0]
            nc.vector.memset(L.vx[:], 1.0).then_inc(ones_column, 1)
            dve.wait_ge(ones_column, 1)
            rounds(dve, front, back, end)

        @block.gpsimd
        def _(pool):
            v = L.qkv[:, 8 * D:12 * D].rearrange("p (j d) -> p j d", d=D)
            bc = lambda a: a[:].rearrange("p (o d) -> p o d", o=1).to_broadcast([P, B4, D])
            with pool.Fori(0, ROUNDS) as r:
                pool.wait_ge(norm_out, r + 1)
                nc.gpsimd.tensor_tensor(v, v, bc(w.gamma), ALU.mult).then_inc(v_scaled, 1)
                pool.wait_ge(v_scaled, r + 1)
                nc.gpsimd.tensor_tensor(v, v, bc(w.beta), ALU.add).then_inc(v_ready, 1)

        @block.scalar
        def _(act):
            def front(r):
                act.wait_ge(xnT_ready, r + 1)
                wait(act, proj, r)
                nc.scalar.activation(L.xnT[:], A[:, 0:512], ACT.Copy).then_inc(xnT_out, 1)

            def back(r, next_front, last_end):
                act.wait_ge(var_ready, r + 1)
                nc.scalar.activation(L.root[:, 0:12], L.var[:, 0:12], ACT.Sqrt).then_inc(root_ready, 1)
                act.wait_ge(norm_in, r + 1)
                for t in (0, 2):
                    for j in range(B4):
                        i = t * B4 + j
                        last = nc.scalar.activation(L.qkv[:, i * D:(i + 1) * D], where[t][:, j * D:(j + 1) * D], ACT.Identity,
                                                    bias=L.total[:, i:i + 1], scale=L.rs[:, i:i + 1])
                last.then_inc(norm_out, 1)
                act.wait_ge(qT_ready, r + 1)
                nc.scalar.activation(L.qT[:], S[1][:, 512:1024], ACT.Copy).then_inc(qT_out, 1)
                last_end()
                next_front()
                act.wait_ge(attT_ready, r + 1)
                nc.scalar.activation(L.attT[:], O[:, 0:512], ACT.Copy).then_inc(attT_out, 1)

            def end(r):
                act.wait_ge(end_var, r + 1)
                nc.scalar.activation(L.root[:, 0:B4], L.var[:, 0:B4], ACT.Sqrt).then_inc(end_root, 1)

            rounds(act, front, back, end)

        @block.tensor
        def _(pe):
            def turn_x(r):
                pe.wait_ge(xn_ready, r + 1)
                wait(pe, xnT_out, r)
                for j in range(B4):
                    last = nc.tensor.transpose(A[:, j * P:(j + 1) * P], L.xn[:, j * D:(j + 1) * D], core.ident[:])
                last.then_inc(xnT_ready, 1)

            def project(r):
                pe.wait_ge(ctx_in, r * 16 + 16)
                pe.wait_ge(xnT_out, r + 1)
                wait(pe, proj_read, r)
                wait(pe, norm_out, r)
                for t, (left, right) in enumerate(((L.xnT, w.wq), (L.ctxT, w.wk), (L.ctxT, w.wv))):
                    for j in range(B4):
                        last = nc.tensor.matmul(where[t][:, j * D:(j + 1) * D], left[:, j * P:(j + 1) * P], right[:], start=True, stop=True)
                last.then_inc(proj, 1)

            def back(r, more):
                pe.wait_ge(kv_in, r + 1)
                for j in range(B4):
                    last = nc.tensor.matmul(T[j // 2][:, (j % 2) * 256:(j % 2) * 256 + 129], L.qkv[:, (4 + j) * D:(5 + j) * D],
                                            L.vx[:, j * 129:(j + 1) * 129], start=True, stop=True)
                last.then_inc(kv_ready, 1)
                for j in range(B4):
                    last = nc.tensor.transpose(S[1][:, 512 + j * P:512 + (j + 1) * P], L.qkv[:, j * D:(j + 1) * D], core.ident[:])
                last.then_inc(qT_ready, 1)
                if more:
                    turn_x(r + 1)
                pe.wait_ge(qT_out, r + 1)
                pe.wait_ge(kv_out, r + 1)
                for j in range(B4):
                    last = nc.tensor.matmul(T[j // 2][:, (j % 2) * 256:(j % 2) * 256 + 144], L.qT[:, j * P:(j + 1) * P],
                                            L.kvm[:, j * 144:(j + 1) * 144], start=True, stop=True)
                last.then_inc(att_ready, 1)
                if more:
                    project(r + 1)
                pe.wait_ge(att_out, r + 1)
                wait(pe, y_out, r)
                for j in range(B4):
                    last = nc.tensor.transpose(O[:, j * P:(j + 1) * P], L.att[:, j * D:(j + 1) * D], core.perm[:])
                last.then_inc(attT_ready, 1)
                pe.wait_ge(attT_out, r + 1)
                for j in range(B4):
                    last = nc.tensor.matmul(O[:, j * D:(j + 1) * D], L.attT[:, j * P:(j + 1) * P], w.wd[:], start=True, stop=True)
                last.then_inc(y_ready, 1)

            turn_x(0)
            project(0)
            back(0, True)
            with pe.Fori(1, ROUNDS - 1) as r:
                back(r, True)
            back(ROUNDS - 1, False)


def norm_and_route(nc, sem, core, w, b1):
    xn_ready, xn_kept, xnT_ready, xnT_out, logit_ready, logit_out = (
        sem("xn_ready"), sem("xn_kept"), sem("xnT_ready"), sem("xnT_out"), sem("logit_ready"), sem("logit_out"))
    bias_landed = sem("bias_landed")
    T, A = core.bankT, [core.bankA, core.bankO]
    routed, dense = w.router is not None, w.dense
    per = routed + dense
    W, B4 = BLOCK * P, BLOCK

    def quads(eng, step, last):
        for c in range(4):
            step(Batch(0, c))
        with eng.Fori(0, (NBLK - 4) // 2) as i:
            step(Batch(i, 4))
            step(Batch(i, 5))
        if last is not None:
            last(Batch(0, NBLK - 1))

    with nc.Block() as block:
        @block.sync
        def _(sp):
            if routed:
                sp.dma_start(core.b1_big[:, 0:b1.shape[0]], b1.partition_broadcast(P)).then_inc(bias_landed, 16)
                sp.wait_ge(bias_landed, 16)

        @block.vector
        def _(dve):
            def logits_out(q):
                wait(dve, logit_ready, q.n + 1)
                nc.vector.tensor_tensor(tile_of(core.logits, q.n, B4 * E).rearrange("p (j e) -> p j e", e=E),
                                        A[q.slot][:, 0:B4 * E].rearrange("p (j e) -> p j e", e=E),
                                        w.router_bias[:].rearrange("p (o e) -> p o e", o=1).to_broadcast([P, B4, E]), ALU.add).then_inc(logit_out, 1)

            def last_logits(q):
                logits_out(q.shift(-1))
                logits_out(q)

            def step(q):
                wait(dve, xnT_ready, q.n - 1)
                if routed:
                    wait(dve, xn_kept, q.n - 1)
                for j in range(B4):
                    n = q.n * B4 + j
                    last = nc.vector.tensor_scalar(core.quad_xn[q.slot][:, j * D:(j + 1) * D], tile_of(core.x, n), tile_of(core.mean, n, 1),
                                                   tile_of(core.rstd, n, 1), ALU.subtract, ALU.mult)
                last.then_inc(xn_ready, 1)
                if routed and exists(q.shift(-2)):
                    logits_out(q.shift(-2))
            quads(dve, step, last_logits if routed else None)

        @block.scalar
        def _(act):
            def step(q):
                wait(act, xnT_ready, q.n + 1)
                if routed:
                    wait(act, logit_ready, q.n - 1)
                    nc.scalar.activation(core.quad_xnT[q.slot][:], T[q.slot][:], ACT.Copy).then_inc(xnT_out, 1)
                if dense:
                    nc.scalar.activation(tile_of(core.xnT, q.n, W), T[q.slot][:], ACT.Copy).then_inc(xnT_out, 1)
                if routed:
                    nc.scalar.activation(tile_of(core.xn_all, q.n, B4 * RW).rearrange("p (j c) -> p j c", c=RW)[:, :, 0:D],
                                         core.quad_xn[q.slot][:].rearrange("p (j d) -> p j d", d=D), ACT.Copy).then_inc(xn_kept, 1)
            quads(act, step, None)

        @block.tensor
        def _(pe):
            def logits(q):
                wait(pe, xnT_out, q.n * per + 1)
                wait(pe, logit_out, q.n - 1)
                for j in range(B4):
                    last = nc.tensor.matmul(A[q.slot][:, j * E:(j + 1) * E], core.quad_xnT[q.slot][:, j * P:(j + 1) * P], w.router[:],
                                            start=True, stop=True)
                last.then_inc(logit_ready, 1)

            def step(q):
                wait(pe, xn_ready, q.n + 1)
                wait(pe, xnT_out, (q.n - 1) * per)
                for j in range(B4):
                    last = nc.tensor.transpose(T[q.slot][:, j * P:(j + 1) * P], core.quad_xn[q.slot][:, j * D:(j + 1) * D], core.ident[:])
                last.then_inc(xnT_ready, 1)
                if routed and exists(q.shift(-1)):
                    logits(q.shift(-1))
            quads(pe, step, logits if routed else None)


def route(nc, sem, core, kind, gate, capacity):
    chain, act_in, act_out, rank_in, rank_ready = sem("chain"), sem("act_in"), sem("act_out"), sem("rank_in"), sem("rank_ready")
    R = core.route
    N = NB * E
    v3 = lambda a: a[:].rearrange("p (n e) -> p n e", e=E)
    row = lambda a: a[:].rearrange("p (n o) -> p n o", o=1).to_broadcast([P, NB, E])
    tg = core.gate[:, gate:gate + 1]
    two = kind == "top2"
    with nc.Block() as block:
        @block.vector
        def _(dve):
            done = [0]

            def link(ins):
                done[0] += 1
                ins.then_inc(chain, 1)
                dve.wait_ge(chain, done[0])

            def first_of_largest(out, values, top, mark, best):
                link(nc.vector.tensor_reduce(out=top[:], in_=v3(values), op=ALU.max, axis=AX))
                link(nc.vector.tensor_tensor(v3(mark), v3(values), row(top), ALU.is_equal))
                link(nc.vector.tensor_tensor(mark[:], mark[:], core.countdown[:], ALU.mult))
                link(nc.vector.tensor_reduce(out=best[:], in_=v3(mark), op=ALU.max, axis=AX))
                link(nc.vector.tensor_tensor(v3(out), v3(mark), row(best), ALU.is_equal))

            if two:
                dve.wait_ge(act_out, 1)
                first_of_largest(R.one, R.prob, R.top, R.mark, R.best)
                link(nc.vector.tensor_scalar(R.left[:], R.one[:], -1.0, 1.0, ALU.mult, ALU.add))
                link(nc.vector.tensor_tensor(R.left[:], R.prob[:], R.left[:], ALU.mult))
                link(nc.vector.tensor_tensor(R.left[:], R.left[:], R.one[:], ALU.subtract))
                first_of_largest(R.other, R.left, R.top, R.mark, R.best)
                link(nc.vector.tensor_tensor(R.chosen[:], R.one[:], R.other[:], ALU.add))
            else:
                link(nc.vector.tensor_reduce(out=R.top[:], in_=v3(core.logits), op=ALU.max, axis=AX))
                nc.vector.tensor_tensor(v3(R.left), v3(core.logits), row(R.top), ALU.subtract).then_inc(act_in, 1)
                dve.wait_ge(act_out, 1)
                link(nc.vector.tensor_reduce(out=R.best[:], in_=v3(R.prob), op=ALU.add, axis=AX))
                link(nc.vector.reciprocal(R.top[:], R.best[:]))
                link(nc.vector.tensor_tensor(v3(R.prob), v3(R.prob), row(R.top), ALU.mult))
                first_of_largest(R.one, R.prob, R.top, R.mark, R.best)
                link(nc.vector.tensor_copy(R.chosen[:], R.one[:]))
            nc.vector.engine_nop().then_inc(rank_in, 1)
            dve.wait_ge(rank_ready, 1)
            link(nc.vector.memset(R.two[:], 0.0))
            link(nc.vector.tensor_copy(R.two[:, E:N], core.bankT[1][:, 0:N - E]))
            a, b = R.two, R.mark
            for shift in (1, 2, 4, 8, 16):
                k = shift * E
                nc.vector.tensor_copy(b[:, 0:k], a[:, 0:k]).then_inc(chain, 1)
                done[0] += 1
                link(nc.vector.tensor_tensor(b[:, k:N], a[:, k:N], a[:, 0:N - k], ALU.add))
                a, b = b, a
            link(nc.vector.tensor_tensor(R.count[:], a[:, N - E:N], core.bankT[1][:, N - E:N], ALU.add))
            link(nc.vector.tensor_tensor(v3(b).rearrange("p n e -> p e n"), R.count[:].rearrange("p (e o) -> p e o", o=1).to_broadcast([P, E, NB]),
                                         core.tile_start[:].rearrange("p (n e) -> p e n", e=E), ALU.is_gt))
            link(nc.vector.tensor_reduce(out=R.tiles[:], in_=v3(b).rearrange("p n e -> p e n"), op=ALU.add, axis=AX))
            c, d = R.tiles, R.scan[0]
            for k, other in ((1, R.scan[0]), (2, R.scan[1]), (4, R.scan[0])):
                nc.vector.tensor_copy(other[:, 0:k], c[:, 0:k]).then_inc(chain, 1)
                done[0] += 1
                link(nc.vector.tensor_tensor(other[:, k:E], c[:, k:E], c[:, 0:E - k], ALU.add))
                c = other
            ends = c
            link(nc.vector.tensor_tensor(R.starts[:], ends[:], R.tiles[:], ALU.subtract))
            link(nc.vector.tensor_tensor(a[:], a[:], core.bankT[0][:, 0:N], ALU.add))
            if capacity is not None:
                link(nc.vector.tensor_scalar(R.left[:], a[:], float(capacity), None, ALU.is_le))
                link(nc.vector.tensor_tensor(R.prob[:], R.prob[:], R.left[:], ALU.mult))
            link(nc.vector.scalar_tensor_tensor(out=v3(a), in0=R.starts[:].rearrange("p (o e) -> p o e", o=1).to_broadcast([P, NB, E]), scalar=float(P),
                                                in1=v3(a), op0=ALU.mult, op1=ALU.add))
            for c, one in enumerate((R.one, R.other) if two else (R.one,)):
                link(nc.vector.tensor_tensor(b[:], one[:], a[:], ALU.mult))
                link(nc.vector.tensor_reduce(out=R.best[:], in_=v3(b), op=ALU.add, axis=AX))
                link(nc.vector.tensor_scalar(core.slots[c][:], R.best[:], -1.0, None, ALU.add))
                link(nc.vector.tensor_tensor(b[:], one[:], R.prob[:], ALU.mult))
                link(nc.vector.tensor_reduce(out=R.best[:], in_=v3(b), op=ALU.add, axis=AX))
                link(nc.vector.tensor_scalar(core.weights[c][:], R.best[:], tg, None, ALU.mult))
            i3 = core.tile_number[:].rearrange("p (i e) -> p i e", e=E)
            link(nc.vector.tensor_tensor(core.tile_mark[:].rearrange("p (i e) -> p i e", e=E), i3,
                                         ends[:].rearrange("p (o e) -> p o e", o=1).to_broadcast([P, TILES2, E]), ALU.is_ge))
            link(nc.vector.tensor_reduce(out=core.tile_sum[:], in_=core.tile_mark[:].rearrange("p (i e) -> p i e", e=E), op=ALU.add, axis=AX))
            link(nc.vector.tensor_scalar(core.tile_expert[:], core.tile_sum[:], float(E - 1), None, ALU.min))

        @block.scalar
        def _(act):
            if two:
                nc.scalar.activation(R.prob[:], core.logits[:], ACT.Sigmoid).then_inc(act_out, 1)
            else:
                act.wait_ge(act_in, 1)
                nc.scalar.activation(R.prob[:], R.left[:], ACT.Exp).then_inc(act_out, 1)

        @block.tensor
        def _(pe):
            pe.wait_ge(rank_in, 1)
            nc.tensor.matmul(core.bankT[0][:, 0:N], core.upper[:], R.chosen[:], start=True, stop=True)
            nc.tensor.matmul(core.bankT[1][:, 0:N], core.ones[:], R.chosen[:], start=True, stop=True).then_inc(rank_ready, 1)


def send_rows(nc, sem, pool, core, rows_in, copies):
    placed = sem("placed")
    for c in range(copies):
        nc.gpsimd.iota(core.xn_all[:].bitcast(I32).rearrange("p (n c) -> p n c", c=RW)[:, :, D:RW], pattern=[[P, NB], [0, 1]], base=c * T_ALL,
                       channel_multiplier=1).then_inc(placed, 1)
        pool.wait_ge(placed, c + 1)
        for n in range(NB):
            nc.gpsimd.indirect_dma_start(rows_in, bass.IndirectOffsetOnAxis(ap=core.slots[c][:, n:n + 1], axis=0),
                                         core.xn_all[:, n * RW:(n + 1) * RW], None).then_inc(core.sent, 16)
        core.sent_before += NB
        pool.wait_ge(core.sent, 16 * core.sent_before)


def dispatch(nc, sem, core, rows_in, copies):
    with nc.Block() as block:
        @block.gpsimd
        def _(pool):
            send_rows(nc, sem, pool, core, rows_in, copies)


def expert_tiles(nc, sem, core, w, rows_in, tiles):
    H = w.chunks * P
    C = w.chunks
    rows_landed, places_out = [sem(f"rows_landed{k}") for k in range(2)], sem("places_out")
    scattered, before = core.scattered, core.scattered_before
    core.scattered_before += tiles // 8 * 64
    xT_ready, xT_out, up_ready, biased, hidden = sem("xT_ready"), sem("xT_out"), sem("up_ready"), sem("biased"), sem("hidden")
    hT_ready, hT_out, y_ready, y_out = sem("hT_ready"), sem("hT_out"), sem("y_ready"), sem("y_out")
    X = core.tile
    T, S, Y = core.bankT, core.bankS, [core.bankA, core.bankO]

    def staged(eng, step):
        known = {}
        for c in range(-1, 8):
            step(Tile(0, c), known)
        with eng.Fori(0, (tiles - 16) // 8) as i:
            known = {}
            for u in range(8):
                step(Tile(i, 8 + u), known)
        known = {}
        for c in range(tiles - 8, tiles + 2):
            step(Tile(0, c), known)

    def real(t):
        return not isinstance(t.n, int) or 0 <= t.n < tiles

    def expert_of(eng, t, known):
        if t.n_key not in known:
            at = core.tile_expert[0:1, bass.ds(t.n, 1)] if not isinstance(t.n, int) else core.tile_expert[0:1, t.n:t.n + 1]
            known[t.n_key] = eng.value_load(at, min_val=0, max_val=E - 1)
        return known[t.n_key]

    def rows(dram, t):
        part = dram[bass.ds(t.n * P, 4 * P), :] if not isinstance(t.n, int) else dram[t.n * P:(t.n + 4) * P, :]
        return part.rearrange("(j p) d -> p j d", p=P)

    with nc.Block() as block:
        @block.sync
        def _(sp):
            def load(t):
                wait(sp, places_out, t.fours - 1)
                sp.dma_start(X.rows[:, t.four * 4 * RW:(t.four + 1) * 4 * RW].rearrange("p (j d) -> p j d", d=RW),
                             rows(rows_in, t)).then_inc(rows_landed[t.four], 16)

            for c in (0, 4, 8, 12):
                load(Tile(0, c))
            with sp.Fori(0, (tiles - 16) // 8) as i:
                load(Tile(i, 16))
                load(Tile(i, 20))

        @block.gpsimd
        def _(pool):
            for t in range(tiles):
                wait(pool, y_out, t + 1)
                wait(pool, places_out, t // 4 + 1)
                nc.gpsimd.indirect_dma_start(core.outputs, bass.IndirectOffsetOnAxis(ap=core.places[:, t:t + 1], axis=0),
                                             X.y[:, t % 8 * D:(t % 8 + 1) * D], None).then_inc(scattered[t // 4 % 2], 16)
            for k in range(2):
                pool.wait_ge(scattered[k], before + tiles // 8 * 64)

        @block.vector
        def _(dve):
            def step(t, known):
                d = t.shift(-2)
                if real(t) and t.in8 % 4 == 3:
                    wait(dve, xT_ready, t.n + 1)
                    to = core.places[:, bass.ds(t.n - 3, 4)] if not isinstance(t.n, int) else core.places[:, t.n - 3:t.n + 1]
                    nc.vector.tensor_scalar(to, X.rows[:, t.four * 4 * RW:(t.four + 1) * 4 * RW].bitcast(I32).rearrange("p (j d) -> p j d", d=RW)[:, :, D],
                                            0, None, ALU.add).then_inc(places_out, 1)
                if real(t):
                    e = expert_of(dve, t, known)
                    wait(dve, up_ready, t.n + 1)
                    wait(dve, hT_ready, t.n - 1)
                    nc.vector.tensor_tensor(X.h[t.slot][:, 0:H], S[t.slot][:, 0:H], core.b1_big[:, bass.ds(e * H, H)], ALU.add).then_inc(biased, 1)
                if real(d):
                    e = expert_of(dve, d, known)
                    wait(dve, y_ready, d.n + 1)
                    if d.in8 % 4 == 0:
                        if not (isinstance(d.turn, int) and d.turn == 0):
                            wait(dve, scattered[d.four], d.turn * 64 + before)
                    nc.vector.tensor_tensor(X.y[:, d.in8 * D:(d.in8 + 1) * D], Y[d.slot][:, 0:D], w.b2[:, bass.ds(e * D, D)], ALU.add).then_inc(y_out, 1)
            staged(dve, step)

        @block.scalar
        def _(act):
            def step(t, known):
                a, c = t.shift(1), t.shift(-1)
                if real(a):
                    wait(act, xT_ready, a.n + 1)
                    wait(act, up_ready, a.n - 1)
                    nc.scalar.activation(X.xT[a.slot][:], T[a.slot][:, 0:P], ACT.Copy).then_inc(xT_out, 1)
                if real(c):
                    wait(act, hT_ready, c.n + 1)
                    wait(act, y_ready, c.n - 1)
                    nc.scalar.activation(X.hT[c.slot][:, 0:H], S[c.slot][:, 512:512 + H], ACT.Copy).then_inc(hT_out, 1)
                if real(t):
                    wait(act, biased, t.n + 1)
                    nc.scalar.activation(X.h[t.slot][:, 0:H], X.h[t.slot][:, 0:H], w.act).then_inc(hidden, 1)
            staged(act, step)

        @block.tensor
        def _(pe):
            def step(t, known):
                a, c, d = t.shift(1), t.shift(-1), t.shift(-2)
                if real(a):
                    wait(pe, rows_landed[a.four], (a.turn + 1) * 16)
                    wait(pe, xT_out, a.n - 1)
                    nc.tensor.transpose(T[a.slot][:, 0:P], X.rows[:, a.in8 * RW:a.in8 * RW + D], core.ident[:]).then_inc(xT_ready, 1)
                if real(t):
                    e = expert_of(pe, t, known)
                    wait(pe, xT_out, t.n + 1)
                    wait(pe, biased, t.n - 1)
                    nc.tensor.matmul(S[t.slot][:, 0:H], X.xT[t.slot][:], w.w1[:, bass.ds(e * H, H)], start=True, stop=True).then_inc(up_ready, 1)
                if real(c):
                    wait(pe, hidden, c.n + 1)
                    wait(pe, hT_out, c.n - 1)
                    for k in range(C):
                        last = nc.tensor.transpose(S[c.slot][:, 512 + k * P:512 + (k + 1) * P], X.h[c.slot][:, k * P:(k + 1) * P], core.ident[:])
                    last.then_inc(hT_ready, 1)
                if real(d):
                    e = expert_of(pe, d, known)
                    wait(pe, hT_out, d.n + 1)
                    wait(pe, y_out, d.n - 1)
                    for k in range(C):
                        last = nc.tensor.matmul(Y[d.slot][:, 0:D], X.hT[d.slot][:, k * P:(k + 1) * P], w.w2[:, bass.ds(e * (C * D) + k * D, D)],
                                                start=(k == 0), stop=(k == C - 1))
                    last.then_inc(y_ready, 1)
            staged(pe, step)


def combine(nc, sem, core, copies, raw, mask):
    mask_in, on, neg = sem("mask_in"), sem("on"), sem("neg")
    landed, added, stats_new = [sem(f"landed{k}") for k in range(2)], sem("added"), sem("stats_new")
    EIGHT, loads = 8, NB // 8 * copies
    with nc.Block() as block:
        @block.sync
        def _(sp):
            for k in range(loads):
                wait(sp, added, k - 1)
                first = k % copies * T_ALL + k // copies * EIGHT * P
                sp.dma_start(core.back[k % 2][:].rearrange("p (n d) -> p n d", d=D),
                             core.outputs[first:first + EIGHT * P, :].rearrange("(n p) d -> p n d", p=P)).then_inc(landed[k % 2], 16)
                if k == 1 and mask is not None:
                    sp.dma_start(raw, mask.partition_broadcast(P)).then_inc(mask_in, 16)

        @block.vector
        def _(dve):
            with dve.Fori(0, loads // 2) as i:
                for u in range(2):
                    c, batches = u % copies, [(i * (2 // copies) + u // copies) * EIGHT + j for j in range(EIGHT)]
                    dve.wait_ge(landed[u], i * 16 + 16)
                    if c:
                        dve.wait_ge(added, i * 2 + u)
                    for j, n in enumerate(batches):
                        xt = tile_of(core.x, n)
                        last = nc.vector.scalar_tensor_tensor(out=xt, in0=core.back[u][:, j * D:(j + 1) * D], scalar=tile_of(core.weights[c], n, 1), in1=xt,
                                                              op0=ALU.mult, op1=ALU.add)
                    last.then_inc(added, 1)
                    if c == copies - 1:
                        dve.wait_ge(added, i * 2 + u + 1)
                        nc.vector.memset(core.pause[:], 0.0)
                        for n in batches:
                            last = nc.vector.bn_stats(tile_of(core.stats, n, 6), tile_of(core.x, n))
                        last.then_inc(stats_new, 1)
            if mask is not None:
                dve.wait_ge(mask_in, 16)
                nc.vector.tensor_scalar(core.key_on[:], raw, 0.0, None, ALU.not_equal).then_inc(on, 1)
                dve.wait_ge(on, 1)
                nc.vector.tensor_scalar(core.key_neg[:, 0:NB * P], core.key_on[:], -1.0, NEG, ALU.add, ALU.mult).then_inc(neg, 1)
                dve.wait_ge(neg, 1)
            dve.wait_ge(stats_new, loads // copies)


def feed_forward(nc, sem, core, w, copies, rows_in, out):
    hidden, hidden_out, y_ready, y_read, added, stats_new = (
        sem("hidden"), sem("hidden_out"), sem("y_ready"), sem("y_read"), sem("added"), sem("stats_new"))
    stored = sem("stored")
    C, X = w.chunks, w.experts
    H = core.bankS
    Y = core.bankT
    W = BLOCK * P
    tiles_at = BLOCK // C if C < BLOCK else 1

    def steps():
        return range(2 * X)

    with nc.Block() as block:
        @block.sync
        def _(sp):
            for s in (hidden_out, y_read, y_ready):
                sp.sem_inc(s, CREDIT)
            if out is not None:
                with sp.Fori(0, NBLK) as i:
                    sp.wait_ge(added, i * X + X)
                    sp.dma_start(out[bass.ds(i * BLOCK, BLOCK)].rearrange("n p d -> p n d"),
                                 tile_of(core.x, i, BLOCK * D).rearrange("p (n d) -> p n d", d=D)).then_inc(stored, 16)
                sp.wait_ge(stored, 16 * NBLK)

        @block.tensor
        def _(pe):
            with pe.Fori(0, NBLK // 2) as i:
                for j in range(2 * X + 1):
                    e, half = j % X, j // X
                    for c in range(C):
                        if j < 2 * X:
                            k = j * C + c
                            pe.wait_ge(hidden_out, i * (2 * X * C) + k - 1 + CREDIT)
                            nc.tensor.matmul(H[k % 2][:, 0:W], w.w1[:, (e * C + c) * P:(e * C + c + 1) * P],
                                             core.xnT[:, bass.ds(i * (2 * W) + half * W, W)], start=True, stop=True).then_inc(hidden, 1)
                        if j >= 1:
                            t = j - 1
                            f = t % X
                            if c == 0:
                                pe.wait_ge(hidden_out, i * (2 * X * C) + (t + 1) * C + CREDIT)
                                pe.wait_ge(y_read, i * (2 * X) + t - 1 + CREDIT)
                            for q in range(c * tiles_at, (c + 1) * tiles_at):
                                for cc in range(C):
                                    last = nc.tensor.matmul(Y[t % 2][:, q * D:(q + 1) * D], core.hidden[t % 2][:, cc * W + q * P:cc * W + (q + 1) * P],
                                                            w.w2[:, (f * C + cc) * D:(f * C + cc + 1) * D], start=(cc == 0), stop=(cc == C - 1))
                            if c == C - 1:
                                last.then_inc(y_ready, 1)

        @block.scalar
        def _(act):
            with act.Fori(0, NBLK // 2) as i:
                for j in steps():
                    e = j % X
                    act.wait_ge(y_ready, i * (2 * X) + j - 1 + CREDIT)
                    for c in range(C):
                        k = j * C + c
                        act.wait_ge(hidden, i * (2 * X * C) + k + 1)
                        nc.scalar.activation(core.hidden[j % 2][:, c * W:(c + 1) * W], H[k % 2][:, 0:W], w.act,
                                             bias=w.b1[:, e * C + c:e * C + c + 1]).then_inc(hidden_out, 1)

        @block.vector
        def _(dve):
            with dve.Fori(0, NBLK // 2) as i:
                for j in steps():
                    e, half = j % X, j // X
                    dve.wait_ge(y_ready, i * (2 * X) + j + 1 + CREDIT)
                    tiles = [i * (2 * BLOCK) + half * BLOCK + q for q in range(BLOCK)]
                    if j:
                        dve.wait_ge(added, i * (2 * X) + j)
                    for q in range(BLOCK):
                        xt = tile_of(core.x, tiles[q])
                        last = nc.vector.scalar_tensor_tensor(out=xt, in0=Y[j % 2][:, q * D:(q + 1) * D], scalar=core.gate[:, w.gate:w.gate + 1], in1=xt,
                                                              op0=ALU.mult, op1=ALU.add)
                    last.then_inc(y_read, 1)
                    dve.wait_ge(y_read, i * (2 * X) + j + 1 + CREDIT)
                    for q in range(BLOCK):
                        xt = tile_of(core.x, tiles[q])
                        last = nc.vector.scalar_tensor_tensor(out=xt, in0=w.b2[:, e * D:(e + 1) * D], scalar=core.gate[:, w.gate:w.gate + 1], in1=xt,
                                                              op0=ALU.mult, op1=ALU.add)
                    last.then_inc(added, 1)
                    if e == X - 1 and out is None:
                        dve.wait_ge(added, i * (2 * X) + j + 1)
                        nc.vector.memset(core.pause[:], 0.0)
                        for q in range(BLOCK):
                            last = nc.vector.bn_stats(tile_of(core.stats, tiles[q], 6), tile_of(core.x, tiles[q]))
                        last.then_inc(stats_new, 1)
            if out is None:
                dve.wait_ge(stats_new, NBLK)
            else:
                dve.wait_ge(added, NBLK * X)

        @block.gpsimd
        def _(pool):
            if copies:
                send_rows(nc, sem, pool, core, rows_in, copies)


class Named:
    pass


def program(nc, a, out):
    ctx = ExitStack()
    with ctx:
        phase = [""]

        def sb(name, cols, dt=F32):
            return ctx.enter_context(nc.sbuf_tensor(name, [P, cols], dt))

        taken = []

        def sem(name):
            taken.append(nc.alloc_semaphore(name=f"{phase[0]}_{name}"))
            return taken[-1]

        def norm_scale():
            ended = list(taken)
            rebuild_norm_scale(nc, sem, core, EPS, ended)
            for s in ended:
                nc.release_semaphore(s)
                taken.remove(s)

        core = Named()
        core.ctxT_dram = a["ctxT"]
        core.bankA = ctx.enter_context(nc.psum_tensor("bankA", [P, 512], F32))
        core.bankS = [ctx.enter_context(nc.psum_tensor(f"bankS{h}", [P, 1024], F32)) for h in range(2)]
        core.bankT = [ctx.enter_context(nc.psum_tensor(f"bankT{h}", [P, 512], F32)) for h in range(2)]
        core.bankO = ctx.enter_context(nc.psum_tensor("bankO", [P, 512], F32))
        core.x = sb("x", NB * D)
        core.xnT = sb("xnT", NB * P)
        core.key_on = sb("key_on", NB * P)
        core.key_neg = sb("key_neg", NB * RW)
        core.stats, core.rstd, core.root = sb("stats", NB * 6), sb("rstd", NB), sb("root", NB)
        core.mean, core.var, core.half_sum, core.half_gap, core.pause = sb("mean", NB), sb("var", NB), sb("half_sum", NB), sb("half_gap", NB), sb("pause", 1)
        core.gate = sb("gate", 8)
        core.ident, core.ones, core.upper = sb("ident", P), sb("ones", P), sb("upper", P)
        core.head_of4, core.own_block, core.own_head = sb("head_of4", PER * P), sb("own_block", D), sb("own_head", HEADS)
        core.perm, core.even16 = sb("perm", P), sb("even16", 2)
        core.countdown = sb("countdown", NB * E)
        core.ctxT = [sb(f"ctxT{s}", P) for s in range(2)]
        core.xn = [sb(f"xn{s}", D) for s in range(2)]
        core.bias, core.top, core.recip = sb("bias", P), sb("top", HEADS), sb("recip", HEADS)
        core.xnTs = [sb(f"xnTs{s}", P) for s in range(2)]
        core.k = sb("k", P)
        core.v_early = sb("v_early", D)
        core.kz, core.qz = [sb(f"kz{s}", PER * P) for s in range(2)], [sb(f"qz{s}", GROUPS * P) for s in range(2)]
        core.v = [sb(f"v{s}", HEADS * (VW + HD + 1)) for s in range(2)]
        core.o, core.oT, core.y = sb("o", D), sb("oT", P), sb("y", D)
        big = sb("big", 2 * HEADS * P + 2 * PER * P)
        core.probs = [big[:, s * HEADS * P:(s + 1) * HEADS * P] for s in range(2)]
        core.probsT = [big[:, 2 * HEADS * P + s * PER * P:2 * HEADS * P + (s + 1) * PER * P] for s in range(2)]
        core.hidden = core.probs
        core.quad_xn, core.quad_xnT = cut(big, (BLOCK * P,) * 2), cut(big[:, 2 * BLOCK * P:], (BLOCK * P,) * 2)
        L = core.lin = Named()
        L.xn, L.xnT, L.qkv, L.vx, L.kvm, L.qT = cut(big, (512, 512, 1536, 4 * 129, 4 * 144, 512))
        lin = sb("lin", 3 * 512 + 72 + 36 + 12 + 12 + 12 + 64 + 64)
        L.ctxT, L.attT, L.y, L.stat6, L.mean, L.total, L.gap, L.var, L.root, L.rs, L.z, L.zr = cut(
            lin, (512, 512, 512, 72, 12, 12, 12, 12, 12, 12, 64, 64))
        L.twice, L.turned, L.part, L.att = core.key_on[:, 0:1024], core.key_on[:, 1024:2048], core.key_on[:, 2048:2560], core.key_on[:, 2560:3072]
        core.logits = sb("logits", NB * E)
        core.weights, core.slots = [sb(f"weights{c}", NB) for c in range(2)], [sb(f"slots{c}", NB, I32) for c in range(2)]
        core.tile_start, core.tile_number, core.tile_mark = sb("tile_start", NB * E), sb("tile_number", TILES2 * E), sb("tile_mark", TILES2 * E)
        core.tile_sum, core.tile_expert = sb("tile_sum", TILES2), sb("tile_expert", TILES2, I32)
        core.sent, core.scattered = nc.alloc_semaphore(name="rows_sent"), [nc.alloc_semaphore(name=f"scattered{k}") for k in range(2)]
        core.sent_before, core.scattered_before = 0, 0
        core.back = cut(big, (8 * D,) * 2)
        core.xn_all, core.b1_big = core.key_neg, core.key_on
        X = core.tile = Named()
        X.h, X.hT, X.xT = (cut(big[:, at:at + 2 * width], (width,) * 2) for at, width in ((0, 512), (1024, 512), (2048, P)))
        X.rows, X.y = big[:, 2304:2304 + 8 * RW], big[:, 2304 + 8 * RW:2304 + 8 * (RW + D)]
        core.rows_in = [nc.dram_tensor(f"rows_in{l}", (tiles * P, RW), F32).ap() for l, tiles in enumerate((TILES2, TILES1, TILES1))]
        core.outputs = nc.dram_tensor("outputs", (2 * T_ALL + EMPTY * P, D), F32).ap()
        core.places = sb("places", TILES2, I32)
        R = core.route = Named()
        R.prob, R.one, R.two, R.mark, R.left, R.other, R.chosen = cut(big, (NB * E,) * 7)
        R.top, R.best = sb("route_top", NB), sb("route_best", NB)
        R.count, R.tiles, R.starts = sb("route_count", E), sb("route_tiles", E), sb("route_starts", E)
        R.scan = [sb(f"route_scan{k}", E) for k in range(2)]
        w1_big = sb("w1_big", 9 * 4 * P)
        w2_big = sb("w2_big", 9 * 4 * D)
        b2_big = sb("b2_big", 9 * D)

        phase[0] = "setup"
        loaded, const0, const1, const2, gate_done = sem("loaded"), sem("const0"), sem("const1"), sem("const2"), sem("gate_done")
        first, chain, zeroed, emptied, numbered, x_in = sem("first"), sem("chain"), sem("zeroed"), sem("emptied"), sem("numbered"), [sem(f"x_in{k}") for k in range(4)]
        W = {}
        early = {f"{k}0" for k in ("wq", "wk", "wv", "wo", "bq", "bk", "bv", "bo")} | {"bq2", "bq3"}
        loads, late = [], []

        def weight_tile(name, cols, src):
            t = sb(name, cols)
            (loads if name in early else late).append((t[:], src))
            return t

        for l in (0, 2, 3):
            w = W[l] = Named()
            w.gate = l
            w.wq, w.wk, w.wv, w.wo = (weight_tile(f"w{k}{l}", D, a[f"w{k}{l}"]) for k in "qkvo")
            w.bq, w.bk = (weight_tile(f"b{k}{l}", 1, a[f"b{k}{l}"].rearrange("(p o) -> p o", o=1)) for k in "qk")
            w.bv, w.bo = (weight_tile(f"b{k}{l}", D, a[f"b{k}{l}"].partition_broadcast(P)) for k in "vo")
        w = W[1] = Named()
        w.gate = 1
        w.wq, w.wk, w.wv, w.wd = (weight_tile(f"w{k}1", D, a[f"w{k}1"]) for k in "qkvd")
        w.gamma, w.beta, w.bd = (weight_tile(n, D, a[n].partition_broadcast(P)) for n in ("gamma", "beta", "bd1"))
        w.em = weight_tile("em", NB, a["em"])
        src = weight_tile("src", P, a["src"])
        ffn = {}
        for l, C, router, act in ((0, 4, "wr0", ACT.Gelu), (1, 2, "wr1", ACT.Relu), (2, 4, "wr2", ACT.Gelu)):
            f = ffn[l] = Named()
            f.chunks, f.act, f.gate, f.dense = C, act, 4 + l, l == 0
            f.w1, f.w2, f.b2 = w1_big, w2_big, b2_big
            f.router = weight_tile(router, E, a[router])
            f.router_bias = sb(f"router_bias{l}", E)
        dense = {}
        for l, at in ((0, E), (3, 0)):
            f = dense[l] = Named()
            f.experts, f.chunks, f.act, f.gate, f.dense, f.router = 1, 4, ACT.Gelu, 4 + l, True, None
            f.w1, f.w2, f.b2 = w1_big[:, at * 512:(at + 1) * 512], w2_big[:, at * 512:(at + 1) * 512], b2_big[:, at * D:(at + 1) * D]
            f.b1 = weight_tile(f"b1_dense{l}", 4, a[f"b1_dense{l}"])
        extra = sb("extra_bias", E)
        loads.append((ffn[0].router_bias[:], a["bg0"].partition_broadcast(P)))
        loads.append((extra[:], a["bias0"].partition_broadcast(P)))
        loads.append((ffn[1].router_bias[:], a["br1"].partition_broadcast(P)))
        loads.append((core.gate[:, 0:4], a["g_xattn"].partition_broadcast(P)))
        loads.append((core.gate[:, 4:8], a["g_ffn"].partition_broadcast(P)))
        for l, tiles in enumerate((TILES2, TILES1, TILES1)):
            for at in range(0, tiles, EMPTY):
                n = min(EMPTY, tiles - at)
                late.append((core.rows_in[l][at * P:(at + n) * P, :].rearrange("(t p) d -> p t d", p=P),
                             core.key_neg[:, 0:n * RW].rearrange("p (t d) -> p t d", d=RW)))

        with nc.Block() as block:
            @block.sync
            def _(sp):
                for k in range(4):
                    part = slice(k * NB // 4, (k + 1) * NB // 4)
                    sp.dma_start(core.x[:].rearrange("p (n d) -> p n d", d=D)[:, part], a["x"].rearrange("n p d -> p n d")[:, part]).then_inc(x_in[k], 16)
                for dst, s in loads:
                    sp.dma_start(dst, s).then_inc(loaded, 16)
                sp.wait_ge(loaded, 16 * len(loads))

            @block.gpsimd
            def _(pool):
                pool.memset(core.ones[:], 1.0)
                pool.memset(core.ident[:], 0.0)
                pool.memset(core.qz[0][:], 0.0)
                pool.memset(core.qz[1][:], 0.0)
                pool.memset(core.perm[:], 0.0)
                pool.memset(core.v[0][:], 0.0)
                pool.memset(core.v[1][:], 0.0).then_inc(zeroed, 1)
                pool.wait_ge(zeroed, 1)
                pool.memset(own_strips(core.v[0])[:, :, :, HD:HD + 1], 1.0)
                pool.memset(own_strips(core.v[1])[:, :, :, HD:HD + 1], 1.0)
                pool.memset(core.head_of4[:], 1.0)
                pool.memset(core.own_block[:], 1.0)
                pool.memset(core.own_head[:], 1.0)
                pool.iota(core.tile_start[:], pattern=[[P, NB], [0, E]], base=0, channel_multiplier=0, allow_small_or_imprecise_dtypes=True)
                pool.iota(core.tile_number[:], pattern=[[1, TILES2], [0, E]], base=0, channel_multiplier=0, allow_small_or_imprecise_dtypes=True)
                pool.iota(core.countdown[:], pattern=[[0, NB], [-1, E]], base=E, channel_multiplier=0,
                          allow_small_or_imprecise_dtypes=True).then_inc(const0, 1)
                pool.wait_ge(const0, 1)
                pool.affine_select(out=core.ident[:], in_=core.ident[:], compare_op=ALU.not_equal, fill=1.0, base=0,
                                   pattern=[[-1, P]], channel_multiplier=1).then_inc(const1, 1)
                pv = core.perm[:].rearrange("p (h a) -> p h a", h=HEADS)
                pool.affine_select(out=pv, in_=pv, compare_op=ALU.not_equal, fill=1.0, base=0,
                                   pattern=[[-1, HEADS], [-HEADS, P // HEADS]], channel_multiplier=1).then_inc(const1, 1)
                pool.affine_select(out=core.upper[:], in_=core.ones[:], compare_op=ALU.is_ge, fill=0.0, base=0,
                                   pattern=[[1, P]], channel_multiplier=-1).then_inc(const1, 1)
                for t, pat in ((core.own_head[:], [[-HD, HEADS]]), (core.own_block[:].rearrange("p (h c) -> p h c", c=HD), [[-HD, HEADS], [0, HD]])):
                    pool.affine_select(out=t, in_=t, compare_op=ALU.is_ge, fill=0.0, base=0, pattern=pat,
                                       channel_multiplier=1).then_inc(const1, 1)
                pool.wait_ge(emptied, 1)
                pool.iota(core.key_neg[:, 0:EMPTY * RW].bitcast(I32).rearrange("p (n c) -> p n c", c=RW)[:, :, D:RW], pattern=[[P, EMPTY], [0, 1]],
                          base=2 * T_ALL, channel_multiplier=1).then_inc(numbered, 1)
                pool.wait_ge(numbered, 1)
                pool.wait_ge(const1, 5)
                for t, pat in ((core.own_head[:], [[HD, HEADS]]), (core.own_block[:].rearrange("p (h c) -> p h c", c=HD), [[HD, HEADS], [0, HD]])):
                    pool.affine_select(out=t, in_=t, compare_op=ALU.is_ge, fill=0.0, base=HD - 1, pattern=pat,
                                       channel_multiplier=-1).then_inc(const2, 1)

            @block.vector
            def _(dve):
                nc.vector.memset(core.key_neg[:, 0:EMPTY * RW], 0.0).then_inc(emptied, 1)
                for k in range(4):
                    dve.wait_ge(x_in[k], 16)
                    with dve.Fori(k * 2, (k + 1) * 2) as i:
                        for u in range(4):
                            nc.vector.bn_stats(tile_of(core.stats, i * 4 + u, 6), tile_of(core.x, i * 4 + u)).then_inc(first, 1)
                dve.wait_ge(const2, 2)
                hs = core.own_head[:].rearrange("p (g s) -> p s g", s=PER)
                nc.vector.tensor_reduce(out=core.top[:, 0:PER], in_=hs, op=ALU.max, axis=AX).then_inc(chain, 1)
                nc.vector.tensor_reduce(out=core.even16[:], in_=core.own_head[:].rearrange("p (q r s) -> p r q s", r=2, s=2), op=ALU.max,
                                        axis=mybir.AxisListType.XY).then_inc(chain, 1)
                dve.wait_ge(chain, 2)
                nc.vector.tensor_tensor(core.head_of4[:].rearrange("p (s k) -> p s k", k=P), core.head_of4[:].rearrange("p (s k) -> p s k", k=P),
                                        core.top[:, 0:PER].rearrange("p (s o) -> p s o", o=1).to_broadcast([P, PER, P]), ALU.mult).then_inc(chain, 1)
                dve.wait_ge(loaded, 16 * len(loads))
                nc.vector.tensor_tensor(ffn[0].router_bias[:], ffn[0].router_bias[:], extra[:], ALU.add).then_inc(chain, 1)
                nc.vector.memset(ffn[2].router_bias[:], 0.0).then_inc(chain, 1)
                for l in (0, 2, 3):
                    nc.vector.tensor_scalar(W[l].bq[:], W[l].bq[:], float(HD) ** -0.5, None, ALU.mult).then_inc(chain, 1)
                dve.wait_ge(first, NB)
                dve.wait_ge(chain, 8)

            @block.scalar
            def _(act):
                act.wait_ge(loaded, 16 * len(loads))
                nc.scalar.activation(core.gate[:], core.gate[:], ACT.Tanh).then_inc(gate_done, 1)

        def ffn_weights(l):
            return [(w1_big[:, 0:a[f"w1_{l}"].shape[1]], a[f"w1_{l}"]),
                    (w2_big[:, 0:a[f"w2_{l}"].shape[1]], a[f"w2_{l}"]),
                    (b2_big[:, 0:a[f"b2_{l}"].shape[0]], a[f"b2_{l}"].partition_broadcast(P))]

        for l in range(4):
            phase[0] = f"norm{l}a"
            norm_scale()
            if l == 1:
                phase[0] = "lin1"
                linear_attention(nc, sem, core, W[1], ffn_weights(1))
                phase[0] = "v1"
            else:
                phase[0] = f"att{l}"
                softmax_attention(nc, sem, core, W[l], l >= 2, src if l == 3 else None, ffn_weights(l) + (late if l == 0 else []))
            phase[0] = f"norm{l}f"
            norm_scale()
            phase[0] = f"xnT{l}"
            norm_and_route(nc, sem, core, ffn[l] if l < 3 else dense[3], a[f"b1_{l}"] if l < 3 else None)
            if l < 3:
                copies = 2 if l == 0 else 1
                phase[0] = f"route{l}"
                route(nc, sem, core, "top2" if l == 0 else "top1", 4 + l, CAPACITY if l == 2 else None)
            if l in dense:
                phase[0] = f"ffn{l}"
                feed_forward(nc, sem, core, dense[l], 2 if l == 0 else 0, core.rows_in[l] if l == 0 else None, out if l == 3 else None)
            elif l < 3:
                dispatch(nc, sem, core, core.rows_in[l], 1)
            if l < 3:
                phase[0] = f"tiles{l}"
                expert_tiles(nc, sem, core, ffn[l], core.rows_in[l], TILES2 if l == 0 else TILES1)
                phase[0] = f"combine{l}"
                raw = {0: None, 1: core.xnT[:, 0:NB * P // 4].bitcast(U8), 2: core.xnT[:].bitcast(I32)}[l]
                combine(nc, sem, core, copies, raw, a[f"mask{l + 1}"] if l else None)


def cut(buffer, widths):
    ends = [sum(widths[:k + 1]) for k in range(len(widths))]
    return [buffer[:, end - width:end] for end, width in zip(ends, widths)]


def laid_out(inputs):
    v = {k: np.asarray(x) for k, x in inputs.items()}
    g = {}
    g["x"] = v["x"]
    g["ctxT"] = v["ctx_1024"].transpose(0, 2, 1)
    for l in (0, 2, 3):
        for k in "qkvo":
            m = v[f"L{l}_xattn_W{k}"]
            g[f"w{k}{l}"] = m if l == 2 else m.T
            g[f"b{k}{l}"] = v[f"L{l}_xattn_b{k}"]
    g["wq1"], g["wk1"], g["wv1"], g["wd1"] = v["L1_xattn_wq"], v["L1_xattn_wk"], v["L1_xattn_wv"], v["L1_xattn_dense_w"]
    g["gamma"], g["beta"], g["bd1"] = v["L1_xattn_ln_gamma"], v["L1_xattn_ln_beta"], v["L1_xattn_dense_b"]
    g["em"] = v["mask_BxS2_ff1"].T
    g["src"] = v["mask_1x1xSxS2_ff0"].reshape(P, P)
    g["mask2"] = v["mask_Bx1xS2_bf1"].view(np.uint8).reshape(-1)
    g["mask3"] = v["mask_BxS2_ik0"].reshape(-1)
    g["g_xattn"], g["g_ffn"] = v["g_xattn"], v["g_ffn"]

    def first(m):
        return m.transpose(1, 0, 2).reshape(D, -1)

    def second(m):
        e, h, d = m.shape
        return m.reshape(e, h // P, P, d).transpose(2, 0, 1, 3).reshape(P, -1)

    def bias(m):
        e, h = m.shape
        return m.reshape(e, h // P, P).transpose(2, 0, 1).reshape(P, -1)

    g["w1_0"] = first(np.concatenate([v["L0_ffn_W1"], v["L0_ffn_Ws1"][None]]).transpose(0, 2, 1))
    g["w2_0"] = second(np.concatenate([v["L0_ffn_W2"], v["L0_ffn_Ws2"][None]]).transpose(0, 2, 1))
    g["b1_0"], g["b1_dense0"] = v["L0_ffn_b1"].reshape(-1), bias(v["L0_ffn_bs1"][None])
    g["b2_0"] = np.concatenate([v["L0_ffn_b2"], v["L0_ffn_bs2"][None]]).reshape(-1)
    g["wr0"], g["bg0"], g["bias0"] = v["L0_ffn_Wg"].T, v["L0_ffn_bg"], v["L0_ffn_bias"]
    g["w1_1"], g["w2_1"], g["b1_1"], g["b2_1"] = first(v["L1_ffn_W1"]), second(v["L1_ffn_W2"]), v["L1_ffn_b1"].reshape(-1), v["L1_ffn_b2"].reshape(-1)
    g["wr1"], g["br1"] = v["L1_ffn_Wr"], v["L1_ffn_br"]
    g["w1_2"], g["w2_2"], g["b1_2"], g["b2_2"] = first(v["L2_ffn_w1"]), second(v["L2_ffn_w2"]), v["L2_ffn_b1"].reshape(-1), v["L2_ffn_b2"].reshape(-1)
    g["wr2"] = v["L2_ffn_router_w"].T
    g["w1_3"], g["w2_3"] = v["L3_ffn_w1"], second(v["L3_ffn_w2"][None])
    g["b1_dense3"], g["b2_3"] = bias(v["L3_ffn_b1"][None]), v["L3_ffn_b2"]

    return g


def kernel(**inputs):
    import concourse.bacc as _bacc
    from concourse.bass_utils import run_bass_kernel_spmd as _run

    g = laid_out(inputs)
    nc = _bacc.Bacc("TRN2", target_bir_lowering=False, num_devices=1)
    arrays, args = {}, {}
    for name, m in g.items():
        m = np.ascontiguousarray(m)
        arrays[f"in_{name}"] = m
        args[name] = nc.dram_tensor(f"in_{name}", m.shape, mybir.dt.from_np(m.dtype), kind="ExternalInput").ap()
    out = nc.dram_tensor("out_x", (NB, P, D), F32, kind="ExternalOutput").ap()
    program(nc, args, out)
    r = _run(nc, [arrays], core_ids=[0])
    return r.results[0]["out_x"]
```
